# Optimizing a Trainium2 kernel written in Bass

```python
import numpy as np
import jax
import jax.numpy as jnp

def _softmax(x, axis=-1):
    return jax.nn.softmax(x, axis=axis)

def _gelu(x):
    return jax.nn.gelu(x, approximate=True)

def _silu(x):
    return jax.nn.silu(x)

def _sigmoid(x):
    return jax.nn.sigmoid(x)

def _layernorm(x, axis=-1, eps=1e-05):
    m = jnp.mean(x, axis=axis, keepdims=True)
    v = jnp.var(x, axis=axis, keepdims=True)
    return (x - m) / jnp.sqrt(v + eps)

def _scatter_add(tgt, idx, src, axis=0):
    return tgt.at[idx].add(src)

def _segment_sum(src, seg, n):
    return jax.ops.segment_sum(src, seg, n)
kernel_name = 'mk_decoder_postln_d1_seqx_r8_2e30d5'

def setup_inputs(seed: int=0):
    np.random.seed(seed)
    _w = jnp.asarray

    def _rec_inputs():
        import jax
        import jax.numpy as jnp
        _rk = jax.random.key(seed)
        x = -0.0003929 + 0.9999 * jax.random.normal(jax.random.fold_in(_rk, 1), (16, 128, 128), jnp.float32)
        _lenS = 128 - jax.random.randint(jax.random.fold_in(_rk, 7), (16,), 0, max(1, 128 // 4) + 1, jnp.int32)
        _lenS2 = 77 - jax.random.randint(jax.random.fold_in(_rk, 8), (16,), 0, max(1, 77 // 4) + 1, jnp.int32)
        _ctx_1024P = jax.random.normal(jax.random.fold_in(_rk, 11), (16, 16, 128), jnp.float32)
        _ctx_1024c = jax.random.dirichlet(jax.random.fold_in(_rk, 511), 0.3 * jnp.ones((16,), jnp.float32), (16, 77))
        _ctx_1024t = jnp.einsum('bsk,bkd->bsd', _ctx_1024c, _ctx_1024P)
        _ctx_1024t = _ctx_1024t * jax.lax.rsqrt(jnp.mean(jnp.square(_ctx_1024t)) + 1e-12) * 0.953939
        ctx_1024 = 4.13588e-05 + 0.999923 * (_ctx_1024t + 0.3 * jax.random.normal(jax.random.fold_in(_rk, 611), (16, 77, 128), jnp.float32))
        return (x, ctx_1024)
    x, ctx_1024 = _rec_inputs()

    def _L0_attn_setup():
        import jax, jax.numpy as jnp
        import numpy as np
        D_MODEL = 128
        D_STATE = 128
        D_CONV = 4
        EXPAND = 2
        HEADDIM = 64
        NGROUPS = 1
        CHUNK = 32
        D_INNER = EXPAND * D_MODEL
        NHEADS = D_INNER // HEADDIM
        D_IN_PROJ = 2 * D_INNER + 2 * NGROUPS * D_STATE + NHEADS
        CONV_DIM = D_INNER + 2 * NGROUPS * D_STATE
        BATCH, SEQLEN = (2, 256)

        def rmsnorm(x, w, eps=1e-06):
            ms = jnp.mean(x * x, axis=-1, keepdims=True)
            return w * (x * jax.lax.rsqrt(ms + eps))

        def layernorm(x, eps=1e-05):
            mu = jnp.mean(x, axis=-1, keepdims=True)
            var = jnp.mean((x - mu) ** 2, axis=-1, keepdims=True)
            return (x - mu) * jax.lax.rsqrt(var + eps)

        def activation_quant(x):
            amax = jnp.clip(jnp.max(jnp.abs(x), axis=-1, keepdims=True), 1e-05, None)
            scale = 127.0 / amax
            q = jnp.clip(jnp.round(x * scale), -128, 127)
            return (jax.lax.stop_gradient(q - x * scale) + x * scale) / scale

        def weight_quant(w):
            scale = jnp.clip(jnp.mean(jnp.abs(w)), 1e-05, None)
            wq = jnp.clip(jnp.round(w / scale), -1.0, 1.0)
            return w + jax.lax.stop_gradient(wq - w)

        def bitlinear(x, w):
            return activation_quant(layernorm(x)) @ weight_quant(w).T

        def segsum(x):
            T = x.shape[-1]
            cs = jnp.cumsum(x, axis=-1)
            ss = cs[..., :, None] - cs[..., None, :]
            mask = jnp.tril(jnp.ones((T, T), dtype=bool))
            return jnp.where(mask, ss, -jnp.inf)

        def ssd(u, a, B, C, chunk):
            b, l, h, p = u.shape
            n = B.shape[-1]
            c = l // chunk
            u = u.reshape(b, c, chunk, h, p)
            a = a.reshape(b, c, chunk, h).transpose(0, 3, 1, 2)
            B = B.reshape(b, c, chunk, h, n)
            C = C.reshape(b, c, chunk, h, n)
            a_cs = jnp.cumsum(a, axis=-1)
            L = jnp.exp(segsum(a))
            Y_diag = jnp.einsum('bclhn,bcshn,bhcls,bcshp->bclhp', C, B, L, u)
            decay_states = jnp.exp(a_cs[..., -1:] - a_cs)
            states = jnp.einsum('bclhn,bhcl,bclhp->bchpn', B, decay_states, u)
            a_chunk = jnp.pad(a_cs[..., -1], ((0, 0), (0, 0), (1, 0)))
            decay_chunk = jnp.exp(segsum(a_chunk))
            states = jnp.concatenate([jnp.zeros_like(states[:, :1]), states], axis=1)
            new_states = jnp.einsum('bhzc,bchpn->bzhpn', decay_chunk, states)
            prev_states = new_states[:, :-1]
            Y_off = jnp.einsum('bclhn,bchpn,bhcl->bclhp', C, prev_states, jnp.exp(a_cs))
            return (Y_diag + Y_off).reshape(b, l, h, p)
        key = jax.random.key(seed)
        ks = jax.random.split(key, 6)
        hidden_states = jax.random.normal(ks[0], (BATCH, SEQLEN, D_MODEL), jnp.float32)
        in_proj_w = jax.random.normal(ks[1], (D_IN_PROJ, D_MODEL), jnp.float32) / np.sqrt(D_MODEL).astype(np.float32)
        out_proj_w = jax.random.normal(ks[2], (D_MODEL, D_INNER), jnp.float32) / np.sqrt(D_INNER).astype(np.float32)
        conv_w = jax.random.normal(ks[3], (CONV_DIM, D_CONV), jnp.float32) * 0.1
        conv_b = jnp.zeros((CONV_DIM,), jnp.float32)
        A_log = jnp.log(jnp.arange(1, NHEADS + 1, dtype=jnp.float32))
        Dp = jnp.ones((NHEADS,), jnp.float32)
        dt_min, dt_max, dt_floor = (0.001, 0.1, 0.0001)
        inv_dt = jnp.exp(jax.random.uniform(ks[4], (NHEADS,)) * (np.log(dt_max) - np.log(dt_min)) + np.log(dt_min))
        inv_dt = jnp.clip(inv_dt, dt_floor, None)
        dt_bias = inv_dt + jnp.log(-jnp.expm1(-inv_dt))
        norm_w = jnp.ones((D_MODEL,), jnp.float32)
        out_norm_w = jnp.ones((D_INNER,), jnp.float32)
        return dict(hidden_states=hidden_states, norm_w=norm_w, in_proj_w=in_proj_w, conv_w=conv_w, conv_b=conv_b, A_log=A_log, Dp=Dp, dt_bias=dt_bias, out_norm_w=out_norm_w, out_proj_w=out_proj_w)
    _L0_attn_all = _L0_attn_setup()
    _L0_attn_in = {k: v for k, v in _L0_attn_all.items() if k in ('norm_w', 'in_proj_w', 'conv_w', 'conv_b', 'A_log', 'Dp', 'dt_bias', 'out_norm_w', 'out_proj_w')}
    del _L0_attn_all

    def _L0_xattn_setup():
        import jax, jax.numpy as jnp
        import numpy as np
        H = 128
        B = 8
        L_CHAR = 256
        L_SUB = 128

        def _linear(x, W, b):
            return jnp.einsum('blh,oh->blo', x, W) + b

        def _interp_linear(x, out_len):
            L_in = x.shape[1]
            pos = (jnp.arange(out_len, dtype=x.dtype) + 0.5) * (L_in / out_len) - 0.5
            pos = jnp.clip(pos, 0.0, L_in - 1)
            lo = jnp.floor(pos).astype(jnp.int32)
            hi = jnp.minimum(lo + 1, L_in - 1)
            w = (pos - lo.astype(x.dtype))[None, :, None]
            return x[:, lo] * (1 - w) + x[:, hi] * w
        key = jax.random.key(seed)
        ks = jax.random.split(key, 18)
        s = 0.02
        inp = {'char_emb': jax.random.normal(ks[0], (B, L_CHAR, H), jnp.float32), 'subword_emb': jax.random.normal(ks[1], (B, L_SUB, H), jnp.float32)}
        names = ['Wq_c', 'Wk_s', 'Wv_s', 'Wq_s', 'Wk_c', 'Wv_c']
        for i, n in enumerate(names):
            inp[n] = jax.random.normal(ks[2 + 2 * i], (H, H), jnp.float32) * s
            inp['b' + n[1:]] = jax.random.normal(ks[3 + 2 * i], (H,), jnp.float32) * s
        inp['Wg'] = jax.random.normal(ks[14], (H, 2 * H), jnp.float32) * s
        inp['bg'] = jax.random.normal(ks[15], (H,), jnp.float32) * s
        return inp
    _L0_xattn_all = _L0_xattn_setup()
    _L0_xattn_in = {k: v for k, v in _L0_xattn_all.items() if k in ('Wq_c', 'bq_c', 'Wk_s', 'bk_s', 'Wv_s', 'bv_s', 'Wq_s', 'bq_s', 'Wk_c', 'bk_c', 'Wv_c', 'bv_c', 'Wg', 'bg')}
    del _L0_xattn_all

    def _L0_ffn_setup():
        import jax, jax.numpy as jnp
        import numpy as np
        B, S, D, E, H, K = (4, 256, 128, 8, 64, 2)
        key = jax.random.key(seed)
        ks = jax.random.split(key, 11)
        sc = 0.02
        return {'x': jax.random.normal(ks[0], (B, S, D), dtype=jnp.float32), 'gate_W': jax.random.normal(ks[1], (D, E), dtype=jnp.float32) * sc, 'W1': jax.random.normal(ks[2], (E, D, H), dtype=jnp.float32) * sc, 'b1': jnp.zeros((E, H), dtype=jnp.float32), 'W2': jax.random.normal(ks[3], (E, H, D), dtype=jnp.float32) * sc, 'b2': jnp.zeros((E, D), dtype=jnp.float32), 'Ws1': jax.random.normal(ks[4], (D, H), dtype=jnp.float32) * sc, 'bs1': jnp.zeros((H,), dtype=jnp.float32), 'Ws2': jax.random.normal(ks[5], (H, D), dtype=jnp.float32) * sc, 'bs2': jnp.zeros((D,), dtype=jnp.float32), 'route_scale': jnp.ones((), dtype=jnp.float32)}
    _L0_ffn_all = _L0_ffn_setup()
    _L0_ffn_in = {k: v for k, v in _L0_ffn_all.items() if k in ('gate_W', 'W1', 'b1', 'W2', 'b2', 'Ws1', 'bs1', 'Ws2', 'bs2', 'route_scale')}
    del _L0_ffn_all
    return {'x': x, 'ctx_1024': ctx_1024, 'L0_attn_norm_w': _L0_attn_in['norm_w'], 'L0_attn_in_proj_w': _L0_attn_in['in_proj_w'], 'L0_attn_conv_w': _L0_attn_in['conv_w'], 'L0_attn_conv_b': _L0_attn_in['conv_b'], 'L0_attn_A_log': _L0_attn_in['A_log'], 'L0_attn_Dp': _L0_attn_in['Dp'], 'L0_attn_dt_bias': _L0_attn_in['dt_bias'], 'L0_attn_out_norm_w': _L0_attn_in['out_norm_w'], 'L0_attn_out_proj_w': _L0_attn_in['out_proj_w'], 'L0_xattn_Wq_c': _L0_xattn_in['Wq_c'], 'L0_xattn_bq_c': _L0_xattn_in['bq_c'], 'L0_xattn_Wk_s': _L0_xattn_in['Wk_s'], 'L0_xattn_bk_s': _L0_xattn_in['bk_s'], 'L0_xattn_Wv_s': _L0_xattn_in['Wv_s'], 'L0_xattn_bv_s': _L0_xattn_in['bv_s'], 'L0_xattn_Wq_s': _L0_xattn_in['Wq_s'], 'L0_xattn_bq_s': _L0_xattn_in['bq_s'], 'L0_xattn_Wk_c': _L0_xattn_in['Wk_c'], 'L0_xattn_bk_c': _L0_xattn_in['bk_c'], 'L0_xattn_Wv_c': _L0_xattn_in['Wv_c'], 'L0_xattn_bv_c': _L0_xattn_in['bv_c'], 'L0_xattn_Wg': _L0_xattn_in['Wg'], 'L0_xattn_bg': _L0_xattn_in['bg'], 'L0_ffn_gate_W': _L0_ffn_in['gate_W'], 'L0_ffn_W1': _L0_ffn_in['W1'], 'L0_ffn_b1': _L0_ffn_in['b1'], 'L0_ffn_W2': _L0_ffn_in['W2'], 'L0_ffn_b2': _L0_ffn_in['b2'], 'L0_ffn_Ws1': _L0_ffn_in['Ws1'], 'L0_ffn_bs1': _L0_ffn_in['bs1'], 'L0_ffn_Ws2': _L0_ffn_in['Ws2'], 'L0_ffn_bs2': _L0_ffn_in['bs2'], 'L0_ffn_route_scale': _L0_ffn_in['route_scale']}

def reference(x, ctx_1024, L0_attn_norm_w, L0_attn_in_proj_w, L0_attn_conv_w, L0_attn_conv_b, L0_attn_A_log, L0_attn_Dp, L0_attn_dt_bias, L0_attn_out_norm_w, L0_attn_out_proj_w, L0_xattn_Wq_c, L0_xattn_bq_c, L0_xattn_Wk_s, L0_xattn_bk_s, L0_xattn_Wv_s, L0_xattn_bv_s, L0_xattn_Wq_s, L0_xattn_bq_s, L0_xattn_Wk_c, L0_xattn_bk_c, L0_xattn_Wv_c, L0_xattn_bv_c, L0_xattn_Wg, L0_xattn_bg, L0_ffn_gate_W, L0_ffn_W1, L0_ffn_b1, L0_ffn_W2, L0_ffn_b2, L0_ffn_Ws1, L0_ffn_bs1, L0_ffn_Ws2, L0_ffn_bs2, L0_ffn_route_scale):
    import jax
    import jax.numpy as jnp

    def _L0_attn_ref(hidden_states, norm_w, in_proj_w, conv_w, conv_b, A_log, Dp, dt_bias, out_norm_w, out_proj_w):
        import jax, jax.numpy as jnp
        import numpy as np
        D_MODEL = 128
        D_STATE = 128
        D_CONV = 4
        EXPAND = 2
        HEADDIM = 64
        NGROUPS = 1
        CHUNK = 32
        D_INNER = EXPAND * D_MODEL
        NHEADS = D_INNER // HEADDIM
        D_IN_PROJ = 2 * D_INNER + 2 * NGROUPS * D_STATE + NHEADS
        CONV_DIM = D_INNER + 2 * NGROUPS * D_STATE
        BATCH, SEQLEN = (2, 256)

        def rmsnorm(x, w, eps=1e-06):
            ms = jnp.mean(x * x, axis=-1, keepdims=True)
            return w * (x * jax.lax.rsqrt(ms + eps))

        def layernorm(x, eps=1e-05):
            mu = jnp.mean(x, axis=-1, keepdims=True)
            var = jnp.mean((x - mu) ** 2, axis=-1, keepdims=True)
            return (x - mu) * jax.lax.rsqrt(var + eps)

        def activation_quant(x):
            amax = jnp.clip(jnp.max(jnp.abs(x), axis=-1, keepdims=True), 1e-05, None)
            scale = 127.0 / amax
            q = jnp.clip(jnp.round(x * scale), -128, 127)
            return (jax.lax.stop_gradient(q - x * scale) + x * scale) / scale

        def weight_quant(w):
            scale = jnp.clip(jnp.mean(jnp.abs(w)), 1e-05, None)
            wq = jnp.clip(jnp.round(w / scale), -1.0, 1.0)
            return w + jax.lax.stop_gradient(wq - w)

        def bitlinear(x, w):
            return activation_quant(layernorm(x)) @ weight_quant(w).T

        def segsum(x):
            T = x.shape[-1]
            cs = jnp.cumsum(x, axis=-1)
            ss = cs[..., :, None] - cs[..., None, :]
            mask = jnp.tril(jnp.ones((T, T), dtype=bool))
            return jnp.where(mask, ss, -jnp.inf)

        def ssd(u, a, B, C, chunk):
            b, l, h, p = u.shape
            n = B.shape[-1]
            c = l // chunk
            u = u.reshape(b, c, chunk, h, p)
            a = a.reshape(b, c, chunk, h).transpose(0, 3, 1, 2)
            B = B.reshape(b, c, chunk, h, n)
            C = C.reshape(b, c, chunk, h, n)
            a_cs = jnp.cumsum(a, axis=-1)
            L = jnp.exp(segsum(a))
            Y_diag = jnp.einsum('bclhn,bcshn,bhcls,bcshp->bclhp', C, B, L, u)
            decay_states = jnp.exp(a_cs[..., -1:] - a_cs)
            states = jnp.einsum('bclhn,bhcl,bclhp->bchpn', B, decay_states, u)
            a_chunk = jnp.pad(a_cs[..., -1], ((0, 0), (0, 0), (1, 0)))
            decay_chunk = jnp.exp(segsum(a_chunk))
            states = jnp.concatenate([jnp.zeros_like(states[:, :1]), states], axis=1)
            new_states = jnp.einsum('bhzc,bchpn->bzhpn', decay_chunk, states)
            prev_states = new_states[:, :-1]
            Y_off = jnp.einsum('bclhn,bchpn,bhcl->bclhp', C, prev_states, jnp.exp(a_cs))
            return (Y_diag + Y_off).reshape(b, l, h, p)
        b, l, _ = hidden_states.shape
        h = rmsnorm(hidden_states, norm_w)
        zxbcdt = bitlinear(h, in_proj_w)
        z = zxbcdt[..., :D_INNER]
        xBC = zxbcdt[..., D_INNER:D_INNER + CONV_DIM]
        dt = zxbcdt[..., D_INNER + CONV_DIM:]
        xp = jnp.pad(xBC, ((0, 0), (D_CONV - 1, 0), (0, 0)))
        conv = sum((xp[:, k:k + l, :] * conv_w[:, k] for k in range(D_CONV))) + conv_b
        xBC = jax.nn.silu(conv)
        x = xBC[..., :D_INNER].reshape(b, l, NHEADS, HEADDIM)
        Bm = xBC[..., D_INNER:D_INNER + NGROUPS * D_STATE].reshape(b, l, NGROUPS, D_STATE)
        Cm = xBC[..., D_INNER + NGROUPS * D_STATE:].reshape(b, l, NGROUPS, D_STATE)
        hpg = NHEADS // NGROUPS
        Bh = jnp.repeat(Bm, hpg, axis=2)
        Ch = jnp.repeat(Cm, hpg, axis=2)
        dt = jax.nn.softplus(dt + dt_bias)
        A = -jnp.exp(A_log)
        y = ssd(x * dt[..., None], dt * A, Bh, Ch, CHUNK)
        y = y + x * Dp[None, None, :, None]
        y = y * jax.nn.silu(z).reshape(b, l, NHEADS, HEADDIM)
        y = rmsnorm(y.reshape(b, l, D_INNER), out_norm_w)
        out = bitlinear(y, out_proj_w)
        return hidden_states + out

    def _L0_xattn_ref(char_emb, subword_emb, Wq_c, bq_c, Wk_s, bk_s, Wv_s, bv_s, Wq_s, bq_s, Wk_c, bk_c, Wv_c, bv_c, Wg, bg):
        import jax, jax.numpy as jnp
        import numpy as np
        H = 128
        B = 8
        L_CHAR = 256
        L_SUB = 128

        def _linear(x, W, b):
            return jnp.einsum('blh,oh->blo', x, W) + b

        def _interp_linear(x, out_len):
            L_in = x.shape[1]
            pos = (jnp.arange(out_len, dtype=x.dtype) + 0.5) * (L_in / out_len) - 0.5
            pos = jnp.clip(pos, 0.0, L_in - 1)
            lo = jnp.floor(pos).astype(jnp.int32)
            hi = jnp.minimum(lo + 1, L_in - 1)
            w = (pos - lo.astype(x.dtype))[None, :, None]
            return x[:, lo] * (1 - w) + x[:, hi] * w
        h = char_emb.shape[-1]
        scale = 1.0 / jnp.sqrt(jnp.asarray(h, char_emb.dtype))
        Q_char = _linear(char_emb, Wq_c, bq_c)
        K_sub = _linear(subword_emb, Wk_s, bk_s)
        V_sub = _linear(subword_emb, Wv_s, bv_s)
        scores = jnp.einsum('bqh,bkh->bqk', Q_char, K_sub) * scale
        char2sub = jnp.einsum('bqk,bkh->bqh', jax.nn.softmax(scores, axis=-1), V_sub)
        Q_sub = _linear(subword_emb, Wq_s, bq_s)
        K_char = _linear(char_emb, Wk_c, bk_c)
        V_char = _linear(char_emb, Wv_c, bv_c)
        scores2 = jnp.einsum('bqh,bkh->bqk', Q_sub, K_char) * scale
        sub2char = jnp.einsum('bqk,bkh->bqh', jax.nn.softmax(scores2, axis=-1), V_char)
        L_char = char_emb.shape[1]
        if sub2char.shape[1] != L_char:
            sub2char = _interp_linear(sub2char, L_char)
        gate_in = jnp.concatenate([char2sub, sub2char], axis=-1)
        gate = jax.nn.sigmoid(jnp.einsum('blh,oh->blo', gate_in, Wg) + bg)
        return gate * char2sub + (1 - gate) * sub2char

    def _L0_ffn_ref(x, gate_W, W1, b1, W2, b2, Ws1, bs1, Ws2, bs2, route_scale):
        import jax, jax.numpy as jnp
        import numpy as np
        B, S, D, E, H, K = (4, 256, 128, 8, 64, 2)
        scores = jax.nn.sigmoid(x @ gate_W) * route_scale
        topk_scores, topk_idx = jax.lax.top_k(scores, K)
        topk_w = topk_scores / topk_scores.sum(-1, keepdims=True)
        onehot = jax.nn.one_hot(topk_idx, E, dtype=x.dtype)
        gate_full = jnp.einsum('bsk,bske->bse', topk_w, onehot)
        h = jax.nn.gelu(jnp.einsum('bsd,edh->bseh', x, W1) + b1, approximate=False)
        y = jnp.einsum('bseh,ehd->bsed', h, W2) + b2
        expert_out = jnp.einsum('bse,bsed->bsd', gate_full, y)
        shared = jax.nn.gelu(x @ Ws1 + bs1, approximate=False) @ Ws2 + bs2
        return expert_out + shared
    x = _layernorm(x + _L0_attn_ref(x, L0_attn_norm_w, L0_attn_in_proj_w, L0_attn_conv_w, L0_attn_conv_b, L0_attn_A_log, L0_attn_Dp, L0_attn_dt_bias, L0_attn_out_norm_w, L0_attn_out_proj_w), axis=-1)
    x = _layernorm(x + _L0_xattn_ref(x, ctx_1024, L0_xattn_Wq_c, L0_xattn_bq_c, L0_xattn_Wk_s, L0_xattn_bk_s, L0_xattn_Wv_s, L0_xattn_bv_s, L0_xattn_Wq_s, L0_xattn_bq_s, L0_xattn_Wk_c, L0_xattn_bk_c, L0_xattn_Wv_c, L0_xattn_bv_c, L0_xattn_Wg, L0_xattn_bg), axis=-1)
    x = _layernorm(x + _L0_ffn_ref(x, L0_ffn_gate_W, L0_ffn_W1, L0_ffn_b1, L0_ffn_W2, L0_ffn_b2, L0_ffn_Ws1, L0_ffn_bs1, L0_ffn_Ws2, L0_ffn_bs2, L0_ffn_route_scale), axis=-1)
    return x

_drawn_inputs = setup_inputs


def setup_inputs(seed=0):
    import zlib

    import numpy as np

    out = dict(_drawn_inputs(seed))
    spreads = {'L0_attn_norm_w': (1.0, 0.2),
     'L0_attn_conv_b': (0.0, 0.1),
     'L0_attn_Dp': (1.0, 0.6),
     'L0_attn_out_norm_w': (1.0, 0.2),
     'L0_ffn_b1': (0.0, 0.8),
     'L0_ffn_b2': (0.0, 0.1),
     'L0_ffn_bs1': (0.0, 0.8),
     'L0_ffn_bs2': (0.0, 0.1)}
    factors = {'L0_xattn_Wq_c': 8.0,
     'L0_xattn_bq_c': 8.0,
     'L0_xattn_Wk_s': 8.0,
     'L0_xattn_bk_s': 8.0,
     'L0_xattn_bv_s': 4.74,
     'L0_xattn_Wq_s': 8.0,
     'L0_xattn_bq_s': 8.0,
     'L0_xattn_Wk_c': 8.0,
     'L0_xattn_bk_c': 8.0,
     'L0_xattn_bv_c': 5.09,
     'L0_xattn_Wg': 8.0,
     'L0_xattn_bg': 8.0,
     'L0_ffn_W1': 4.321,
     'L0_ffn_W2': 3.85,
     'L0_ffn_Ws1': 2.962,
     'L0_ffn_Ws2': 2.701}
    for name, (base, spread) in spreads.items():
        noise = np.random.default_rng([zlib.crc32(name.encode()), seed]).standard_normal(out[name].shape)
        drawn = base * np.exp(spread * noise) if base else spread * noise
        out[name] = jnp.asarray(drawn.astype(out[name].dtype))
    for name, factor in factors.items():
        out[name] = (out[name] * factor).astype(out[name].dtype)
    return out
```

```python
import numpy as np
import concourse.bass as bass
from concourse import mybir
from contextlib import ExitStack

FP32 = mybir.dt.float32
BF16 = mybir.dt.bfloat16
ALU = mybir.AluOpType
ACT = mybir.ActivationFunctionType
AXIS = mybir.AxisListType

NB, L, D = 16, 128, 128
LS = 77
GB = 4
NG = NB // GB
T = GB * L
TS = GB * LS
DI, NH, HD = 256, 4, 64
NC = 4
TAPS = 4
E, HID = 8, 64
NE = E * HID // 128
MAGIC = 12582912.0
INV_SQRT_D = float(1.0 / np.sqrt(np.float32(D)))

_COLS = [("win", 772), ("wout", 256), ("conv_w", NC * TAPS), ("conv_b", NC),
         ("wq_c", 128), ("wk_s", 128), ("wq_s", 128), ("wk_c", 128),
         ("wv_s", 128), ("wv_sT", 128), ("wv_c", 128), ("wv_cT", 128), ("wgT", 256),
         ("bq_c", 1), ("bk_s", 1), ("bq_s", 1), ("bk_c", 1), ("bv_s", 1), ("bv_c", 1),
         ("gate_w", E), ("w1", 512), ("ws1", HID), ("b1", NE), ("bs1", 1),
         ("w2", 512), ("w2s", 128)]
_ROWS = [("norm_w", D), ("out_norm_w", DI), ("Dp", NH), ("A_log", NH), ("dt_bias", NH),
         ("bg", 128), ("bv_s", 128), ("bv_c", 128), ("bs2", D), ("route_scale", 1)]
_CONSTS = [("ident", 128), ("upto", 128), ("after", 128), ("interp", 128), ("sel", (NE + 1) * 128), ("prio", E)]


def _places(cols):
    at, out = 0, {}
    for name, n in cols:
        out[name] = (at, at + n)
        at += n
    return out, at


COL, NCOL = _places(_COLS)
ROW, NROW = _places(_ROWS)
CST, NCST = _places(_CONSTS)


class Steps:

    def __init__(self, eng, sem):
        self.eng, self.sem, self.base, self.n = eng, sem, 0, 0

    def mark(self, ins):
        ins.then_inc(self.sem, 1)
        self.n += 1
        return self.base + self.n

    def wait(self, count):
        self.eng.wait_ge(self.sem, count)

    def link(self, ins):
        self.wait(self.mark(ins))

    def enter(self, start, g, per):
        self.base, self.n = start + g * per, 0

    def leave(self, start, steps, per):
        assert self.n == per, (self.n, per)
        self.base, self.n = start + steps * per, 0


def build(nc, x, ctxT, wpack, rpack, cpack, out):
    ctx = ExitStack()
    with ctx:
        def sb(name, shape, dt=FP32):
            return ctx.enter_context(nc.sbuf_tensor(name, shape, dt))

        def sem(name):
            return ctx.enter_context(nc.semaphore(name))

        W = sb("W", [128, NCOL])
        R = sb("R", [128, NROW])
        C = sb("C", [128, NCST])

        def w(name, rows=128):
            a, b = COL[name]
            return W[0:rows, a:b]

        def r(name, rows=128):
            a, b = ROW[name]
            return R[0:rows, a:b]

        def c_(name, rows=128):
            a, b = CST[name]
            return C[0:rows, a:b]

        ident, upto, after = c_("ident"), c_("upto"), c_("after")
        ident_bf = sb("ident_bf", [128, 128], BF16)
        ones = sb("ones", [128, 128])
        neg_half = sb("neg_half", [128, GB])
        neg_one = sb("neg_one", [128, GB])
        eps5 = sb("eps5", [128, GB])
        eps6 = sb("eps6", [128, GB])
        win_q = sb("win_q", [128, 772], BF16)
        wout_q = sb("wout_q", [128, 2, 128], BF16)
        low = sb("low", [128, 772])
        wsum = sb("wsum", [128, 2])
        wscale = sb("wscale", [128, 4])

        x_all = sb("x_all", [128, NB, D])
        ms_x = sb("ms_x", [128, GB])
        mv_u = sb("mv_u", [128, GB, 2])
        amax_u = sb("amax_u", [128, GB])
        s_in = sb("s_in", [128, NB])
        f_in = sb("f_in", [128, NB])
        pool_t = [sb(f"pool_t{i}", [128, GB]) for i in range(3)]
        qT = sb("qT", [128, NB * L], BF16)
        x_tok = sb("x_tok", [128, NB, DI])
        z_tok = sb("z_tok", [128, NB, DI])
        dt_tok = sb("dt_tok", [128, NB, NH])
        g_all = sb("g_all", [128, NB, L])

        u = sb("u", [128, GB, D])
        uc = sb("uc", [128, GB, D])
        magic_bias = sb("magic_bias", [128, 1])
        junk = sb("junk", [128, GB, DI])
        stats = sb("stats", [128, GB, 6])
        qm = sb("qm", [128, GB, D])
        q_bf = sb("q_bf", [128, GB, D], BF16)
        diag = sb("diag", [128, GB, 128])
        s_row = sb("s_row", [128, T])
        xs = sb("xs", [128, NC, GB, TAPS - 1 + L])
        acc = sb("acc", [128, NC, GB, L])
        xbc = sb("xbc", [128, NC, GB, L])

        a1T = sb("a1T", [128, 128])
        a2T = sb("a2T", [128, 128])
        wvs = sb("wvs", [128, 256])
        wvc = sb("wvc", [128, 256])
        vec = sb("vec", [128, 6])
        brow = sb("brow", [1, 512])
        v_dt = sb("v_dt", [128, NB * NH])
        na_dt = sb("na_dt", [128, NB * NH])
        e_dt = sb("e_dt", [128, NB * NH])
        l_dt = sb("l_dt", [128, NB * NH])
        a_log = sb("a_log", [128, NH])
        dt_sp = sb("dt_sp", [128, NB, NH])
        a_dt = sb("a_dt", [128, NB, NH])

        seg = xbc[:, :, :, :]
        ex = acc[:, :, :, :]
        u_dt = sb("u_dt", [128, GB, DI])
        x_d = sb("x_d", [128, GB, DI])
        x2x = u[:, :, :]
        y = sb("y", [128, GB, DI])
        flat = xs[:, :, :, :].rearrange("p c b l -> p (c b l)")
        y_w = flat[:, 0:GB * DI].rearrange("p (b c) -> p b c", b=GB)
        y_qm = flat[:, GB * DI:2 * GB * DI].rearrange("p (b c) -> p b c", b=GB)
        y_c = sb("y_c", [128, GB, DI])
        y_q = sb("y_q", [128, GB, DI], BF16)
        y_qT = sb("y_qT", [128, GB, 2, L], BF16)
        ms_y = sb("ms_y", [128, GB])
        mv_y = sb("mv_y", [128, GB, 2])
        amax_y = sb("amax_y", [128, GB])
        s_out = sb("s_out", [128, NB])
        f_out = sb("f_out", [128, NB])
        stats_s = sb("stats_s", [128, GB, 6])
        res1 = uc[:, :, :]
        mv1 = sb("mv1", [128, GB, 2])
        rstd1 = sb("rstd1", [128, GB])
        x1 = sb("x1", [128, NB, D])
        x1_s = sb("x1_s", [128, GB, D])
        x1T = sb("x1T", [128, GB, L])

        ctx_s = sb("ctx_s", [128, TS])
        p1 = sb("p1", [128, TS])
        p2 = sb("p2", [128, TS])
        row1 = sb("row1", [1, TS])
        row2 = sb("row2", [1, TS])
        vvs = sb("vvs", [LS, GB, 256])
        vvc = sb("vvc", [128, GB, 256])
        nmx1 = sb("nmx1", [128, GB])
        den1 = sb("den1", [128, GB])
        rden1 = sb("rden1", [128, GB])
        nmx2 = sb("nmx2", [LS, GB])
        den2 = sb("den2", [LS, GB])
        rden2 = sb("rden2", [LS, GB])
        e1 = sb("e1", [128, GB, LS])
        e1n = sb("e1n", [128, GB, LS])
        e1T = sb("e1T", [LS, GB, L])
        e2 = sb("e2", [LS, GB, L])
        ipn = sb("ipn", [LS, GB, L])
        w2i = sb("w2i", [128, GB, L])
        th = diag[:, :, :]
        s2c = qm[:, :, :]
        s2c_x1 = sb("s2c_x1", [128, GB, D])
        dif = sb("dif", [128, GB, D])
        res2 = sb("res2", [128, GB, D])
        stats_x = sb("stats_x", [128, GB, 6])
        mv2 = sb("mv2", [128, GB, 2])
        rstd2 = sb("rstd2", [128, GB])
        x2_s = sb("x2_s", [128, GB, D])
        x2T_s = sb("x2T_s", [128, GB, L])
        x2T = sb("x2T", [128, NB * L])
        x2b = x_all
        logit = sb("logit", [128, NB, E])

        xf = x_tok[:, :, :].rearrange("p b c -> p (b c)")
        zf = z_tok[:, :, :].rearrange("p b c -> p (b c)")
        hid = xf[:, 0:NE * T].rearrange("p (t n) -> p t n", t=NE)
        hid_s = xf[:, NE * T:(NE + 1) * T]
        res3 = xf[:, 5 * T:6 * T].rearrange("p (b d) -> p b d", b=GB)
        y_out = xf[:, 6 * T:7 * T].rearrange("p (b d) -> p b d", b=GB)
        (score, top, first, rest, pick, second) = (
            zf[:, i * NB * E:(i + 1) * NB * E].rearrange("p (b e) -> p b e", e=E) for i in range(6))
        gT = qT[0:3 * E, 0:T]
        sel_bf = low[0:3 * E, 0:(NE + 1) * 64].bitcast(BF16)
        max1 = sb("max1", [128, NB])
        max2 = sb("max2", [128, NB])
        prio1 = sb("prio1", [128, NB])
        gate3 = sb("gate3", [128, NB, 3 * E], BF16)
        stats_o = sb("stats_o", [128, GB, 6])
        mv3 = sb("mv3", [128, GB, 2])
        rstd3 = sb("rstd3", [128, GB])

        bank = [ctx.enter_context(nc.psum_tensor(f"bank{i}", [128, 512], FP32)) for i in range(8)]

        x_in = sem("x_in")
        w_in = sem("w_in")
        r_in = sem("r_in")
        c_in = sem("c_in")
        act_steps = sem("act_steps")
        dve_steps = sem("dve_steps")
        pool_steps = sem("pool_steps")
        pool_settled = sem("pool_settled")
        dve_settled = sem("dve_settled")
        consts_ready = sem("consts_ready")
        ident_ready = sem("ident_ready")
        wsum_ready = sem("wsum_ready")
        wsum_psum = sem("wsum_psum")
        win_ready = sem("win_ready")
        magic_ready = sem("magic_ready")
        u_ready = sem("u_ready")
        ms_ready = sem("ms_ready")
        amax_ready = sem("amax_ready")
        f_ready = sem("f_ready")
        qm_ready = sem("qm_ready")
        q_ready = sem("q_ready")
        diag_ready = sem("diag_ready")
        qt_psum = sem("qt_psum")
        srow_psum = sem("srow_psum")
        qt_ready = sem("qt_ready")
        srow_ready = sem("srow_ready")
        zx_psum = sem("zx_psum")
        xs_ready = sem("xs_ready")
        tap0_ready = sem("tap0_ready")
        conv_ready = sem("conv_ready")
        silu_ready = sem("silu_ready")
        g_psum = sem("g_psum")
        xt_psum = sem("xt_psum")
        g_ready = sem("g_ready")
        xtok_ready = sem("xtok_ready")
        zd_psum = sem("zd_psum")
        zd_ready = sem("zd_ready")
        out_done = sem("out_done")
        sel_ready = sem("sel_ready")
        score_ready = sem("score_ready")
        gate_ready = sem("gate_ready")
        gt_psum = sem("gt_psum")
        gt_ready = sem("gt_ready")
        h_psum = sem("h_psum")
        gb_psum = sem("gb_psum")
        hid_ready = sem("hid_ready")
        hs_ready = sem("hs_ready")
        hg_ready = sem("hg_ready")
        moe_psum = sem("moe_psum")
        res3_ready = sem("res3_ready")
        var3_ready = sem("var3_ready")
        rstd3_ready = sem("rstd3_ready")
        yout_ready = sem("yout_ready")
        a_psum = sem("a_psum")
        attw_ready = sem("attw_ready")
        dt_v = sem("dt_v")
        dt_l = sem("dt_l")
        dt_ready = sem("dt_ready")
        seg_ready = sem("seg_ready")
        u_dt_ready = sem("u_dt_ready")
        ss_psum = sem("ss_psum")
        ex_ready = sem("ex_ready")
        m_ready = sem("m_ready")
        y_psum = sem("y_psum")
        y_ready = sem("y_ready")
        x2x_ready = sem("x2x_ready")
        msy_ready = sem("msy_ready")
        yw_ready = sem("yw_ready")
        amaxy_ready = sem("amaxy_ready")
        fout_ready = sem("fout_ready")
        yqm_ready = sem("yqm_ready")
        yq_ready = sem("yq_ready")
        yqt_psum = sem("yqt_psum")
        yqt_ready = sem("yqt_ready")
        proj_psum = sem("proj_psum")
        var1_ready = sem("var1_ready")
        rstd1_ready = sem("rstd1_ready")
        x1_ready = sem("x1_ready")
        x1t_psum = sem("x1t_psum")
        x1t_ready = sem("x1t_ready")
        ctx_in = sem("ctx_in")
        p_psum = sem("p_psum")
        vvs_psum = sem("vvs_psum")
        p_ready = sem("p_ready")
        vvs_ready = sem("vvs_ready")
        vvc_psum = sem("vvc_psum")
        vvc_ready = sem("vvc_ready")
        s1_psum = sem("s1_psum")
        s2_psum = sem("s2_psum")
        nmx1_ready = sem("nmx1_ready")
        nmx2_ready = sem("nmx2_ready")
        e1_ready = sem("e1_ready")
        e2_ready = sem("e2_ready")
        e1n_ready = sem("e1n_ready")
        ipn_ready = sem("ipn_ready")
        e1t_psum = sem("e1t_psum")
        w2i_psum = sem("w2i_psum")
        e1t_ready = sem("e1t_ready")
        w2i_ready = sem("w2i_ready")
        o_psum = sem("o_psum")
        s2c_ready = sem("s2c_ready")
        th_ready = sem("th_ready")
        rs_ready = sem("rs_ready")
        dif_ready = sem("dif_ready")
        dif_part = sem("dif_part")
        var2_ready = sem("var2_ready")
        rstd2_ready = sem("rstd2_ready")
        x2_ready = sem("x2_ready")
        x2b_ready = sem("x2b_ready")
        x2t_psum = sem("x2t_psum")
        x2t_ready = sem("x2t_ready")
        logit_psum = sem("logit_psum")
        logit_ready = sem("logit_ready")
        dbg_done = sem("dbg_done")

        X_DMA = 16 * NG
        N_CONSTS = 6

        block = ctx.enter_context(nc.Block())

        def batch(g, j):
            return bass.ds(g * GB + j, 1)

        def group(g):
            return bass.ds(g * GB, GB)

        @block.sync
        def _(sp):
            for g in range(NG):
                sp.dma_start(x_all[:, g * GB:(g + 1) * GB, :],
                             x[g * GB:(g + 1) * GB].rearrange("b l d -> l b d")).then_inc(x_in, 16)
                if g == 0:
                    sp.dma_start(W[:, 0:772], wpack[:, 0:772]).then_inc(w_in, 16)
            sp.dma_start(W[:, 772:NCOL], wpack[:, 772:NCOL]).then_inc(w_in, 16)
            def load_context(g):
                sp.wait_ge(vvs_psum, 2 * g)
                sp.wait_ge(x_in, X_DMA)
                sp.dma_start(ctx_s[:, :], ctxT[:, bass.ds(g * TS, TS)]).then_inc(ctx_in, 16)

            load_context(0)
            with sp.Fori(1, NG) as g:
                load_context(g)
            with sp.Fori(0, NG) as g:
                sp.wait_ge(yout_ready, g + 1)
                sp.wait_ge(x_in, X_DMA)
                sp.dma_start(out[group(g)].rearrange("b l d -> l b d"), y_out).then_inc(out_done, 16)
            sp.wait_ge(out_done, 16 * NG)

        @block.gpsimd
        def _(pool):
            steps = Steps(pool, pool_steps)
            pool.memset(ones[:, :], 1.0).then_inc(consts_ready, 1)
            pool.memset(neg_half[:, :], -0.5).then_inc(consts_ready, 1)
            pool.memset(neg_one[:, :], -1.0).then_inc(consts_ready, 1)
            pool.memset(xs[:, :, :, 0:TAPS - 1], 0.0).then_inc(consts_ready, 1)
            pool.memset(eps5[:, :], 1e-5).then_inc(consts_ready, 1)
            pool.memset(eps6[:, :], 1e-6).then_inc(consts_ready, 1)
            pool.wait_ge(consts_ready, N_CONSTS)

            def rsqrt(dst, src):
                steps.link(pool.tensor_tensor(dst, src, neg_half[:, :], ALU.pow))

            def scaled_input(g):
                pool.wait_ge(amax_ready, g)
                settle()
                pool.tensor_tensor(u[:, :, :], x_all[:, group(g), :],
                                   r("norm_w").unsqueeze(1).to_broadcast([128, GB, D]), ALU.mult).then_inc(u_ready, 1)

            def settle():
                pool.sem_inc(pool_settled, 1)

            def quant_scales(g, ms, mv, amax, s_to, f_to, ready):
                a, b, t = (p[:, :] for p in pool_t)
                gs = group(g)
                steps.link(pool.tensor_tensor(a, ms[:, :], eps6[:, :], ALU.add))
                rsqrt(a, a)
                steps.link(pool.tensor_tensor(b, a, a, ALU.mult))
                steps.link(pool.tensor_tensor(b, b, mv[:, :, 1], ALU.mult))
                steps.link(pool.tensor_tensor(b, b, eps5[:, :], ALU.add))
                rsqrt(b, b)
                steps.link(pool.tensor_tensor(t, a, b, ALU.mult))
                steps.link(pool.tensor_tensor(a, t, amax[:, :], ALU.mult))
                settle()
                steps.link(pool.tensor_scalar(a, a, 1e-5, 1.0 / 127.0, ALU.max, ALU.mult))
                steps.link(pool.tensor_tensor(b, a, neg_one[:, :], ALU.pow))
                pool.tensor_tensor(s_to[:, gs], a, ones[:, 0:GB], ALU.mult)
                pool.tensor_tensor(f_to[:, gs], t, b, ALU.mult).then_inc(ready, 1)

            def input_scales(g):
                pool.wait_ge(ms_ready, GB * (g + 1))
                pool.wait_ge(amax_ready, g + 1)
                quant_scales(g, ms_x, mv_u, amax_u, s_in, f_in, f_ready)

            PER = 10
            pool.wait_ge(r_in, 16)
            pool.wait_ge(x_in, X_DMA)
            scaled_input(0)
            steps.enter(0, 0, PER)
            input_scales(0)
            steps.leave(0, 1, PER)
            with pool.Fori(0, NG - 1) as g:
                steps.enter(PER, g, PER)
                scaled_input(g + 1)
                input_scales(g + 1)
                steps.leave(PER, NG - 1, PER)

            def weights_of_scan(g):
                pool.wait_ge(ss_psum, GB * g)
                pool.wait_ge(y_psum, 2 * g)
                pool.wait_ge(y_ready, 2 * g)
                settle()
                for j in range(GB):
                    pool.tensor_tensor(seg[:, j], upto.unsqueeze(1).to_broadcast([128, NH, L]),
                                       a_dt[:, batch(g, j), :].rearrange("p a h -> p (a h)").unsqueeze(2).to_broadcast([128, NH, L]),
                                       ALU.mult).then_inc(seg_ready, 1)
                    pool.tensor_tensor(u_dt[:, j].rearrange("p (h c) -> p h c", h=NH),
                                       x_tok[:, batch(g, j), :].rearrange("p a (h c) -> p (a h) c", h=NH),
                                       dt_sp[:, batch(g, j), :].rearrange("p a h -> p (a h)").unsqueeze(2).to_broadcast([128, NH, HD]),
                                       ALU.mult)
                    pool.tensor_tensor(x_d[:, j].rearrange("p (h c) -> p h c", h=NH),
                                       x_tok[:, batch(g, j), :].rearrange("p a (h c) -> p (a h) c", h=NH),
                                       r("Dp").unsqueeze(2).to_broadcast([128, NH, HD]),
                                       ALU.mult).then_inc(u_dt_ready, 1)

            def scaled_y(g):
                pool.wait_ge(amaxy_ready, g)
                for i in range(2):
                    pool.wait_ge(y_ready, 2 * g + i + 1)
                    pool.tensor_tensor(y_w[:, 2 * i:2 * i + 2], y[:, 2 * i:2 * i + 2],
                                       r("out_norm_w").unsqueeze(1).to_broadcast([128, 2, DI]),
                                       ALU.mult).then_inc(yw_ready, 1)

            def y_scales(g):
                pool.wait_ge(msy_ready, GB * (g + 1))
                pool.wait_ge(amaxy_ready, g + 1)
                quant_scales(g, ms_y, mv_y, amax_y, s_out, f_out, fout_ready)

            def rstd(g, var, var_ready, dst, ready):
                pool.wait_ge(var_ready, g + 1)
                steps.link(pool.tensor_tensor(dst[:, :], var[:, :, 1], eps5[:, :], ALU.add))
                pool.tensor_tensor(dst[:, :], dst[:, :], neg_half[:, :], ALU.pow).then_inc(ready, 1)

            def attention_residual(g):
                pool.wait_ge(dif_ready, g)
                for j in range(GB):
                    pool.wait_ge(s2c_ready, GB * g + j + 1)
                    settle()
                    pool.tensor_tensor(s2c_x1[:, j, :], s2c[:, j, :],
                                       x1[:, batch(g, j), :].rearrange("p a d -> p (a d)"), ALU.add).then_inc(rs_ready, 1)

            def expert_residual(g):
                pool.wait_ge(x2_ready, g + 1)
                settle()
                pool.tensor_tensor(x2b[:, group(g), :], x2_s[:, :, :],
                                   r("bs2").unsqueeze(1).to_broadcast([128, GB, D]), ALU.add).then_inc(x2b_ready, 1)

            start = NG * PER
            pool.wait_ge(dt_ready, 1)
            pool.wait_ge(xtok_ready, 2 * NG)
            pool.wait_ge(c_in, 16)
            S_PER, X_PER = 11, 1
            steps.base, steps.n = start, 0
            weights_of_scan(0)
            scaled_y(0)
            y_scales(0)
            rstd(0, mv1, var1_ready, rstd1, rstd1_ready)
            steps.leave(start, 1, S_PER)
            start += S_PER
            with pool.Fori(0, NG - 1) as g:
                steps.enter(start, g, S_PER + X_PER)
                weights_of_scan(g + 1)
                attention_residual(g)
                rstd(g, mv2, var2_ready, rstd2, rstd2_ready)
                expert_residual(g)
                scaled_y(g + 1)
                y_scales(g + 1)
                rstd(g + 1, mv1, var1_ready, rstd1, rstd1_ready)
                steps.leave(start, NG - 1, S_PER + X_PER)
            attention_residual(NG - 1)
            rstd(NG - 1, mv2, var2_ready, rstd2, rstd2_ready)
            expert_residual(NG - 1)

            start = steps.base + steps.n
            with pool.Fori(0, NG) as g:
                steps.enter(start, g, 1)
                rstd(g, mv3, var3_ready, rstd3, rstd3_ready)
                steps.leave(start, NG, 1)

        @block.scalar
        def _(act):
            steps = Steps(act, act_steps)
            act.dma_start(R[:, :], rpack.rearrange("(a n) -> a n", a=1).to_broadcast([128, NROW])).then_inc(r_in, 16)
            act.dma_start(C[:, :], cpack).then_inc(c_in, 16)
            act.wait_ge(c_in, 16)
            act.activation(ident_bf[:, :], ident, ACT.Copy).then_inc(ident_ready, 1)

            def mean_square(g):
                act.wait_ge(ms_ready, GB * g)
                for j in range(GB):
                    act.activation(junk[:, j, 0:D], x_all[:, batch(g, j), :], ACT.Square, scale=float(D ** -0.5),
                                   accum_out=ms_x[:, j:j + 1]).then_inc(ms_ready, 1)

            def quantise(g):
                act.wait_ge(f_ready, g + 1)
                act.wait_ge(q_ready, g)
                for j in range(GB):
                    act.activation(qm[:, j, :], uc[:, j, :], ACT.Identity, bias=magic_bias[:, 0:1],
                                   scale=f_in[:, batch(g, j)]).then_inc(qm_ready, 1)

            def evacuate_q(g):
                act.wait_ge(qt_psum, g + 1)
                act.activation(qT[:, bass.ds(g * T, T)], bank[4][:, 0:T // 2].bitcast(BF16), ACT.Copy)\
                   .then_inc(qt_ready, 1)
                act.wait_ge(srow_psum, g + 1)
                act.wait_ge(xs_ready, NC * g)
                act.activation(s_row[:, :], bank[5][:, :], ACT.Copy).then_inc(srow_ready, 1)

            def conv_first_tap(g):
                for c in range(NC):
                    act.wait_ge(xs_ready, NC * g + c + 1)
                    act.activation(acc[:, c, :, :], xs[:, c, :, TAPS - 1:], ACT.Identity,
                                   bias=w("conv_b")[:, c:c + 1],
                                   scale=w("conv_w")[:, c * TAPS + TAPS - 1:c * TAPS + TAPS]).then_inc(tap0_ready, 1)

            def gates(g):
                for j in range(GB):
                    act.wait_ge(zd_psum, GB * g + j + 1)
                    act.activation(z_tok[:, batch(g, j), :], bank[6 + j % 2][:, 0:DI], ACT.Silu,
                                   scale=s_in[:, batch(g, j)])
                    act.activation(dt_tok[:, batch(g, j), :], bank[6 + j % 2][:, DI:DI + NH], ACT.Identity,
                                   scale=s_in[:, batch(g, j)]).then_inc(zd_ready, 1)

            def silu_xbc(g):
                act.wait_ge(g_psum, g)
                act.wait_ge(xt_psum, 2 * g)
                for c in range(NC):
                    act.wait_ge(conv_ready, NC * g + c + 1)
                    act.activation(xbc[:, c, :, :], acc[:, c, :, :], ACT.Silu).then_inc(silu_ready, 1)

            def evacuate_x(g):
                for i in range(2):
                    act.wait_ge(xt_psum, 2 * g + i + 1)
                    act.activation(x_tok[:, bass.ds(g * GB + 2 * i, 2), :],
                                   bank[i][:, :].rearrange("p (b c) -> p b c", b=2), ACT.Copy).then_inc(xtok_ready, 1)

            def project(g):
                conv_first_tap(g)
                gates(g)
                silu_xbc(g)
                evacuate_x(g)

            act.preload_act_table(ACT.Silu)
            act.wait_ge(magic_ready, 1)
            act.wait_ge(x_in, X_DMA)
            mean_square(0)
            quantise(0)
            evacuate_q(0)
            act.wait_ge(w_in, 32)
            with act.Fori(0, NG - 1) as g:
                mean_square(g + 1)
                project(g)
                quantise(g + 1)
                evacuate_q(g + 1)
            project(NG - 1)

            act.preload_act_table_set("natural_log_exp_and_others")
            act.wait_ge(dt_v, 1)
            steps.link(act.activation(e_dt[:, :], na_dt[:, :], ACT.Exp))
            act.activation(l_dt[:, :], e_dt[:, :], ACT.Ln, bias=ones[:, 0:1])
            act.activation(a_log[:, :], r("A_log"), ACT.Exp).then_inc(dt_l, 1)
            act.preload_act_table(ACT.Tanh)

            def decays(g):
                act.wait_ge(y_psum, 2 * g)
                for j in range(GB):
                    act.wait_ge(ss_psum, GB * g + j + 1)
                    act.activation(ex[:, j].rearrange("p h l -> p (h l)"), bank[j % 2][:, :], ACT.Exp).then_inc(ex_ready, 1)

            def twice_x(g):
                act.wait_ge(var1_ready, g)
                act.activation(x2x[:, :, :], x_all[:, group(g), :], ACT.Copy, scale=2.0).then_inc(x2x_ready, 1)

            def y_square(g):
                act.wait_ge(msy_ready, GB * g)
                for j in range(GB):
                    act.wait_ge(y_ready, 2 * g + j // 2 + 1)
                    act.activation(junk[:, j, :], y[:, j, :], ACT.Square, scale=float(DI ** -0.5),
                                   accum_out=ms_y[:, j:j + 1]).then_inc(msy_ready, 1)

            def y_quantise(g):
                act.wait_ge(fout_ready, g + 1)
                act.wait_ge(yq_ready, g)
                for j in range(GB):
                    act.activation(y_qm[:, j, :], y_c[:, j, :], ACT.Identity, bias=magic_bias[:, 0:1],
                                   scale=f_out[:, batch(g, j)]).then_inc(yqm_ready, 1)

            def y_evacuate(g):
                act.wait_ge(yqt_psum, g + 1)
                act.activation(y_qT[:, :, :, :].rearrange("p b c l -> p (b c l)"), bank[0][:, :].bitcast(BF16),
                               ACT.Copy).then_inc(yqt_ready, 1)

            def x1_evacuate(g):
                act.wait_ge(x1t_psum, g + 1)
                act.activation(x1T[:, :, :].rearrange("p b l -> p (b l)"), bank[2][:, :], ACT.Copy).then_inc(x1t_ready, 1)

            def context_side(g):
                act.wait_ge(p_psum, 4 * g + 4)
                act.wait_ge(s2_psum, g)
                act.activation(p1[:, :], bank[4][:, 0:TS], ACT.Identity, bias=vec[:, 0:1], scale=INV_SQRT_D)
                act.activation(p2[:, :], bank[5][:, 0:TS], ACT.Identity, bias=vec[:, 1:2], scale=INV_SQRT_D)
                act.activation(row1[:, :], bank[6][0:1, 0:TS], ACT.Identity, bias=vec[0:1, 4:5], scale=INV_SQRT_D)
                act.activation(row2[:, :], bank[7][0:1, 0:TS], ACT.Identity, bias=vec[0:1, 5:6],
                               scale=INV_SQRT_D).then_inc(p_ready, 1)
                act.wait_ge(o_psum, GB * g)
                for i in range(2):
                    act.wait_ge(vvs_psum, 2 * g + i + 1)
                    act.activation(vvs[:, 2 * i:2 * i + 2, :].rearrange("p b c -> p (b c)"), bank[4 + i][0:LS, :],
                                   ACT.Copy).then_inc(vvs_ready, 1)

            def token_values(g):
                for i in range(2):
                    act.wait_ge(vvc_psum, 2 * g + i + 1)
                    act.activation(vvc[:, 2 * i:2 * i + 2, :].rearrange("p b c -> p (b c)"), bank[4 + i][:, :],
                                   ACT.Copy).then_inc(vvc_ready, 1)

            def softmax_exps(g):
                act.wait_ge(nmx1_ready, g + 1)
                act.wait_ge(e1n_ready, g)
                for j in range(GB):
                    act.activation(e1[:, j, :], bank[6][:, j * LS:(j + 1) * LS], ACT.Exp, bias=nmx1[:, j:j + 1],
                                   accum_out=den1[:, j:j + 1]).then_inc(e1_ready, 1)
                act.wait_ge(nmx2_ready, g + 1)
                act.wait_ge(w2i_psum, g)
                for j in range(GB):
                    act.activation(e2[:, j, :], bank[7][0:LS, j * L:(j + 1) * L], ACT.Exp, bias=nmx2[:, j:j + 1],
                                   accum_out=den2[:, j:j + 1]).then_inc(e2_ready, 1)

            def mixers(g):
                act.wait_ge(e1t_psum, g + 1)
                act.activation(e1T[:, :, :].rearrange("p b l -> p (b l)"), bank[4][0:LS, :], ACT.Copy).then_inc(e1t_ready, 1)
                act.wait_ge(w2i_psum, g + 1)
                act.activation(w2i[:, :, :].rearrange("p b l -> p (b l)"), bank[5][:, :], ACT.Copy).then_inc(w2i_ready, 1)

            def mixed(g):
                act.wait_ge(dif_ready, g)
                act.wait_ge(rs_ready, GB * g)
                for j in range(GB):
                    act.wait_ge(o_psum, GB * g + j + 1)
                    act.activation(s2c[:, j, :], bank[6 + j % 2][:, 256:384], ACT.Copy).then_inc(s2c_ready, 1)
                    act.activation(th[:, j, :], bank[6 + j % 2][:, 128:256], ACT.Tanh, scale=0.5).then_inc(th_ready, 1)

            def x2_evacuate(g):
                act.wait_ge(x2t_psum, g + 1)
                act.wait_ge(logit_psum, g)
                act.activation(x2T_s[:, :, :].rearrange("p b l -> p (b l)"), bank[4][:, :], ACT.Copy).then_inc(x2t_ready, 1)
                act.activation(x2T[:, bass.ds(g * T, T)], bank[4][:, :], ACT.Copy).then_inc(x2t_ready, 1)

            def attention_part(g):
                context_side(g)
                token_values(g)
                softmax_exps(g)
                mixers(g)
                mixed(g)
                x2_evacuate(g)

            def scan(g):
                twice_x(g)
                decays(g)
                y_square(g)
                y_quantise(g)
                y_evacuate(g)
                x1_evacuate(g)

            act.wait_ge(attw_ready, 1)
            scan(0)
            with act.Fori(0, NG - 1) as g:
                attention_part(g)
                scan(g + 1)
            attention_part(NG - 1)

            act.preload_act_table(ACT.Gelu)
            act.wait_ge(win_ready, 1)
            act.activation(sel_bf, c_("sel", 3 * E), ACT.Copy).then_inc(sel_ready, 1)
            act.wait_ge(logit_ready, NG)
            act.activation(score, logit[:, :, :], ACT.Tanh, scale=0.5).then_inc(score_ready, 1)

            def expert_hidden(g):
                act.wait_ge(gt_psum, g + 1)
                act.activation(gT, bank[5][0:3 * E, :], ACT.Copy).then_inc(gt_ready, 1)
                act.wait_ge(moe_psum, g)
                for t in range(NE):
                    act.wait_ge(h_psum, (NE + 1) * g + t + 1)
                    act.activation(hid[:, t, :], bank[t % 2][:, :], ACT.Gelu, bias=w("b1")[:, t:t + 1]).then_inc(hid_ready, 1)
                act.wait_ge(h_psum, (NE + 1) * (g + 1))
                act.activation(hid_s[0:HID, :], bank[NE % 2][0:HID, :], ACT.Gelu, bias=w("bs1", HID)).then_inc(hs_ready, 1)
                act.wait_ge(gb_psum, (NE + 1) * (g + 1))
                act.activation(hid_s[HID:96, :], bank[2 + NE % 2][HID:96, :], ACT.Copy).then_inc(hs_ready, 1)

            with act.Fori(0, NG) as g:
                expert_hidden(g)

        @block.vector
        def _(dve):
            steps = Steps(dve, dve_steps)
            dve.memset(magic_bias[:, :], MAGIC).then_inc(magic_ready, 1)
            dve.wait_ge(w_in, 32)
            win, wout = w("win"), w("wout")
            dve.tensor_reduce(wsum[:, 0:1], win, AXIS.X, ALU.add, apply_absolute_value=True)
            dve.tensor_reduce(wsum[:, 1:2], wout, AXIS.X, ALU.add, apply_absolute_value=True).then_inc(wsum_ready, 1)
            dve.wait_ge(wsum_psum, 1)
            steps.link(dve.tensor_copy(wscale[:, 0:2], bank[7][:, 0:2]))
            steps.link(dve.tensor_scalar(wscale[:, 0:1], wscale[:, 0:1], 1.0 / (772 * D), 1e-5, ALU.mult, ALU.max))
            steps.link(dve.tensor_scalar(wscale[:, 1:2], wscale[:, 1:2], 1.0 / (DI * D), 1e-5, ALU.mult, ALU.max))
            steps.link(dve.tensor_scalar(wscale[:, 2:4], wscale[:, 0:2], -0.5, None, ALU.mult))
            steps.link(dve.tensor_scalar(wscale[:, 0:2], wscale[:, 0:2], 0.5, None, ALU.mult))
            steps.link(dve.tensor_scalar(low[:, :], win, wscale[:, 2:3], None, ALU.is_lt))
            steps.link(dve.scalar_tensor_tensor(win_q[:, :], win, wscale[:, 0:1], low[:, :], ALU.is_gt, ALU.subtract))
            steps.link(dve.tensor_scalar(low[:, 0:DI], wout, wscale[:, 3:4], None, ALU.is_lt))
            dve.scalar_tensor_tensor(wout_q[:, :, :].rearrange("p a b -> p (a b)"), wout, wscale[:, 1:2],
                                     low[:, 0:DI], ALU.is_gt, ALU.subtract).then_inc(win_ready, 1)

            def settle():
                dve.sem_inc(dve_settled, 1)

            def input_stats(g):
                dve.wait_ge(u_ready, g + 1)
                dve.wait_ge(qm_ready, GB * g)
                for j in range(GB):
                    at = steps.mark(dve.bn_stats(stats[:, j, :], u[:, j, :]))
                steps.wait(at)
                settle()
                for j in range(GB):
                    at = steps.mark(dve.bn_aggr(mv_u[:, j, :], stats[:, j, :]))
                steps.wait(at)
                for j in range(GB):
                    at = steps.mark(dve.tensor_scalar(uc[:, j, :], u[:, j, :], mv_u[:, j, 0:1], None,
                                                      ALU.subtract))
                steps.wait(at)
                dve.tensor_reduce(amax_u[:, :], uc[:, :, :], AXIS.X, ALU.max,
                                  apply_absolute_value=True).then_inc(amax_ready, 1)

            def round_q(g):
                dve.wait_ge(f_ready, g + 1)
                dve.wait_ge(srow_psum, g)
                dve.wait_ge(qt_psum, g)
                for j in range(GB):
                    ins = dve.tensor_scalar(diag[:, j, :], ident, s_in[:, batch(g, j)], None, ALU.mult)
                ins.then_inc(diag_ready, 1)
                dve.wait_ge(qm_ready, GB * (g + 1))
                dve.tensor_scalar(q_bf[:, :, :], qm[:, :, :], MAGIC, None, ALU.subtract).then_inc(q_ready, 1)

            def conv(g):
                dve.wait_ge(srow_ready, g + 1)
                for c in range(NC):
                    dve.wait_ge(zx_psum, NC * g + c + 1)
                    dve.tensor_tensor(xs[:, c, :, TAPS - 1:], bank[c][:, :].rearrange("p (b l) -> p b l", b=GB),
                                      s_row[:, :].rearrange("p (b l) -> p b l", b=GB), ALU.mult).then_inc(xs_ready, 1)
                done = [0] * NC
                for k in range(TAPS - 2, -1, -1):
                    for c in range(NC):
                        if k == TAPS - 2:
                            dve.wait_ge(tap0_ready, NC * g + c + 1)
                        else:
                            steps.wait(done[c])
                        ins = dve.scalar_tensor_tensor(acc[:, c, :, :], xs[:, c, :, k:k + L],
                                                       w("conv_w")[:, c * TAPS + k:c * TAPS + k + 1],
                                                       acc[:, c, :, :], ALU.mult, ALU.add)
                        if k:
                            done[c] = steps.mark(ins)
                        else:
                            ins.then_inc(conv_ready, 1)

            def mask_g(g):
                dve.wait_ge(g_psum, g + 1)
                dve.tensor_tensor(g_all[:, group(g), :], bank[2][:, :].rearrange("p (b l) -> p b l", b=GB),
                                  upto.unsqueeze(1).to_broadcast([128, GB, L]), ALU.mult).then_inc(g_ready, 1)

            dve.wait_ge(c_in, 16)
            PER = 3 * GB + 2 * NC
            start = steps.base + steps.n
            steps.base, steps.n = start, 0
            input_stats(0)
            round_q(0)
            start, steps.n = start + steps.n, 0
            with dve.Fori(0, NG - 1) as g:
                steps.enter(start, g, PER)
                input_stats(g + 1)
                conv(g)
                mask_g(g)
                round_q(g + 1)
                steps.leave(start, NG - 1, PER)
            conv(NG - 1)
            mask_g(NG - 1)
            start, steps.base = steps.base + steps.n, steps.base + steps.n
            steps.n = 0

            dve.wait_ge(a_psum, 1)
            dve.tensor_copy(a1T[:, :], bank[0][:, 0:128])
            dve.tensor_copy(a2T[:, :], bank[0][:, 128:256])
            dve.tensor_copy(wvs[:, 128:256], bank[0][:, 256:384])
            dve.tensor_copy(wvc[:, 0:128], bank[0][:, 384:512])
            dve.tensor_copy(wvs[:, 0:128], w("wv_sT"))
            dve.tensor_copy(wvc[:, 128:256], w("wv_cT"))
            dve.tensor_scalar(vec[:, 0:2], bank[1][:, 0:2], INV_SQRT_D, None, ALU.mult)
            dve.tensor_copy(vec[:, 2:4], bank[1][:, 2:4])
            dve.tensor_scalar(vec[0:1, 4:6], bank[1][0:1, 4:6], INV_SQRT_D, None, ALU.mult)
            dve.tensor_copy(brow[:, 0:128], r("bv_s", 1))
            dve.tensor_tensor(brow[:, 128:256], bank[1][0:1, 8:136], r("bg", 1), ALU.add)
            dve.tensor_copy(brow[:, 256:384], bank[1][0:1, 136:264])
            dve.tensor_copy(brow[:, 384:512], r("bv_c", 1)).then_inc(attw_ready, 1)

            dve.wait_ge(zd_ready, GB * NG)
            steps.link(dve.tensor_tensor(v_dt[:, :].rearrange("p (b h) -> p b h", h=NH), dt_tok[:, :, :],
                                         r("dt_bias").unsqueeze(1).to_broadcast([128, NB, NH]), ALU.add))
            dve.scalar_tensor_tensor(na_dt[:, :], v_dt[:, :], -1.0, v_dt[:, :], ALU.mult, ALU.min).then_inc(dt_v, 1)
            dve.wait_ge(dt_l, 1)
            steps.link(dve.scalar_tensor_tensor(dt_sp[:, :, :].rearrange("p b h -> p (b h)"), v_dt[:, :], 0.0, l_dt[:, :],
                                                ALU.max, ALU.add))
            dve.scalar_tensor_tensor(a_dt[:, :, :], dt_sp[:, :, :], -1.0, a_log[:, :].unsqueeze(1).to_broadcast([128, NB, NH]),
                                     ALU.mult, ALU.mult).then_inc(dt_ready, 1)

            def decay_gram(g):
                for j in range(GB):
                    dve.wait_ge(ex_ready, GB * g + j + 1)
                    dve.tensor_tensor(ex[:, j], ex[:, j],
                                      g_all[:, batch(g, j), :].to_broadcast([128, NH, L]),
                                      ALU.mult).then_inc(m_ready, 1)

            def gate_y(g):
                dve.wait_ge(u_dt_ready, GB * (g + 1))
                dve.wait_ge(yw_ready, 2 * g)
                dve.wait_ge(msy_ready, GB * g)
                for i in range(2):
                    dve.wait_ge(y_psum, 2 * g + i + 1)
                    pair = y[:, 2 * i:2 * i + 2, :]
                    steps.link(dve.tensor_tensor(pair, bank[2 + i][:, :].rearrange("p (b c) -> p b c", b=2),
                                                 x_d[:, 2 * i:2 * i + 2, :], ALU.add))
                    dve.tensor_tensor(pair, pair, z_tok[:, bass.ds(g * GB + 2 * i, 2), :], ALU.mult).then_inc(y_ready, 1)

            def moments(g, src, stats_to, mv_to):
                for j in range(GB):
                    at = steps.mark(dve.bn_stats(stats_to[:, j, :], src[:, j, :]))
                steps.wait(at)
                settle()
                for j in range(GB):
                    ins = dve.bn_aggr(mv_to[:, j, :], stats_to[:, j, :])
                return ins

            def y_stats(g):
                dve.wait_ge(yw_ready, 2 * (g + 1))
                dve.wait_ge(yqm_ready, GB * g)
                steps.link(moments(g, y_w, stats_s, mv_y))
                for j in range(GB):
                    at = steps.mark(dve.tensor_scalar(y_c[:, j, :], y_w[:, j, :], mv_y[:, j, 0:1], None,
                                                      ALU.subtract))
                steps.wait(at)
                dve.tensor_reduce(amax_y[:, :], y_c[:, :, :], AXIS.X, ALU.max,
                                  apply_absolute_value=True).then_inc(amaxy_ready, 1)

            def y_round(g):
                dve.wait_ge(yqm_ready, GB * (g + 1))
                dve.wait_ge(yqt_psum, g)
                dve.tensor_scalar(y_q[:, :, :], y_qm[:, :, :], MAGIC, None, ALU.subtract).then_inc(yq_ready, 1)

            def first_norm(g):
                dve.wait_ge(proj_psum, g + 1)
                dve.wait_ge(x2x_ready, g + 1)
                for j in range(GB):
                    at = steps.mark(dve.scalar_tensor_tensor(res1[:, j, :], bank[1][:, j * D:(j + 1) * D],
                                                             s_out[:, batch(g, j)], x2x[:, j, :], ALU.mult, ALU.add))
                steps.wait(at)
                moments(g, res1, stats_s, mv1).then_inc(var1_ready, 1)
                dve.wait_ge(rstd1_ready, g + 1)
                dve.wait_ge(x1t_psum, g)
                for j in range(GB):
                    at = steps.mark(dve.tensor_scalar(x1_s[:, j, :], res1[:, j, :], mv1[:, j, 0:1],
                                                      rstd1[:, j:j + 1], ALU.subtract, ALU.mult))
                steps.wait(at)
                dve.tensor_copy(x1[:, group(g), :], x1_s[:, :, :]).then_inc(x1_ready, 1)

            def softmaxes(g):
                dve.wait_ge(s1_psum, g + 1)
                dve.wait_ge(e1_ready, GB * g)
                dve.tensor_reduce(nmx1[:, :], bank[6][:, 0:TS].rearrange("p (b k) -> p b k", b=GB), AXIS.X, ALU.max,
                                  negate=True).then_inc(nmx1_ready, 1)
                dve.wait_ge(s2_psum, g + 1)
                dve.wait_ge(e2_ready, GB * g)
                dve.tensor_reduce(nmx2[:, :], bank[7][0:LS, :].rearrange("p (b k) -> p b k", b=GB), AXIS.X, ALU.max,
                                  negate=True).then_inc(nmx2_ready, 1)
                dve.wait_ge(e1_ready, GB * (g + 1))
                dve.wait_ge(e1t_psum, g)
                steps.link(dve.reciprocal(rden1[:, :], den1[:, :]))
                dve.tensor_tensor(e1n[:, :, :], e1[:, :, :], rden1[:, :].unsqueeze(2).to_broadcast([128, GB, LS]),
                                  ALU.mult).then_inc(e1n_ready, 1)
                dve.wait_ge(e2_ready, GB * (g + 1))
                dve.wait_ge(w2i_psum, g)
                steps.link(dve.reciprocal(rden2[:, :], den2[:, :]))
                for j in range(GB):
                    ins = dve.tensor_scalar(ipn[:, j, :], c_("interp", LS), rden2[:, j:j + 1], None, ALU.mult)
                ins.then_inc(ipn_ready, 1)

            def blend(g):
                for j in range(GB):
                    dve.wait_ge(s2c_ready, GB * g + j + 1)
                    dve.wait_ge(th_ready, GB * g + j + 1)
                    dve.tensor_tensor(dif[:, j, :], bank[6 + j % 2][:, 0:D], s2c[:, j, :], ALU.subtract).then_inc(dif_part, 1)
                dve.wait_ge(dif_part, GB * (g + 1))
                steps.link(dve.scalar_tensor_tensor(dif[:, :, :], th[:, :, :], 1.0, dif[:, :, :], ALU.add, ALU.mult))
                dve.wait_ge(rs_ready, GB * (g + 1))
                dve.scalar_tensor_tensor(res2[:, :, :], dif[:, :, :], 0.5, s2c_x1[:, :, :], ALU.mult,
                                         ALU.add).then_inc(dif_ready, 1)

            def second_norm(g):
                dve.wait_ge(dif_ready, g + 1)
                moments(g, res2, stats_x, mv2).then_inc(var2_ready, 1)
                dve.wait_ge(rstd2_ready, g + 1)
                dve.wait_ge(x2t_psum, g)
                dve.wait_ge(x2b_ready, g)
                for j in range(GB):
                    ins = dve.tensor_scalar(x2_s[:, j, :], res2[:, j, :], mv2[:, j, 0:1],
                                            rstd2[:, j:j + 1], ALU.subtract, ALU.mult)
                ins.then_inc(x2_ready, 1)

            def router_logits(g):
                dve.wait_ge(logit_psum, g + 1)
                dve.tensor_copy(logit[:, group(g), :], bank[5][:, 0:GB * E].rearrange("p (b e) -> p b e", e=E))\
                   .then_inc(logit_ready, 1)

            def scan(g):
                decay_gram(g)
                gate_y(g)
                y_stats(g)
                y_round(g)
                first_norm(g)

            def attention(g):
                softmaxes(g)
                blend(g)
                second_norm(g)
                router_logits(g)

            start = steps.base + steps.n
            S_PER = 2 + GB + 1 + GB + GB + GB + GB
            X_PER = 2 + 1 + GB
            steps.base, steps.n = start, 0
            scan(0)
            steps.leave(start, 1, S_PER)
            start += S_PER
            with dve.Fori(0, NG - 1) as g:
                steps.enter(start, g, S_PER + X_PER)
                attention(g)
                scan(g + 1)
                steps.leave(start, NG - 1, S_PER + X_PER)
            attention(NG - 1)

            bc = lambda v: v.unsqueeze(2).to_broadcast([128, NB, E])
            dve.wait_ge(score_ready, 1)
            steps.link(dve.tensor_scalar(score, score, 0.5, 0.5, ALU.mult, ALU.add))
            steps.link(dve.tensor_scalar(score, score, r("route_scale"), None, ALU.mult))
            prio = c_("prio").unsqueeze(1).to_broadcast([128, NB, E])

            def pick_largest(src, largest, mask):
                steps.link(dve.tensor_reduce(largest[:, :], src, AXIS.X, ALU.max))
                steps.link(dve.tensor_tensor(pick, src, bc(largest[:, :]), ALU.is_equal))
                steps.link(dve.tensor_tensor(pick, pick, prio, ALU.mult))
                steps.link(dve.tensor_reduce(prio1[:, :], pick, AXIS.X, ALU.max))
                steps.link(dve.tensor_tensor(mask, pick, bc(prio1[:, :]), ALU.is_equal))

            pick_largest(score, max1, first)
            steps.link(dve.scalar_tensor_tensor(rest, first, -3.0e38, score, ALU.mult, ALU.add))
            pick_largest(rest, max2, second)
            steps.link(dve.tensor_tensor(first, first, second, ALU.add))
            steps.link(dve.tensor_tensor(max1[:, :], max1[:, :], max2[:, :], ALU.add))
            steps.link(dve.reciprocal(max2[:, :], max1[:, :]))
            steps.link(dve.tensor_tensor(first, first, score, ALU.mult))
            steps.link(dve.tensor_tensor(top, first, bc(max2[:, :]), ALU.mult))
            steps.link(dve.tensor_copy(gate3[:, :, 0:E], top))
            steps.link(dve.tensor_tensor(rest, top, gate3[:, :, 0:E], ALU.subtract))
            steps.link(dve.tensor_copy(gate3[:, :, E:2 * E], rest))
            steps.link(dve.tensor_tensor(pick, rest, gate3[:, :, E:2 * E], ALU.subtract))
            dve.tensor_copy(gate3[:, :, 2 * E:3 * E], pick).then_inc(gate_ready, 1)

            def gate_hidden(g):
                for t in range(NE):
                    dve.wait_ge(hid_ready, NE * g + t + 1)
                    dve.wait_ge(gb_psum, (NE + 1) * g + t + 1)
                    dve.tensor_tensor(hid[:, t, :], hid[:, t, :], bank[2 + t % 2][:, :], ALU.mult).then_inc(hg_ready, 1)

            def last_norm(g):
                dve.wait_ge(moe_psum, g + 1)
                steps.link(dve.tensor_tensor(res3, bank[6][:, :].rearrange("p (b d) -> p b d", b=GB),
                                             x2b[:, group(g), :], ALU.add))
                moments(g, res3, stats_o, mv3).then_inc(var3_ready, 1)
                dve.wait_ge(rstd3_ready, g + 1)
                dve.wait_ge(out_done, 16 * g)
                for j in range(GB):
                    ins = dve.tensor_scalar(y_out[:, j, :], res3[:, j, :], mv3[:, j, 0:1],
                                            rstd3[:, j:j + 1], ALU.subtract, ALU.mult)
                ins.then_inc(yout_ready, 1)

            start = steps.base + steps.n
            with dve.Fori(0, NG) as g:
                steps.enter(start, g, 1 + GB)
                gate_hidden(g)
                last_norm(g)
                steps.leave(start, NG, 1 + GB)

        @block.tensor
        def _(pe):
            def transpose_q(g):
                pe.wait_ge(diag_ready, g + 1)
                pe.wait_ge(srow_ready, g)
                pe.matmul(bank[5][:, :], ones[:, :], diag[:, :, :].rearrange("p b l -> p (b l)"),
                          start=True, stop=True).then_inc(srow_psum, 1)
                pe.wait_ge(q_ready, g + 1)
                pe.wait_ge(qt_ready, g)
                for j in range(GB):
                    ins = pe.transpose(bank[4][:, j * 64:(j + 1) * 64].bitcast(BF16), q_bf[:, j, :], ident_bf[:, :])
                ins.then_inc(qt_psum, 1)

            def project(g):
                pe.wait_ge(qt_ready, g + 1)
                pe.wait_ge(xtok_ready, 2 * g)
                pe.wait_ge(g_ready, g)
                for c in range(NC):
                    pe.matmul(bank[c][:, :], win_q[:, c * 128:(c + 1) * 128], qT[:, bass.ds(g * T, T)],
                              start=True, stop=True).then_inc(zx_psum, 1)
                for j in range(GB):
                    pe.wait_ge(zd_ready, GB * g + max(j - 1, 0))
                    pe.matmul(bank[6 + j % 2][:, 0:DI + NH], qT[:, bass.ds(g * T + j * L, L)],
                              win_q[:, 512:772], start=True, stop=True).then_inc(zd_psum, 1)

            def mix(g):
                pe.wait_ge(silu_ready, NC * (g + 1))
                for j in range(GB):
                    ins = pe.matmul(bank[2][:, j * L:(j + 1) * L], xbc[:, 2, j, :], xbc[:, 3, j, :],
                                    start=True, stop=True)
                ins.then_inc(g_psum, 1)
                for j in range(GB):
                    for c in range(2):
                        col = (j % 2) * DI + c * 128
                        ins = pe.transpose(bank[j // 2][:, col:col + 128], xbc[:, c, j, :], ident)
                    if j % 2:
                        ins.then_inc(xt_psum, 1)

            pe.wait_ge(consts_ready, N_CONSTS)
            pe.wait_ge(wsum_ready, 1)
            pe.matmul(bank[7][:, 0:2], ones[:, :], wsum[:, :], start=True, stop=True).then_inc(wsum_psum, 1)
            pe.wait_ge(c_in, 16)
            pe.wait_ge(ident_ready, 1)
            transpose_q(0)
            pe.wait_ge(win_ready, 1)
            with pe.Fori(0, NG - 1) as g:
                project(g)
                mix(g)
                transpose_q(g + 1)
            project(NG - 1)
            mix(NG - 1)

            pe.wait_ge(xtok_ready, 2 * NG)
            pe.wait_ge(zd_ready, GB * NG)
            pe.wait_ge(g_ready, NG)

            for at, lhs, rhs in ((0, w("wk_s"), w("wq_c")), (128, w("wq_s"), w("wk_c")),
                                 (256, w("wv_s"), w("wgT")[:, 0:128]), (384, w("wv_c"), w("wgT")[:, 128:256])):
                pe.matmul(bank[0][:, at:at + 128], lhs, rhs, start=True, stop=True)
            for at, lhs, rhs in ((0, w("wq_c"), w("bk_s")), (1, w("wk_c"), w("bq_s")),
                                 (2, w("wk_s"), w("bq_c")), (3, w("wq_s"), w("bk_c"))):
                pe.matmul(bank[1][:, at:at + 1], lhs, rhs, start=True, stop=True)
            for at, lhs, rhs in ((4, w("bq_c"), w("bk_s")), (5, w("bq_s"), w("bk_c")),
                                 (8, w("bv_s"), w("wgT")[:, 0:128]), (136, w("bv_c"), w("wgT")[:, 128:256])):
                ins = pe.matmul(bank[1][0:1, at:at + rhs.shape[1]], lhs, rhs, start=True, stop=True)
            ins.then_inc(a_psum, 1)

            def log_decays(g):
                pe.wait_ge(x1t_psum, g)
                for j in range(GB):
                    pe.wait_ge(seg_ready, GB * g + j + 1)
                    if j == 0:
                        pe.wait_ge(yqt_ready, g)
                    elif j == 1:
                        pe.wait_ge(var1_ready, g)
                    else:
                        pe.wait_ge(ex_ready, GB * g + j - 1)
                    pe.matmul(bank[j % 2][:, :], after, seg[:, j].rearrange("p h l -> p (h l)"),
                              start=True, stop=True).then_inc(ss_psum, 1)

            def scan_out(g):
                pe.wait_ge(y_ready, 2 * g)
                pe.wait_ge(x1t_ready, g)
                for j in range(GB):
                    pe.wait_ge(m_ready, GB * g + j + 1)
                    pe.wait_ge(u_dt_ready, GB * g + j + 1)
                    for h in range(NH):
                        ins = pe.matmul(bank[2 + j // 2][:, (j % 2) * DI + h * HD:(j % 2) * DI + (h + 1) * HD],
                                        ex[:, j, h, :], u_dt[:, j, h * HD:(h + 1) * HD], start=True, stop=True)
                    if j % 2:
                        ins.then_inc(y_psum, 1)

            def project_out(g):
                pe.wait_ge(yq_ready, g + 1)
                pe.wait_ge(ex_ready, GB * (g + 1))
                for j in range(GB):
                    for c in range(2):
                        ins = pe.transpose(bank[0][:, (2 * j + c) * 64:(2 * j + c + 1) * 64].bitcast(BF16),
                                           y_q[:, j, c * 128:(c + 1) * 128], ident_bf[:, :])
                ins.then_inc(yqt_psum, 1)
                pe.wait_ge(yqt_ready, g + 1)
                for j in range(GB):
                    for c in range(2):
                        ins = pe.matmul(bank[1][:, j * D:(j + 1) * D], y_qT[:, j, c, :], wout_q[:, c, :],
                                        start=c == 0, stop=c == 1)
                ins.then_inc(proj_psum, 1)

            def transpose_x1(g):
                pe.wait_ge(x1_ready, g + 1)
                for j in range(GB):
                    ins = pe.transpose(bank[2][:, j * L:(j + 1) * L], x1_s[:, j, :], ident)
                ins.then_inc(x1t_psum, 1)

            def context_side(g):
                pe.wait_ge(ctx_in, 16 * (g + 1))
                pe.wait_ge(x2t_ready, 2 * g)
                pe.wait_ge(logit_ready, g)
                pe.wait_ge(dif_ready, g)
                pe.matmul(bank[4][:, 0:TS], a1T[:, :], ctx_s[:, :], start=True, stop=True).then_inc(p_psum, 1)
                pe.matmul(bank[5][:, 0:TS], a2T[:, :], ctx_s[:, :], start=True, stop=True).then_inc(p_psum, 1)
                pe.matmul(bank[6][0:1, 0:TS], vec[:, 2:3], ctx_s[:, :], start=True, stop=True).then_inc(p_psum, 1)
                pe.matmul(bank[7][0:1, 0:TS], vec[:, 3:4], ctx_s[:, :], start=True, stop=True).then_inc(p_psum, 1)
                pe.wait_ge(p_ready, g + 1)
                for j in range(GB):
                    o = bank[4 + j // 2][0:LS, (j % 2) * 256:(j % 2 + 1) * 256]
                    pe.matmul(o, ctx_s[:, j * LS:(j + 1) * LS], wvs[:, :], start=True, stop=False)
                    ins = pe.matmul(o, ones[0:1, 0:LS], brow[:, 0:256], start=False, stop=True)
                    if j % 2:
                        ins.then_inc(vvs_psum, 1)

            def scores(g):
                pe.wait_ge(x1t_ready, g + 1)
                for j in range(GB):
                    o = bank[6][:, j * LS:(j + 1) * LS]
                    pe.matmul(o, x1T[:, j, :], p1[:, j * LS:(j + 1) * LS], start=True, stop=False)
                    ins = pe.matmul(o, ones[0:1, :], row1[:, j * LS:(j + 1) * LS], start=False, stop=True)
                ins.then_inc(s1_psum, 1)
                for j in range(GB):
                    o = bank[7][0:LS, j * L:(j + 1) * L]
                    pe.matmul(o, p2[:, j * LS:(j + 1) * LS], x1T[:, j, :], start=True, stop=False)
                    ins = pe.matmul(o, row2[:, j * LS:(j + 1) * LS], ones[0:1, :], start=False, stop=True)
                ins.then_inc(s2_psum, 1)
                for j in range(GB):
                    if j % 2 == 0:
                        pe.wait_ge(vvs_ready, 2 * g + j // 2 + 1)
                    o = bank[4 + j // 2][:, (j % 2) * 256:(j % 2 + 1) * 256]
                    pe.matmul(o, x1T[:, j, :], wvc[:, :], start=True, stop=False)
                    ins = pe.matmul(o, ones[0:1, :], brow[:, 256:512], start=False, stop=True)
                    if j % 2:
                        ins.then_inc(vvc_psum, 1)

            def mixers(g):
                pe.wait_ge(e1n_ready, g + 1)
                pe.wait_ge(vvc_ready, 2 * (g + 1))
                for j in range(GB):
                    ins = pe.transpose(bank[4][0:LS, j * L:(j + 1) * L], e1n[:, j, :], ident)
                ins.then_inc(e1t_psum, 1)
                pe.wait_ge(ipn_ready, g + 1)
                for j in range(GB):
                    ins = pe.matmul(bank[5][:, j * L:(j + 1) * L], e2[:, j, :], ipn[:, j, :], start=True, stop=True)
                ins.then_inc(w2i_psum, 1)

            def attend(g):
                pe.wait_ge(e1t_ready, g + 1)
                pe.wait_ge(w2i_ready, g + 1)
                for j in range(GB):
                    if j >= 2:
                        pe.wait_ge(dif_part, GB * g + j - 1)
                    b = bank[6 + j % 2]
                    pe.matmul(b[:, 0:256], e1T[:, j, :], vvs[:, j, :], start=True, stop=False)
                    pe.matmul(b[:, 128:256], w2i[:, j, :], vvc[:, j, 0:128], start=False, stop=True)
                    pe.matmul(b[:, 256:384], w2i[:, j, :], vvc[:, j, 128:256], start=True, stop=True).then_inc(o_psum, 1)

            def transpose_x2(g):
                pe.wait_ge(x2_ready, g + 1)
                for j in range(GB):
                    ins = pe.transpose(bank[4][:, j * L:(j + 1) * L], x2_s[:, j, :], ident)
                ins.then_inc(x2t_psum, 1)
                pe.wait_ge(x2t_ready, 2 * g + 1)
                for j in range(GB):
                    ins = pe.matmul(bank[5][:, j * E:(j + 1) * E], x2T_s[:, j, :], w("gate_w"), start=True, stop=True)
                ins.then_inc(logit_psum, 1)

            def scan(g):
                log_decays(g)
                scan_out(g)
                project_out(g)
                transpose_x1(g)

            def attention(g):
                context_side(g)
                scores(g)
                mixers(g)
                attend(g)
                transpose_x2(g)

            pe.wait_ge(attw_ready, 1)
            scan(0)
            with pe.Fori(0, NG - 1) as g:
                attention(g)
                scan(g + 1)
            attention(NG - 1)

            pe.wait_ge(gate_ready, 1)
            pe.wait_ge(sel_ready, 1)
            pe.wait_ge(x2t_ready, 2 * NG)
            pe.wait_ge(logit_ready, NG)

            def up(g):
                pe.wait_ge(moe_psum, g)
                pe.wait_ge(gb_psum, (NE + 1) * g)
                for j in range(GB):
                    ins = pe.matmul(bank[5][0:3 * E, j * L:(j + 1) * L],
                                    gate3[:, batch(g, j), :].rearrange("p a e -> p (a e)"), ident_bf[:, :],
                                    start=True, stop=True)
                ins.then_inc(gt_psum, 1)
                pe.wait_ge(gt_ready, g + 1)
                for t in range(NE + 1):
                    if t >= 2:
                        pe.wait_ge(hid_ready, NE * g + t - 1)
                        pe.wait_ge(hg_ready, NE * g + t - 1)
                    elif t == 1:
                        pe.wait_ge(hg_ready, NE * g)
                    else:
                        pe.wait_ge(hs_ready, 2 * g)
                    pe.matmul(bank[2 + t % 2][:, :], sel_bf[:, t * 128:(t + 1) * 128], gT,
                              start=True, stop=True).then_inc(gb_psum, 1)
                    if t < NE:
                        pe.matmul(bank[t % 2][:, :], w("w1")[:, t * 128:(t + 1) * 128], x2T[:, bass.ds(g * T, T)],
                                  start=True, stop=True).then_inc(h_psum, 1)
                    else:
                        pe.matmul(bank[t % 2][0:HID, :], w("ws1"), x2T[:, bass.ds(g * T, T)],
                                  start=True, stop=True).then_inc(h_psum, 1)

            def down(g):
                pe.wait_ge(hg_ready, NE * (g + 1))
                pe.wait_ge(hs_ready, 2 * (g + 1))
                pe.wait_ge(var3_ready, g)
                for j in range(GB):
                    for t in range(NE):
                        pe.matmul(bank[6][:, j * D:(j + 1) * D], hid[:, t, j * L:(j + 1) * L],
                                  w("w2")[:, t * D:(t + 1) * D], start=t == 0, stop=False)
                    ins = pe.matmul(bank[6][:, j * D:(j + 1) * D], hid_s[0:96, j * L:(j + 1) * L], w("w2s", 96),
                                    start=False, stop=True)
                ins.then_inc(moe_psum, 1)

            with pe.Fori(0, NG) as g:
                up(g)
                down(g)


def kernel(**inputs):
    import numpy as _np
    import concourse.bacc as _bacc
    from concourse import mybir as _mybir
    from concourse.bass_utils import run_bass_kernel_spmd as _run

    a = {k.removeprefix("L0_"): _np.asarray(v) for k, v in inputs.items()}
    f32 = _np.float32

    def tiles(m):
        n = m.shape[0] // 128
        return m.reshape(n, 128, -1).transpose(1, 0, 2).reshape(128, -1)

    def column(v):
        out = _np.zeros((128, 1), f32)
        out[:v.shape[0], 0] = v
        return out

    w_in = a["attn_in_proj_w"]
    w2s = _np.zeros((128, 128), f32)
    w2s[:HID] = a["ffn_Ws2"]
    w2s[HID:HID + E] = a["ffn_b2"]
    parts = {
        "win": _np.concatenate([w_in[DI:DI + 512], w_in[:DI], w_in[DI + 512:]]).T,
        "wout": tiles(a["attn_out_proj_w"].T),
        "conv_w": tiles(a["attn_conv_w"]), "conv_b": tiles(a["attn_conv_b"][:, None]),
        "wq_c": a["xattn_Wq_c"], "wk_s": a["xattn_Wk_s"], "wq_s": a["xattn_Wq_s"], "wk_c": a["xattn_Wk_c"],
        "wv_s": a["xattn_Wv_s"], "wv_sT": a["xattn_Wv_s"].T, "wv_c": a["xattn_Wv_c"], "wv_cT": a["xattn_Wv_c"].T,
        "wgT": tiles(a["xattn_Wg"].T),
        "bq_c": a["xattn_bq_c"][:, None], "bk_s": a["xattn_bk_s"][:, None],
        "bq_s": a["xattn_bq_s"][:, None], "bk_c": a["xattn_bk_c"][:, None],
        "bv_s": a["xattn_bv_s"][:, None], "bv_c": a["xattn_bv_c"][:, None],
        "gate_w": a["ffn_gate_W"], "w1": a["ffn_W1"].transpose(1, 0, 2).reshape(D, E * HID), "ws1": a["ffn_Ws1"],
        "b1": tiles(a["ffn_b1"].reshape(-1, 1)), "bs1": column(a["ffn_bs1"]),
        "w2": tiles(a["ffn_W2"].reshape(E * HID, D)), "w2s": w2s,
    }
    wpack = _np.concatenate([parts[n] for n, _ in _COLS], axis=1)
    rows = {
        "norm_w": a["attn_norm_w"], "out_norm_w": a["attn_out_norm_w"], "Dp": a["attn_Dp"],
        "A_log": a["attn_A_log"], "dt_bias": a["attn_dt_bias"], "bg": a["xattn_bg"],
        "bv_s": a["xattn_bv_s"], "bv_c": a["xattn_bv_c"], "bs2": a["ffn_bs2"],
        "route_scale": a["ffn_route_scale"].reshape(1),
    }
    rpack = _np.concatenate([rows[n] for n, _ in _ROWS])

    i = _np.arange(128)
    interp = _np.zeros((128, L), f32)
    pos = _np.clip((_np.arange(L, dtype=f32) + f32(0.5)) * f32(LS / L) - f32(0.5), f32(0.0), f32(LS - 1))
    lo = _np.floor(pos).astype(_np.int32)
    hi = _np.minimum(lo + 1, LS - 1)
    frac = (pos - lo.astype(f32)).astype(f32)
    for l in range(L):
        interp[lo[l], l] += f32(1) - frac[l]
        interp[hi[l], l] += frac[l]
    sel = _np.zeros((128, NE + 1, 128), f32)
    for part in range(3):
        for e in range(E):
            sel[part * E + e, e * HID // 128, e * HID % 128:e * HID % 128 + HID] = 1
            sel[part * E + e, NE, HID + e] = 1
    prio = _np.broadcast_to(_np.arange(E, 0, -1).astype(f32), (128, E))
    cpack = _np.concatenate([_np.eye(128, dtype=f32), (i[:, None] <= i[None, :]).astype(f32),
                             (i[:, None] > i[None, :]).astype(f32), interp, sel.reshape(128, -1), prio], axis=1)

    arrays = {"x": a["x"], "ctxT": a["ctx_1024"].transpose(2, 0, 1).reshape(D, NB * LS),
              "wpack": wpack, "rpack": rpack, "cpack": cpack}
    nc = _bacc.Bacc("TRN2", target_bir_lowering=False, num_devices=1)
    args = []
    for name in arrays:
        arrays[name] = _np.ascontiguousarray(arrays[name])
        args.append(nc.dram_tensor(name, arrays[name].shape, _mybir.dt.from_np(arrays[name].dtype),
                                   kind="ExternalInput").ap())
    args.append(nc.dram_tensor("out", (NB, L, D), FP32, kind="ExternalOutput").ap())
    build(nc, *args)
    res = _run(nc, [arrays], core_ids=[0])
    return res.results[0]["out"]
```

```python
import numpy as np
import concourse.bass as bass
from concourse import mybir
from contextlib import ExitStack

FP32 = mybir.dt.float32
BF16 = mybir.dt.bfloat16
ALU = mybir.AluOpType
ACT = mybir.ActivationFunctionType
AXIS = mybir.AxisListType

NB, L, D = 16, 128, 128
LS = 77
GB = 2
NG = NB // GB
T = GB * L
TS = GB * LS
DI, NH, HD = 256, 4, 64
NC = 4
TAPS = 4
E, HID = 8, 64
NE = E * HID // 128
MAGIC = 12582912.0
FB = 4
NF = NB // FB
FT = FB * L
INV_SQRT_D = float(1.0 / np.sqrt(np.float32(D)))

_COLS = [("win", 772), ("wout", 256), ("conv_w", NC * TAPS), ("conv_b", NC),
         ("wq_c", 128), ("wk_s", 128), ("wq_s", 128), ("wk_c", 128),
         ("wv_s", 128), ("wv_sT", 128), ("wv_c", 128), ("wv_cT", 128), ("wgT", 256),
         ("bq_c", 1), ("bk_s", 1), ("bq_s", 1), ("bk_c", 1), ("bv_s", 1), ("bv_c", 1),
         ("gate_w", E), ("w1", 512), ("ws1", HID), ("b1", NE), ("bs1", 1),
         ("w2", 512), ("w2s", 128)]
_ROWS = [("norm_w", D), ("out_norm_w", DI), ("Dp", NH), ("A_log", NH), ("dt_bias", NH),
         ("bg", 128), ("bv_s", 128), ("bv_c", 128), ("bs2", D), ("route_scale", 1)]
_CONSTS = [("ident", 128), ("upto", 128), ("after", 128), ("interp", 128), ("sel", (NE + 1) * 128), ("prio", E)]


def _places(cols):
    at, out = 0, {}
    for name, n in cols:
        out[name] = (at, at + n)
        at += n
    return out, at


COL, NCOL = _places(_COLS)
ROW, NROW = _places(_ROWS)
CST, NCST = _places(_CONSTS)


class Steps:

    def __init__(self, eng, sem):
        self.eng, self.sem, self.base, self.n = eng, sem, 0, 0

    def mark(self, ins):
        ins.then_inc(self.sem, 1)
        self.n += 1
        return self.base + self.n

    def wait(self, count):
        self.eng.wait_ge(self.sem, count)

    def link(self, ins):
        self.wait(self.mark(ins))

    def total(self):
        return self.base + self.n

    def enter(self, start, steps, per):
        self.base, self.n = start + steps * per, 0

    def leave(self, start, steps, per):
        assert self.n == per, (self.n, per)
        self.base, self.n = start + steps * per, 0


def build(nc, x, ctxT, wpack, rpack, cpack, out):
    ctx = ExitStack()
    with ctx:
        def sb(name, shape, dt=FP32):
            return ctx.enter_context(nc.sbuf_tensor(name, shape, dt))

        def sem(name):
            return ctx.enter_context(nc.semaphore(name))

        counters = []

        def counter(name):
            counters.append(sem(name))
            return counters[-1]

        def did(n):
            return n + 1

        W = sb("W", [128, NCOL])
        R = sb("R", [128, NROW])
        C = sb("C", [128, NCST])

        def w(name, rows=128):
            a, b = COL[name]
            return W[0:rows, a:b]

        def r(name, rows=128):
            a, b = ROW[name]
            return R[0:rows, a:b]

        def c_(name, rows=128):
            a, b = CST[name]
            return C[0:rows, a:b]

        ident, upto, after = c_("ident"), c_("upto"), c_("after")
        ident_bf = sb("ident_bf", [128, 128], BF16)
        ones = sb("ones", [128, 128])
        neg_half = sb("neg_half", [128, GB])
        neg_one = sb("neg_one", [128, GB])
        neg_half4 = sb("neg_half4", [128, FB])
        eps5 = sb("eps5", [128, FB])
        magic_bias = sb("magic_bias", [128, 1])
        win_q = sb("win_q", [128, 772], BF16)
        wout_q = sb("wout_q", [128, 2, 128], BF16)
        low = sb("low", [128, 772])
        wsum = sb("wsum", [128, 2])
        wscale = sb("wscale", [128, 4])
        ident_d = sb("ident_d", [128, NH, 128])
        a_exp = sb("a_exp", [128, NH])
        a1T = sb("a1T", [128, 128])
        a2T = sb("a2T", [128, 128])
        wvs = sb("wvs", [128, 256])
        wvc = sb("wvc", [128, 256])
        vec = sb("vec", [128, 6])
        cvec2 = sb("cvec2", [128, 1])
        bq_all = sb("bq_all", [128, 2, 128])
        cv1 = sb("cv1", [128, 128])
        bcol = sb("bcol", [128, 2, 128])

        x_all = sb("x_all", [128, NB, D])
        x_tok = sb("x_tok", [128, NB, DI])
        z_tok = sb("z_tok", [128, NB, DI])
        g_all = sb("g_all", [128, NB, L])
        dt_sp = sb("dt_sp", [128, NB, NH])
        a_dt = sb("a_dt", [128, NB, NH])
        s_in = sb("s_in", [128, NB])
        x1 = sb("x1", [128, NB, D])
        x2T = sb("x2T", [128, NB * L])
        x2b = x_all
        logit = sb("logit", [128, NB, E])

        u = sb("u", [128, GB, D])
        uc = sb("uc", [128, GB, D])
        junk = sb("junk", [128, GB, D])
        stats = sb("stats", [128, GB, 6])
        ms_x = sb("ms_x", [128, GB])
        mv_u = sb("mv_u", [128, GB, 2])
        amax_u = sb("amax_u", [128, GB])
        s_x = sb("s_x", [128, GB])
        f_x = sb("f_x", [128, GB])
        pool_t = [sb(f"pool_t{i}", [128, GB]) for i in range(3)]
        qm = sb("qm", [128, GB, D])
        q_bf = sb("q_bf", [128, GB, D], BF16)
        diag = sb("diag", [128, GB, 128])
        qT = sb("qT", [128, T], BF16)
        s_row = sb("s_row", [128, T])
        xs = sb("xs", [128, NC, GB, TAPS - 1 + L])
        acc = sb("acc", [128, NC, GB, L])
        xbc = sb("xbc", [128, NC, GB, L])
        dt_raw = sb("dt_raw", [128, GB, NH])
        v_dt = sb("v_dt", [128, GB * NH])
        na_dt = sb("na_dt", [128, GB * NH])
        e_dt = sb("e_dt", [128, GB * NH])
        l_dt = sb("l_dt", [128, GB * NH])

        seg = sb("seg", [128, GB, NH, L])
        ex = sb("ex", [128, GB, NH, L])
        u_dt = sb("u_dt", [128, GB, DI])
        y = sb("y", [128, GB, DI])
        junk_y = sb("junk_y", [128, GB, DI])
        y_w = sb("y_w", [128, GB, DI])
        y_c = sb("y_c", [128, GB, DI])
        y_qm = sb("y_qm", [128, GB, DI])
        y_q = sb("y_q", [128, GB, DI], BF16)
        y_qT = sb("y_qT", [128, GB, 2, L], BF16)
        ms_y = sb("ms_y", [128, GB])
        mv_y = sb("mv_y", [128, GB, 2])
        amax_y = sb("amax_y", [128, GB])
        s_y = sb("s_y", [128, GB])
        f_y = sb("f_y", [128, GB])
        stats_y = sb("stats_y", [128, GB, 6])
        x2x = sb("x2x", [128, GB, D])
        res1 = sb("res1", [128, GB, D])
        stats1 = sb("stats1", [128, GB, 6])
        mv1 = sb("mv1", [128, GB, 2])
        rstd1 = sb("rstd1", [128, GB])
        x1_s = sb("x1_s", [128, GB, D])
        x1T = sb("x1T", [128, GB, L])

        BIAS = 96
        KR = BIAS + 1
        ctx_s = sb("ctx_s", [128, TS])
        p1 = sb("p1", [128, TS])
        p2 = sb("p2", [128, TS])
        vvs = sb("vvs", [128, GB, 384])
        vvc = sb("vvc", [128, GB, 256])
        nmx1 = sb("nmx1", [128, GB])
        den1 = sb("den1", [128, GB])
        rden1 = sb("rden1", [128, GB])
        mx2 = sb("mx2", [LS, GB])
        shift2 = sb("shift2", [LS, GB])
        nmx2 = sb("nmx2", [LS, GB])
        den2 = sb("den2", [LS, GB])
        rden2 = sb("rden2", [LS, GB])
        e1 = sb("e1", [128, GB, LS])
        e1n = sb("e1n", [128, GB, KR])
        e1T = sb("e1T", [KR, GB, L])
        e2 = sb("e2", [LS, GB, L])
        ipn = sb("ipn", [LS, GB, L])
        w2i = sb("w2i", [128, GB, L])
        eg = sb("eg", [128, GB, D])
        gt = sb("gt", [128, GB, D])
        s2c = sb("s2c", [128, GB, D])
        s2c_x1 = sb("s2c_x1", [128, GB, D])
        dif = sb("dif", [128, GB, D])
        res2 = sb("res2", [128, GB, D])
        stats2 = sb("stats2", [128, GB, 6])
        mv2 = sb("mv2", [128, GB, 2])
        rstd2 = sb("rstd2", [128, GB])
        x2_s = sb("x2_s", [128, GB, D])
        x2T_s = sb("x2T_s", [128, GB, L])

        xf = x_tok[:, :, :].rearrange("p b c -> p (b c)")
        zf = z_tok[:, :, :].rearrange("p b c -> p (b c)")
        hid = xf[:, 0:NE * FT].rearrange("p (t n) -> p t n", t=NE)
        hid_s = xf[:, NE * FT:(NE + 1) * FT]
        res3 = xf[:, 5 * FT:6 * FT].rearrange("p (b d) -> p b d", b=FB)
        y_out = xf[:, 6 * FT:7 * FT].rearrange("p (b d) -> p b d", b=FB)
        (score, top, first, rest, pick, second) = (
            zf[:, i * NB * E:(i + 1) * NB * E].rearrange("p (b e) -> p b e", e=E) for i in range(6))
        gT = sb("gT", [3 * E, FT], BF16)
        sel_bf = sb("sel_bf", [3 * E, (NE + 1) * 128], BF16)
        max1 = sb("max1", [128, NB])
        max2 = sb("max2", [128, NB])
        prio1 = sb("prio1", [128, NB])
        gate3 = sb("gate3", [128, NB, 3 * E], BF16)
        stats3 = sb("stats3", [128, FB, 6])
        mv3 = sb("mv3", [128, FB, 2])
        rstd3 = sb("rstd3", [128, FB])

        bank = [ctx.enter_context(nc.psum_tensor(f"bank{i}", [128, 512], FP32)) for i in range(8)]

        x0_in = sem("x0_in")
        x_in = sem("x_in")
        sp_settled = sem("sp_settled")
        w_in = sem("w_in")
        w2_in = sem("w2_in")
        r_in = sem("r_in")
        c_in = sem("c_in")
        act_steps = sem("act_steps")
        dve_steps = sem("dve_steps")
        pool_steps = sem("pool_steps")
        pool_settled = sem("pool_settled")
        dve_settled = sem("dve_settled")
        consts_ready = sem("consts_ready")
        ident_ready = sem("ident_ready")
        magic_ready = sem("magic_ready")
        wsum_ready = sem("wsum_ready")
        wsum_psum = sem("wsum_psum")
        win_ready = sem("win_ready")
        aexp_ready = sem("aexp_ready")
        bcol_ready = sem("bcol_ready")
        a_psum = sem("a_psum")
        attw_ready = sem("attw_ready")
        sel_ready = sem("sel_ready")
        score_ready = sem("score_ready")
        gate_ready = sem("gate_ready")
        out_done = counter("out_done")
        ctx_in = sem("ctx_in")
        (u_ready, ms_ready, amax_ready, fx_ready, qm_ready, q_ready, diag_ready, q_psum, qt_ready, zx_psum,
         xs_ready, tap0_ready, conv_ready, silu_ready, g_psum, xt_psum, g_ready, xtok_ready, zd_psum, zd_ready,
         v_ready, l_ready, dt_ready) = (counter(n) for n in (
            "u_ready ms_ready amax_ready fx_ready qm_ready q_ready diag_ready q_psum qt_ready zx_psum "
            "xs_ready tap0_ready conv_ready silu_ready g_psum xt_psum g_ready xtok_ready zd_psum zd_ready "
            "v_ready l_ready dt_ready").split())
        (seg_ready, udt_ready, ss_psum, ex_ready, m_ready, y_psum, y_ready, msy_ready, yw_ready, amaxy_ready,
         fy_ready, yqm_ready, yq_ready, yqt_psum, yqt_ready, proj_psum, x2x_ready, var1_ready, rstd1_ready,
         x1s_ready, x1_ready, x1t_psum, x1t_ready) = (counter(n) for n in (
            "seg_ready udt_ready ss_psum ex_ready m_ready y_psum y_ready msy_ready yw_ready amaxy_ready "
            "fy_ready yqm_ready yq_ready yqt_psum yqt_ready proj_psum x2x_ready var1_ready rstd1_ready "
            "x1s_ready x1_ready x1t_psum x1t_ready").split())
        (p_psum, vvs_psum, p_ready, vvs_ready, vvc_psum, vvc_ready, s1_psum, s2_psum, nmx1_ready, nmx2_ready,
         e1_ready, e2_ready, e1n_ready, ipn_ready, e1t_psum, w2i_psum, e1t_ready, w2i_ready, o_psum, s2c_ready,
         eg_ready, rs_ready, dif_part, res2_ready, var2_ready, rstd2_ready, x2_ready, x2b_ready, x2t_psum,
         x2t_ready, logit_psum, logit_ready) = (counter(n) for n in (
            "p_psum vvs_psum p_ready vvs_ready vvc_psum vvc_ready s1_psum s2_psum nmx1_ready nmx2_ready "
            "e1_ready e2_ready e1n_ready ipn_ready e1t_psum w2i_psum e1t_ready w2i_ready o_psum s2c_ready "
            "eg_ready rs_ready dif_part res2_ready var2_ready rstd2_ready x2_ready x2b_ready x2t_psum "
            "x2t_ready logit_psum logit_ready").split())
        (gt_psum, gt_ready, h_psum, gb_psum, hid_ready, hs_ready, hg_ready, moe_psum, var3_ready, rstd3_ready,
         yout_ready) = (counter(n) for n in (
            "gt_psum gt_ready h_psum gb_psum hid_ready hs_ready hg_ready moe_psum var3_ready rstd3_ready "
            "yout_ready").split())

        W_FIRST = COL["wq_c"][0]
        N_CONSTS = 10

        def batch(g, j):
            return bass.ds(g * GB + j, 1)

        def group(g):
            return bass.ds(g * GB, GB)

        ATT, SCAN_B, SCAN_A, PROJ = 0, 1, 2, 3

        def main_loop(eng, steps, blocks):
            def step(k):
                for fn, lead in blocks:
                    if not isinstance(k, int) or 0 <= k + lead < NG:
                        fn(k + lead)

            for k in range(-PROJ, 0):
                step(k)
            before = steps.total()
            step(0)
            start = steps.total()
            per = start - before
            with eng.Fori(1, NG - PROJ) as k:
                steps.enter(start, k - 1, per)
                step(k)
                steps.leave(start, NG - PROJ - 1, per)
            for k in range(NG - PROJ, NG):
                step(k)

        block = ctx.enter_context(nc.Block())

        @block.sync
        def _(sp):
            sp.dma_start(x_all[:, 0:4, :], x[0:4].rearrange("b l d -> l b d")).then_inc(x0_in, 16)
            sp.dma_start(W[:, 0:W_FIRST], wpack[:, 0:W_FIRST]).then_inc(w_in, 16)
            for i in range(1, 4):
                sp.dma_start(x_all[:, 4 * i:4 * i + 4, :],
                             x[4 * i:4 * i + 4].rearrange("b l d -> l b d")).then_inc(x_in, 16)
            sp.dma_start(W[:, W_FIRST:NCOL], wpack[:, W_FIRST:NCOL]).then_inc(w2_in, 16)
            for s in counters:
                sp.sem_inc(s, 1)

            def load_context(g):
                sp.wait_ge(vvs_psum, did(g))
                sp.wait_ge(s1_psum, did(g))
                sp.wait_ge(s2_psum, did(g))
                sp.sem_inc(sp_settled, 1)
                sp.dma_start(ctx_s[:, :], ctxT[:, bass.ds(g * TS, TS)]).then_inc(ctx_in, 16)

            load_context(0)
            with sp.Fori(1, NG) as g:
                load_context(g)

            with sp.Fori(0, NF) as g:
                sp.wait_ge(yout_ready, did(g + 1))
                sp.sem_inc(sp_settled, 1)
                sp.dma_start(out[bass.ds(g * FB, FB)].rearrange("b l d -> l b d"), y_out).then_inc(out_done, 16)
            sp.wait_ge(out_done, did(16 * NF))

        @block.gpsimd
        def _(pool):
            steps = Steps(pool, pool_steps)
            for what, value in ((ones[:, :], 1.0), (neg_half[:, :], -0.5), (neg_one[:, :], -1.0), (neg_half4[:, :], -0.5),
                                (eps5[:, :], 1e-5), (xs[:, :, :, 0:TAPS - 1], 0.0), (vvs[:, :, :], 0.0),
                                (e1n[:, :, :], 0.0), (bcol[:, :, :], 0.0)):
                pool.memset(what, value).then_inc(consts_ready, 1)
            pool.wait_ge(consts_ready, N_CONSTS - 1)
            pool.memset(e1n[:, :, BIAS:KR], 1.0).then_inc(consts_ready, 1)
            pool.wait_ge(consts_ready, N_CONSTS)

            def settle():
                pool.sem_inc(pool_settled, 1)

            def quant_scales(ms, mv, amax, s_to, f_to, ready):
                a, b, t = (p[:, :] for p in pool_t)
                settle()
                steps.link(pool.tensor_scalar(a, ms[:, :], 1e-5, 1e-11, ALU.mult, ALU.add))
                steps.link(pool.tensor_tensor(b, a, mv[:, :, 1], ALU.add))
                steps.link(pool.tensor_tensor(t, b, neg_half[:, :], ALU.pow))
                steps.link(pool.tensor_tensor(a, t, amax[:, :], ALU.mult))
                settle()
                steps.link(pool.tensor_scalar(s_to[:, :], a, 1e-5, 1.0 / 127.0, ALU.max, ALU.mult))
                steps.link(pool.tensor_tensor(b, s_to[:, :], neg_one[:, :], ALU.pow))
                pool.tensor_tensor(f_to[:, :], t, b, ALU.mult).then_inc(ready, 1)

            def rstd(var, dst, half, ready):
                steps.link(pool.tensor_tensor(dst[:, :], var[:, :, 1], eps5[:, 0:half.shape[1]], ALU.add))
                pool.tensor_tensor(dst[:, :], dst[:, :], half, ALU.pow).then_inc(ready, 1)

            def scaled_input(g):
                pool.wait_ge(amax_ready, did(g))
                settle()
                pool.tensor_tensor(u[:, :, :], x_all[:, group(g), :],
                                   r("norm_w").unsqueeze(1).to_broadcast([128, GB, D]), ALU.mult).then_inc(u_ready, 1)

            def input_scales(g):
                pool.wait_ge(ms_ready, did(GB * (g + 1)))
                pool.wait_ge(amax_ready, did(g + 1))
                pool.wait_ge(zd_ready, did(GB * g))
                pool.wait_ge(diag_ready, did(g))
                quant_scales(ms_x, mv_u, amax_u, s_x, f_x, fx_ready)

            def scan_inputs(g):
                pool.wait_ge(dt_ready, did(g + 1))
                pool.wait_ge(ss_psum, did(GB * g))
                pool.wait_ge(y_psum, did(g))
                pool.wait_ge(xtok_ready, did(g + 1))
                settle()
                for j in range(GB):
                    pool.tensor_tensor(seg[:, j], upto.unsqueeze(1).to_broadcast([128, NH, L]),
                                       a_dt[:, batch(g, j), :].rearrange("p a h -> p (a h)").unsqueeze(2)
                                       .to_broadcast([128, NH, L]), ALU.mult).then_inc(seg_ready, 1)
                    pool.tensor_tensor(u_dt[:, j].rearrange("p (h c) -> p h c", h=NH),
                                       x_tok[:, batch(g, j), :].rearrange("p a (h c) -> p (a h) c", h=NH),
                                       dt_sp[:, batch(g, j), :].rearrange("p a h -> p (a h)").unsqueeze(2)
                                       .to_broadcast([128, NH, HD]), ALU.mult).then_inc(udt_ready, 1)

            def scaled_y(g):
                pool.wait_ge(y_ready, did(g + 1))
                pool.wait_ge(amaxy_ready, did(g))
                pool.tensor_tensor(y_w[:, :, :], y[:, :, :], r("out_norm_w").unsqueeze(1).to_broadcast([128, GB, DI]),
                                   ALU.mult).then_inc(yw_ready, 1)

            def y_scales(g):
                pool.wait_ge(msy_ready, did(GB * (g + 1)))
                pool.wait_ge(amaxy_ready, did(g + 1))
                pool.wait_ge(var1_ready, did(g))
                quant_scales(ms_y, mv_y, amax_y, s_y, f_y, fy_ready)

            def first_rstd(g):
                pool.wait_ge(var1_ready, did(g + 1))
                rstd(mv1, rstd1, neg_half[:, :], rstd1_ready)

            def attention_residual(g):
                pool.wait_ge(s2c_ready, did(GB * (g + 1)))
                pool.wait_ge(x1_ready, did(g + 1))
                pool.wait_ge(res2_ready, did(g))
                settle()
                pool.tensor_tensor(s2c_x1[:, :, :], s2c[:, :, :], x1[:, group(g), :], ALU.add).then_inc(rs_ready, 1)

            def second_rstd(g):
                pool.wait_ge(var2_ready, did(g + 1))
                rstd(mv2, rstd2, neg_half[:, :], rstd2_ready)

            def expert_residual(g):
                pool.wait_ge(x2_ready, did(g + 1))
                settle()
                pool.tensor_tensor(x2b[:, group(g), :], x2_s[:, :, :],
                                   r("bs2").unsqueeze(1).to_broadcast([128, GB, D]), ALU.add).then_inc(x2b_ready, 1)

            pool.wait_ge(r_in, 16)
            pool.wait_ge(c_in, 16)
            pool.wait_ge(x0_in, 16)
            pool.wait_ge(x_in, 16 * 3)
            main_loop(pool, steps, [
                (scaled_input, 3), (first_rstd, 0), (scan_inputs, 1), (scaled_y, 1), (attention_residual, 0),
                (y_scales, 1), (input_scales, 3), (second_rstd, 0), (expert_residual, 0)])

            start = steps.total()
            with pool.Fori(0, NF) as g:
                steps.enter(start, g, 1)
                pool.wait_ge(var3_ready, did(g + 1))
                rstd(mv3, rstd3, neg_half4[:, :], rstd3_ready)
                steps.leave(start, NF, 1)

        @block.scalar
        def _(act):
            steps = Steps(act, act_steps)
            act.dma_start(R[:, :], rpack.rearrange("(a n) -> a n", a=1).to_broadcast([128, NROW])).then_inc(r_in, 16)
            act.dma_start(C[:, :], cpack).then_inc(c_in, 16)
            act.wait_ge(c_in, 16)
            act.activation(ident_bf[:, :], ident, ACT.Copy).then_inc(ident_ready, 1)
            act.activation(sel_bf[:, :], c_("sel", 3 * E), ACT.Copy).then_inc(sel_ready, 1)
            act.wait_ge(r_in, 16)
            act.activation(a_exp[:, :], r("A_log"), ACT.Exp).then_inc(aexp_ready, 1)

            def mean_square(g):
                act.wait_ge(fx_ready, did(g))
                act.wait_ge(ms_ready, did(GB * g))
                for j in range(GB):
                    act.activation(junk[:, j, :], x_all[:, batch(g, j), :], ACT.Square, scale=float(D ** -0.5),
                                   accum_out=ms_x[:, j:j + 1]).then_inc(ms_ready, 1)

            def quantise(g):
                act.wait_ge(fx_ready, did(g + 1))
                act.wait_ge(q_ready, did(g))
                for j in range(GB):
                    act.activation(qm[:, j, :], uc[:, j, :], ACT.Identity, bias=magic_bias[:, 0:1],
                                   scale=f_x[:, j:j + 1]).then_inc(qm_ready, 1)

            def evacuate_q(g):
                act.wait_ge(q_psum, did(g + 1))
                act.wait_ge(zd_psum, did(GB * g))
                act.wait_ge(xs_ready, did(2 * g))
                act.activation(s_row[:, :], bank[2][:, 0:T], ACT.Copy)
                act.activation(qT[:, :], bank[2][:, T:T + T // 2].bitcast(BF16), ACT.Copy).then_inc(qt_ready, 1)

            def first_tap(g):
                act.wait_ge(silu_ready, did(2 * g))
                for c in range(NC):
                    act.wait_ge(xs_ready, did(2 * g + c // 2 + 1))
                    act.activation(acc[:, c, :, :], xs[:, c, :, TAPS - 1:], ACT.Identity,
                                   bias=w("conv_b")[:, c:c + 1],
                                   scale=w("conv_w")[:, c * TAPS + TAPS - 1:c * TAPS + TAPS]).then_inc(tap0_ready, 1)

            def gates(g):
                act.wait_ge(v_ready, did(g))
                for j in range(GB):
                    act.wait_ge(zd_psum, did(GB * g + j + 1))
                    act.activation(z_tok[:, batch(g, j), :], bank[j][:, 0:DI], ACT.Silu, scale=s_x[:, j:j + 1])
                    act.activation(dt_raw[:, j, :], bank[j][:, DI:DI + NH], ACT.Identity,
                                   scale=s_x[:, j:j + 1]).then_inc(zd_ready, 1)

            def silu_xbc(g):
                act.wait_ge(g_psum, did(g))
                act.wait_ge(xt_psum, did(g))
                for i in (1, 0):
                    act.wait_ge(conv_ready, did(NC * g + NC // 2 * (2 - i)))
                    act.activation(xbc[:, 2 * i:2 * i + 2, :, :], acc[:, 2 * i:2 * i + 2, :, :],
                                   ACT.Silu).then_inc(silu_ready, 1)

            def evacuate_x(g):
                act.wait_ge(xt_psum, did(g + 1))
                act.activation(x_tok[:, group(g), :], bank[1][:, :].rearrange("p (b c) -> p b c", b=GB),
                               ACT.Copy).then_inc(xtok_ready, 1)

            def softplus_log(g):
                act.wait_ge(v_ready, did(g + 1))
                act.wait_ge(dt_ready, did(g))
                steps.link(act.activation(e_dt[:, :], na_dt[:, :], ACT.Exp))
                act.activation(l_dt[:, :], e_dt[:, :], ACT.Ln, bias=ones[:, 0:1]).then_inc(l_ready, 1)

            def silus(g):
                act.preload_act_table(ACT.Silu)
                gates(g)
                silu_xbc(g)
                act.preload_act_table_set("natural_log_exp_and_others")

            def decays(g):
                act.wait_ge(y_psum, did(g))
                for j in range(GB):
                    act.wait_ge(ss_psum, did(GB * g + j + 1))
                    act.activation(ex[:, j].rearrange("p h l -> p (h l)"), bank[3 + j][:, :], ACT.Exp).then_inc(ex_ready, 1)

            def y_square(g):
                act.wait_ge(fy_ready, did(g))
                act.wait_ge(msy_ready, did(GB * g))
                act.wait_ge(y_ready, did(g + 1))
                for j in range(GB):
                    act.activation(junk_y[:, j, :], y[:, j, :], ACT.Square, scale=float(DI ** -0.5),
                                   accum_out=ms_y[:, j:j + 1]).then_inc(msy_ready, 1)

            def double_x(g):
                act.wait_ge(var1_ready, did(g))
                act.activation(x2x[:, :, :], x_all[:, group(g), :], ACT.Copy, scale=2.0).then_inc(x2x_ready, 1)

            def y_quantise(g):
                act.wait_ge(fy_ready, did(g + 1))
                act.wait_ge(yq_ready, did(g))
                for j in range(GB):
                    act.activation(y_qm[:, j, :], y_c[:, j, :], ACT.Identity, bias=magic_bias[:, 0:1],
                                   scale=f_y[:, j:j + 1]).then_inc(yqm_ready, 1)

            def y_evacuate(g):
                act.wait_ge(yqt_psum, did(g + 1))
                act.wait_ge(proj_psum, did(g))
                act.activation(y_qT[:, :, :, :].rearrange("p b c l -> p (b c l)"),
                               bank[4][:, 0:GB * DI // 2].bitcast(BF16), ACT.Copy).then_inc(yqt_ready, 1)

            def x1_evacuate(g):
                act.wait_ge(x1t_psum, did(g + 1))
                act.wait_ge(vvc_psum, did(g))
                act.wait_ge(s2_psum, did(g))
                act.activation(x1T[:, :, :].rearrange("p b l -> p (b l)"), bank[4][:, 0:T], ACT.Copy).then_inc(x1t_ready, 1)

            def context_keys(g):
                act.wait_ge(p_psum, did(g + 1))
                act.wait_ge(s2_psum, did(g))
                act.activation(p1[:, :], bank[5][:, 0:TS], ACT.Identity, bias=vec[:, 0:1], scale=INV_SQRT_D)
                act.activation(p2[:, :], bank[5][:, TS:2 * TS], ACT.Identity, bias=vec[:, 1:2],
                               scale=INV_SQRT_D).then_inc(p_ready, 1)

            def context_values(g):
                act.wait_ge(vvs_psum, did(g + 1))
                act.wait_ge(o_psum, did(GB * g))
                act.activation(vvs[0:LS, :, 0:256], bank[6][0:LS, :].rearrange("p (b c) -> p b c", b=GB),
                               ACT.Copy).then_inc(vvs_ready, 1)

            def first_exps(g):
                act.wait_ge(nmx1_ready, did(g + 1))
                act.wait_ge(e1n_ready, did(g))
                for j in range(GB):
                    act.activation(e1[:, j, :], bank[7][:, j * LS:(j + 1) * LS], ACT.Exp, bias=nmx1[:, j:j + 1],
                                   accum_out=den1[:, j:j + 1]).then_inc(e1_ready, 1)

            def second_exps(g):
                act.wait_ge(nmx2_ready, did(g + 1))
                act.wait_ge(w2i_psum, did(g))
                act.wait_ge(ipn_ready, did(g))
                for j in range(GB):
                    act.activation(e2[:, j, :], bank[5][0:LS, j * L:(j + 1) * L], ACT.Exp, bias=nmx2[:, j:j + 1],
                                   accum_out=den2[:, j:j + 1]).then_inc(e2_ready, 1)

            def token_values(g):
                act.wait_ge(vvc_psum, did(g + 1))
                act.wait_ge(o_psum, did(GB * g))
                act.activation(vvc[:, :, :].rearrange("p b c -> p (b c)"), bank[6][:, :], ACT.Copy).then_inc(vvc_ready, 1)

            def evacuate_e1(g):
                act.wait_ge(e1t_psum, did(g + 1))
                act.wait_ge(o_psum, did(GB * g))
                act.activation(e1T[:, :, :].rearrange("p b l -> p (b l)"), bank[7][0:KR, 0:T], ACT.Copy).then_inc(e1t_ready, 1)

            def evacuate_w2(g):
                act.wait_ge(w2i_psum, did(g + 1))
                act.wait_ge(o_psum, did(GB * g))
                act.activation(w2i[:, :, :].rearrange("p b l -> p (b l)"), bank[5][:, 0:T], ACT.Copy).then_inc(w2i_ready, 1)

            def mixed(g):
                act.wait_ge(dif_part, did(GB * g))
                act.wait_ge(rs_ready, did(g))
                act.wait_ge(res2_ready, did(g))
                for j in range(GB):
                    act.wait_ge(o_psum, did(GB * g + j + 1))
                    act.activation(s2c[:, j, :], bank[6 + j][:, 256:384], ACT.Copy).then_inc(s2c_ready, 1)
                    act.activation(eg[:, j, :], bank[6 + j][:, 128:256], ACT.Exp, scale=-1.0).then_inc(eg_ready, 1)

            def x2_evacuate(g):
                act.wait_ge(x2t_psum, did(g + 1))
                act.wait_ge(logit_psum, did(g))
                act.activation(x2T_s[:, :, :].rearrange("p b l -> p (b l)"), bank[5][:, 0:T], ACT.Copy).then_inc(x2t_ready, 1)
                act.activation(x2T[:, bass.ds(g * T, T)], bank[5][:, 0:T], ACT.Copy).then_inc(x2t_ready, 1)

            act.preload_act_table_set("natural_log_exp_and_others")
            act.wait_ge(magic_ready, 1)
            act.wait_ge(x0_in, 16)
            act.wait_ge(x_in, 16 * 3)
            act.wait_ge(w_in, 16)
            act.wait_ge(consts_ready, N_CONSTS)
            act.wait_ge(attw_ready, 1)
            main_loop(act, steps, [
                (evacuate_x, 1), (quantise, 2), (context_keys, 0), (double_x, 1), (x1_evacuate, 0),
                (mean_square, 3), (evacuate_q, 2), (context_values, 0), (first_exps, 0), (decays, 1),
                (second_exps, 0), (first_tap, 2), (evacuate_e1, 0), (token_values, 0), (evacuate_w2, 0),
                (y_square, 1), (mixed, 0), (silus, 2), (y_quantise, 1), (y_evacuate, 1), (softplus_log, 2),
                (x2_evacuate, 0)])

            act.preload_act_table(ACT.Gelu)
            act.wait_ge(logit_ready, did(NG))
            act.activation(score, logit[:, :, :], ACT.Tanh, scale=0.5).then_inc(score_ready, 1)

            def expert_hidden(g):
                act.wait_ge(gt_psum, did(g + 1))
                act.wait_ge(gb_psum, did((NE + 1) * g))
                act.activation(gT[:, :], bank[5][0:3 * E, :], ACT.Copy).then_inc(gt_ready, 1)
                act.wait_ge(moe_psum, did(g))
                for t in range(NE):
                    act.wait_ge(h_psum, did((NE + 1) * g + t + 1))
                    act.activation(hid[:, t, :], bank[t % 2][:, :], ACT.Gelu, bias=w("b1")[:, t:t + 1]).then_inc(hid_ready, 1)
                act.wait_ge(h_psum, did((NE + 1) * (g + 1)))
                act.activation(hid_s[0:HID, :], bank[NE % 2][0:HID, :], ACT.Gelu, bias=w("bs1", HID)).then_inc(hs_ready, 1)
                act.wait_ge(gb_psum, did((NE + 1) * (g + 1)))
                act.activation(hid_s[HID:96, :], bank[2 + NE % 2][HID:96, :], ACT.Copy).then_inc(hs_ready, 1)

            with act.Fori(0, NF) as g:
                expert_hidden(g)

        @block.vector
        def _(dve):
            steps = Steps(dve, dve_steps)

            def settle():
                dve.sem_inc(dve_settled, 1)

            dve.memset(magic_bias[:, :], MAGIC).then_inc(magic_ready, 1)
            dve.wait_ge(w_in, 16)
            win, wout = w("win"), w("wout")
            dve.tensor_reduce(wsum[:, 0:1], win, AXIS.X, ALU.add, apply_absolute_value=True)
            dve.tensor_reduce(wsum[:, 1:2], wout, AXIS.X, ALU.add, apply_absolute_value=True).then_inc(wsum_ready, 1)
            dve.wait_ge(wsum_psum, 1)
            steps.link(dve.tensor_copy(wscale[:, 0:2], bank[7][:, 0:2]))
            steps.link(dve.tensor_scalar(wscale[:, 0:1], wscale[:, 0:1], 1.0 / (772 * D), 1e-5, ALU.mult, ALU.max))
            steps.link(dve.tensor_scalar(wscale[:, 1:2], wscale[:, 1:2], 1.0 / (DI * D), 1e-5, ALU.mult, ALU.max))
            steps.link(dve.tensor_scalar(wscale[:, 2:4], wscale[:, 0:2], -0.5, None, ALU.mult))
            steps.link(dve.tensor_scalar(wscale[:, 0:2], wscale[:, 0:2], 0.5, None, ALU.mult))
            steps.link(dve.tensor_scalar(low[:, :], win, wscale[:, 2:3], None, ALU.is_lt))
            steps.link(dve.scalar_tensor_tensor(win_q[:, :], win, wscale[:, 0:1], low[:, :], ALU.is_gt, ALU.subtract))
            steps.link(dve.tensor_scalar(low[:, 0:DI], wout, wscale[:, 3:4], None, ALU.is_lt))
            dve.scalar_tensor_tensor(wout_q[:, :, :].rearrange("p a b -> p (a b)"), wout, wscale[:, 1:2],
                                     low[:, 0:DI], ALU.is_gt, ALU.subtract).then_inc(win_ready, 1)

            dve.wait_ge(r_in, 16)
            dve.wait_ge(c_in, 16)
            for h in range(NH):
                steps.link(dve.tensor_scalar(ident_d[:, h, :], ident, r("Dp")[:, h:h + 1], None, ALU.mult))
            dve.wait_ge(w2_in, 16)
            dve.wait_ge(consts_ready, N_CONSTS)
            dve.tensor_copy(bcol[:, 0, BIAS:KR], w("bv_s"))
            dve.tensor_copy(bcol[:, 1, BIAS:KR], w("bv_c"))
            dve.tensor_scalar(bq_all[:, 0, :], ones[:, :], w("bq_c"), None, ALU.mult)
            dve.tensor_scalar(bq_all[:, 1, :], ones[:, :], w("bq_s"), None, ALU.mult).then_inc(bcol_ready, 1)
            dve.wait_ge(a_psum, 1)
            dve.tensor_copy(a1T[:, :], bank[0][:, 0:128])
            dve.tensor_copy(a2T[:, :], bank[0][:, 128:256])
            dve.tensor_copy(wvs[:, 128:256], bank[0][:, 256:384])
            dve.tensor_copy(wvc[:, 0:128], bank[0][:, 384:512])
            dve.tensor_copy(wvs[:, 0:128], w("wv_sT"))
            dve.tensor_copy(wvc[:, 128:256], w("wv_cT"))
            steps.link(dve.tensor_scalar(vec[:, :], bank[2][:, 0:6], INV_SQRT_D, None, ALU.mult))
            dve.tensor_copy(cvec2[:, :], bank[2][:, 3:4])
            dve.tensor_scalar(cv1[:, :], ones[:, :], vec[:, 2:3], None, ALU.mult)
            for j in range(GB):
                steps.link(dve.tensor_copy(vvs[BIAS:KR, j, :], bank[1][BIAS:KR, 0:384]))
                ins = dve.tensor_tensor(vvs[BIAS:KR, j, 128:256], bank[1][BIAS:KR, 128:256], R[BIAS:KR, ROW["bg"][0]:ROW["bg"][1]],
                                        ALU.add)
            ins.then_inc(attw_ready, 1)

            def moments(src, stats_to, mv_to, n):
                for j in range(n):
                    at = steps.mark(dve.bn_stats(stats_to[:, j, :], src[:, j, :]))
                steps.wait(at)
                settle()
                for j in range(n):
                    ins = dve.bn_aggr(mv_to[:, j, :], stats_to[:, j, :])
                return ins

            def centred(dst, src, mv_of):
                for j in range(GB):
                    at = steps.mark(dve.tensor_scalar(dst[:, j, :], src[:, j, :], mv_of[:, j, 0:1], None, ALU.subtract))
                steps.wait(at)

            def input_stats(g):
                dve.wait_ge(u_ready, did(g + 1))
                dve.wait_ge(fx_ready, did(g))
                dve.wait_ge(qm_ready, did(GB * g))
                steps.link(moments(u, stats, mv_u, GB))
                centred(uc, u, mv_u)
                dve.tensor_reduce(amax_u[:, :], uc[:, :, :], AXIS.X, ALU.max,
                                  apply_absolute_value=True).then_inc(amax_ready, 1)

            def step_diagonal(g):
                dve.wait_ge(fx_ready, did(g + 1))
                dve.wait_ge(q_psum, did(g))
                for j in range(GB):
                    ins = dve.tensor_scalar(diag[:, j, :], ident, s_x[:, j:j + 1], None, ALU.mult)
                ins.then_inc(diag_ready, 1)

            def round_q(g):
                dve.wait_ge(q_psum, did(g))
                dve.wait_ge(qm_ready, did(GB * (g + 1)))
                dve.tensor_scalar(q_bf[:, :, :], qm[:, :, :], MAGIC, None, ALU.subtract).then_inc(q_ready, 1)

            def conv(g):
                dve.wait_ge(qt_ready, did(g + 1))
                dve.wait_ge(tap0_ready, did(NC * g))
                dve.wait_ge(conv_ready, did(NC * g))
                for i in range(2):
                    dve.wait_ge(zx_psum, did(2 * g + i + 1))
                    dve.tensor_tensor(xs[:, 2 * i:2 * i + 2, :, TAPS - 1:],
                                      bank[i][:, :].rearrange("p (c b l) -> p c b l", c=2, b=GB),
                                      s_row[:, :].rearrange("p (b l) -> p b l", b=GB).unsqueeze(1)
                                      .to_broadcast([128, 2, GB, L]), ALU.mult).then_inc(xs_ready, 1)

            def taps(g, tiles):
                done = [0] * NC
                for k in range(TAPS - 2, -1, -1):
                    for c in tiles:
                        if k == TAPS - 2:
                            dve.wait_ge(tap0_ready, did(NC * g + c + 1))
                        else:
                            steps.wait(done[c])
                        ins = dve.scalar_tensor_tensor(acc[:, c, :, :], xs[:, c, :, k:k + L],
                                                       w("conv_w")[:, c * TAPS + k:c * TAPS + k + 1],
                                                       acc[:, c, :, :], ALU.mult, ALU.add)
                        if k:
                            done[c] = steps.mark(ins)
                        else:
                            ins.then_inc(conv_ready, 1)

            def taps_bc(g):
                taps(g, (2, 3))

            def taps_x(g):
                taps(g, (0, 1))

            def mask_g(g):
                dve.wait_ge(g_psum, did(g + 1))
                dve.tensor_tensor(g_all[:, group(g), :], bank[0][:, 0:T].rearrange("p (b l) -> p b l", b=GB),
                                  upto.unsqueeze(1).to_broadcast([128, GB, L]), ALU.mult).then_inc(g_ready, 1)

            def softplus_start(g):
                dve.wait_ge(dt_ready, did(g))
                dve.wait_ge(zd_ready, did(GB * (g + 1)))
                dve.wait_ge(l_ready, did(g))
                steps.link(dve.tensor_tensor(v_dt[:, :].rearrange("p (b h) -> p b h", h=NH), dt_raw[:, :, :],
                                             r("dt_bias").unsqueeze(1).to_broadcast([128, GB, NH]), ALU.add))
                dve.scalar_tensor_tensor(na_dt[:, :], v_dt[:, :], -1.0, v_dt[:, :], ALU.mult, ALU.min).then_inc(v_ready, 1)

            def softplus_end(g):
                dve.wait_ge(l_ready, did(g + 1))
                steps.link(dve.scalar_tensor_tensor(dt_sp[:, group(g), :].rearrange("p b h -> p (b h)"), v_dt[:, :], 0.0,
                                                    l_dt[:, :], ALU.max, ALU.add))
                dve.scalar_tensor_tensor(a_dt[:, group(g), :], dt_sp[:, group(g), :], -1.0,
                                         a_exp[:, :].unsqueeze(1).to_broadcast([128, GB, NH]),
                                         ALU.mult, ALU.mult).then_inc(dt_ready, 1)

            def decay_gram(g):
                for j in range(GB):
                    dve.wait_ge(ex_ready, did(GB * g + j + 1))
                    dve.tensor_tensor(ex[:, j], ex[:, j], g_all[:, batch(g, j), :].to_broadcast([128, NH, L]),
                                      ALU.mult).then_inc(m_ready, 1)

            def gate_y(g):
                dve.wait_ge(y_psum, did(g + 1))
                dve.wait_ge(yw_ready, did(g))
                dve.wait_ge(msy_ready, did(GB * g))
                dve.tensor_tensor(y[:, :, :], bank[3][:, :].rearrange("p (b c) -> p b c", b=GB),
                                  z_tok[:, group(g), :], ALU.mult).then_inc(y_ready, 1)

            def y_stats(g):
                dve.wait_ge(yw_ready, did(g + 1))
                dve.wait_ge(fy_ready, did(g))
                dve.wait_ge(yqm_ready, did(GB * g))
                steps.link(moments(y_w, stats_y, mv_y, GB))
                centred(y_c, y_w, mv_y)
                dve.tensor_reduce(amax_y[:, :], y_c[:, :, :], AXIS.X, ALU.max,
                                  apply_absolute_value=True).then_inc(amaxy_ready, 1)

            def y_round(g):
                dve.wait_ge(yqm_ready, did(GB * (g + 1)))
                dve.wait_ge(yqt_psum, did(g))
                dve.tensor_scalar(y_q[:, :, :], y_qm[:, :, :], MAGIC, None, ALU.subtract).then_inc(yq_ready, 1)

            def first_residual(g):
                dve.wait_ge(proj_psum, did(g + 1))
                dve.wait_ge(x2x_ready, did(g + 1))
                dve.wait_ge(x1s_ready, did(g))
                for j in range(GB):
                    at = steps.mark(dve.scalar_tensor_tensor(res1[:, j, :], bank[3][:, j * D:(j + 1) * D],
                                                             s_y[:, j:j + 1], x2x[:, j, :], ALU.mult, ALU.add))
                steps.wait(at)
                moments(res1, stats1, mv1, GB).then_inc(var1_ready, 1)

            def first_norm(g):
                dve.wait_ge(rstd1_ready, did(g + 1))
                dve.wait_ge(x1t_psum, did(g))
                for j in range(GB):
                    ins = dve.tensor_scalar(x1_s[:, j, :], res1[:, j, :], mv1[:, j, 0:1], rstd1[:, j:j + 1],
                                            ALU.subtract, ALU.mult)
                ins.then_inc(x1s_ready, 1)

            def keep_x1(g):
                dve.wait_ge(x1s_ready, did(g + 1))
                dve.tensor_copy(x1[:, group(g), :], x1_s[:, :, :]).then_inc(x1_ready, 1)

            def first_max(g):
                dve.wait_ge(s1_psum, did(g + 1))
                dve.wait_ge(e1_ready, did(GB * g))
                steps.link(dve.tensor_reduce(nmx1[:, :], bank[7][:, 0:TS].rearrange("p (b k) -> p b k", b=GB), AXIS.X,
                                             ALU.max, negate=True))
                dve.tensor_scalar(nmx1[:, :], nmx1[:, :], vec[:, 4:5], vec[:, 4:5], ALU.subtract,
                                  ALU.add).then_inc(nmx1_ready, 1)

            def second_max(g):
                dve.wait_ge(s2_psum, did(g + 1))
                dve.wait_ge(e2_ready, did(GB * g))
                dve.tensor_scalar(shift2[:, :], bank[5][0:LS, T:T + GB], INV_SQRT_D, vec[0:LS, 5:6], ALU.mult, ALU.add)
                steps.link(dve.tensor_reduce(mx2[:, :], bank[5][0:LS, 0:T].rearrange("p (b k) -> p b k", b=GB), AXIS.X,
                                             ALU.max))
                steps.link(dve.tensor_tensor(mx2[:, :], mx2[:, :], shift2[:, :], ALU.add))
                dve.tensor_tensor(nmx2[:, :], shift2[:, :], mx2[:, :], ALU.subtract).then_inc(nmx2_ready, 1)

            def first_weights(g):
                dve.wait_ge(e1_ready, did(GB * (g + 1)))
                dve.wait_ge(e1t_psum, did(g))
                steps.link(dve.reciprocal(rden1[:, :], den1[:, :]))
                dve.tensor_tensor(e1n[:, :, 0:LS], e1[:, :, :], rden1[:, :].unsqueeze(2).to_broadcast([128, GB, LS]),
                                  ALU.mult).then_inc(e1n_ready, 1)

            def second_weights(g):
                dve.wait_ge(e2_ready, did(GB * (g + 1)))
                dve.wait_ge(w2i_psum, did(g))
                steps.link(dve.reciprocal(rden2[:, :], den2[:, :]))
                for j in range(GB):
                    ins = dve.tensor_scalar(ipn[:, j, :], c_("interp", LS), rden2[:, j:j + 1], None, ALU.mult)
                ins.then_inc(ipn_ready, 1)

            def difference(g):
                dve.wait_ge(res2_ready, did(g))
                for j in range(GB):
                    dve.wait_ge(s2c_ready, did(GB * g + j + 1))
                    dve.wait_ge(eg_ready, did(GB * g + j + 1))
                    dve.tensor_tensor(dif[:, j, :], bank[6 + j][:, 0:D], s2c[:, j, :], ALU.subtract).then_inc(dif_part, 1)

            def gate_attention(g):
                dve.wait_ge(eg_ready, did(GB * (g + 1)))
                dve.wait_ge(res2_ready, did(g))
                steps.link(dve.tensor_scalar(gt[:, :, :], eg[:, :, :], 1.0, None, ALU.add))
                steps.link(dve.reciprocal(gt[:, :, :], gt[:, :, :]))

            def blend(g):
                dve.wait_ge(dif_part, did(GB * (g + 1)))
                steps.link(dve.tensor_tensor(dif[:, :, :], dif[:, :, :], gt[:, :, :], ALU.mult))
                dve.wait_ge(rs_ready, did(g + 1))
                dve.wait_ge(x2_ready, did(g))
                dve.tensor_tensor(res2[:, :, :], dif[:, :, :], s2c_x1[:, :, :], ALU.add).then_inc(res2_ready, 1)

            def second_moments(g):
                dve.wait_ge(res2_ready, did(g + 1))
                moments(res2, stats2, mv2, GB).then_inc(var2_ready, 1)

            def second_norm(g):
                dve.wait_ge(rstd2_ready, did(g + 1))
                dve.wait_ge(x2t_psum, did(g))
                dve.wait_ge(x2b_ready, did(g))
                for j in range(GB):
                    ins = dve.tensor_scalar(x2_s[:, j, :], res2[:, j, :], mv2[:, j, 0:1], rstd2[:, j:j + 1],
                                            ALU.subtract, ALU.mult)
                ins.then_inc(x2_ready, 1)

            def router_logits(g):
                dve.wait_ge(logit_psum, did(g + 1))
                dve.tensor_copy(logit[:, group(g), :], bank[6][:, 0:GB * E].rearrange("p (b e) -> p b e", e=E))\
                   .then_inc(logit_ready, 1)

            dve.wait_ge(aexp_ready, 1)
            main_loop(dve, steps, [
                (mask_g, 1), (round_q, 2), (first_norm, 0), (input_stats, 3), (first_max, 0), (second_max, 0),
                (keep_x1, 0), (first_weights, 0), (decay_gram, 1), (conv, 2), (second_weights, 0), (gate_y, 1),
                (taps_bc, 2), (y_stats, 1), (taps_x, 2), (difference, 0), (gate_attention, 0), (blend, 0),
                (second_moments, 0), (y_round, 1), (softplus_start, 2), (second_norm, 0), (step_diagonal, 3),
                (first_residual, 1), (softplus_end, 2), (router_logits, 0)])

            bc = lambda v: v.unsqueeze(2).to_broadcast([128, NB, E])
            prio = c_("prio").unsqueeze(1).to_broadcast([128, NB, E])
            dve.wait_ge(score_ready, 1)
            steps.link(dve.tensor_scalar(score, score, 0.5, 0.5, ALU.mult, ALU.add))
            steps.link(dve.tensor_scalar(score, score, r("route_scale"), None, ALU.mult))

            def pick_largest(src, largest, mask):
                steps.link(dve.tensor_reduce(largest[:, :], src, AXIS.X, ALU.max))
                steps.link(dve.tensor_tensor(pick, src, bc(largest[:, :]), ALU.is_equal))
                steps.link(dve.tensor_tensor(pick, pick, prio, ALU.mult))
                steps.link(dve.tensor_reduce(prio1[:, :], pick, AXIS.X, ALU.max))
                steps.link(dve.tensor_tensor(mask, pick, bc(prio1[:, :]), ALU.is_equal))

            pick_largest(score, max1, first)
            steps.link(dve.scalar_tensor_tensor(rest, first, -3.0e38, score, ALU.mult, ALU.add))
            pick_largest(rest, max2, second)
            steps.link(dve.tensor_tensor(first, first, second, ALU.add))
            steps.link(dve.tensor_tensor(max1[:, :], max1[:, :], max2[:, :], ALU.add))
            steps.link(dve.reciprocal(max2[:, :], max1[:, :]))
            steps.link(dve.tensor_tensor(first, first, score, ALU.mult))
            steps.link(dve.tensor_tensor(top, first, bc(max2[:, :]), ALU.mult))
            steps.link(dve.tensor_copy(gate3[:, :, 0:E], top))
            steps.link(dve.tensor_tensor(rest, top, gate3[:, :, 0:E], ALU.subtract))
            steps.link(dve.tensor_copy(gate3[:, :, E:2 * E], rest))
            steps.link(dve.tensor_tensor(pick, rest, gate3[:, :, E:2 * E], ALU.subtract))
            dve.tensor_copy(gate3[:, :, 2 * E:3 * E], pick).then_inc(gate_ready, 1)

            def gate_hidden(g):
                for t in range(NE):
                    dve.wait_ge(hid_ready, did(NE * g + t + 1))
                    dve.wait_ge(gb_psum, did((NE + 1) * g + t + 1))
                    dve.tensor_tensor(hid[:, t, :], hid[:, t, :], bank[2 + t % 2][:, :], ALU.mult).then_inc(hg_ready, 1)

            def last_norm(g):
                dve.wait_ge(moe_psum, did(g + 1))
                dve.wait_ge(rstd3_ready, did(g))
                steps.link(dve.tensor_tensor(res3, bank[6][:, :].rearrange("p (b d) -> p b d", b=FB),
                                             x2b[:, bass.ds(g * FB, FB), :], ALU.add))
                moments(res3, stats3, mv3, FB).then_inc(var3_ready, 1)
                dve.wait_ge(rstd3_ready, did(g + 1))
                dve.wait_ge(out_done, did(16 * g))
                for j in range(FB):
                    ins = dve.tensor_scalar(y_out[:, j, :], res3[:, j, :], mv3[:, j, 0:1], rstd3[:, j:j + 1],
                                            ALU.subtract, ALU.mult)
                ins.then_inc(yout_ready, 1)

            start = steps.total()
            with dve.Fori(0, NF) as g:
                steps.enter(start, g, 1 + FB)
                gate_hidden(g)
                last_norm(g)
                steps.leave(start, NF, 1 + FB)

        @block.tensor
        def _(pe):
            pe.wait_ge(consts_ready, N_CONSTS)
            pe.wait_ge(wsum_ready, 1)
            pe.matmul(bank[7][:, 0:2], ones[:, :], wsum[:, :], start=True, stop=True).then_inc(wsum_psum, 1)

            pe.wait_ge(w2_in, 16)
            pe.wait_ge(c_in, 16)
            for at, lhs, rhs in ((0, w("wk_s"), w("wq_c")), (128, w("wq_s"), w("wk_c")),
                                 (256, w("wv_s"), w("wgT")[:, 0:128]), (384, w("wv_c"), w("wgT")[:, 128:256])):
                pe.matmul(bank[0][:, at:at + 128], lhs, rhs, start=True, stop=True)
            pe.wait_ge(bcol_ready, 1)
            for at, lhs, rhs in ((0, w("wq_c"), w("bk_s")), (1, w("wk_c"), w("bq_s")),
                                 (2, w("wk_s"), w("bq_c")), (3, w("wq_s"), w("bk_c")),
                                 (4, bq_all[:, 0, :], w("bk_s")), (5, bq_all[:, 1, :], w("bk_c"))):
                pe.matmul(bank[2][:, at:at + 1], lhs, rhs, start=True, stop=True)
            pe.matmul(bank[1][:, 0:128], bcol[:, 0, :], ident, start=True, stop=True)
            pe.matmul(bank[1][:, 256:384], bcol[:, 1, :], ident, start=True, stop=True)
            pe.matmul(bank[1][:, 128:256], bcol[:, 0, :], w("wgT")[:, 0:128], start=True, stop=False)
            pe.matmul(bank[1][:, 128:256], bcol[:, 1, :], w("wgT")[:, 128:256], start=False, stop=True).then_inc(a_psum, 1)

            def transpose_q(g):
                pe.wait_ge(diag_ready, did(g + 1))
                pe.wait_ge(q_ready, did(g + 1))
                pe.wait_ge(qt_ready, did(g))
                pe.matmul(bank[2][:, 0:T], ones[:, :], diag[:, :, :].rearrange("p b l -> p (b l)"), start=True, stop=True)
                for j in range(GB):
                    ins = pe.transpose(bank[2][:, T + j * 64:T + (j + 1) * 64].bitcast(BF16), q_bf[:, j, :], ident_bf[:, :])
                ins.then_inc(q_psum, 1)

            def project(g):
                pe.wait_ge(qt_ready, did(g + 1))
                pe.wait_ge(g_ready, did(g))
                pe.wait_ge(xtok_ready, did(g))
                for c in range(NC):
                    ins = pe.matmul(bank[c // 2][:, c % 2 * T:(c % 2 + 1) * T], win_q[:, c * 128:(c + 1) * 128], qT[:, :],
                                    start=True, stop=True)
                    if c % 2:
                        ins.then_inc(zx_psum, 1)

            def project_gates(g):
                for j in range(GB):
                    pe.wait_ge(xs_ready, did(2 * g + j + 1))
                    pe.matmul(bank[j][:, 0:DI + NH], qT[:, j * L:(j + 1) * L], win_q[:, 512:772],
                              start=True, stop=True).then_inc(zd_psum, 1)

            def gram(g):
                pe.wait_ge(zd_ready, did(GB * (g + 1)))
                pe.wait_ge(silu_ready, did(2 * g + 1))
                for j in range(GB):
                    ins = pe.matmul(bank[0][:, j * L:(j + 1) * L], xbc[:, 2, j, :], xbc[:, 3, j, :], start=True, stop=True)
                ins.then_inc(g_psum, 1)

            def transpose_xc(g):
                pe.wait_ge(zd_ready, did(GB * (g + 1)))
                pe.wait_ge(silu_ready, did(2 * g + 2))
                for j in range(GB):
                    for c in range(2):
                        ins = pe.transpose(bank[1][:, j * DI + c * 128:j * DI + (c + 1) * 128], xbc[:, c, j, :], ident)
                ins.then_inc(xt_psum, 1)

            def log_decays(g):
                pe.wait_ge(var1_ready, did(g))
                pe.wait_ge(x1t_ready, did(g))
                for j in range(GB):
                    pe.wait_ge(seg_ready, did(GB * g + j + 1))
                    pe.matmul(bank[3 + j][:, :], after, seg[:, j].rearrange("p h l -> p (h l)"),
                              start=True, stop=True).then_inc(ss_psum, 1)

            def scan_out(g):
                for j in range(GB):
                    pe.wait_ge(m_ready, did(GB * g + j + 1))
                    pe.wait_ge(udt_ready, did(GB * g + j + 1))
                    for h in range(NH):
                        o = bank[3][:, j * DI + h * HD:j * DI + (h + 1) * HD]
                        pe.matmul(o, ex[:, j, h, :], u_dt[:, j, h * HD:(h + 1) * HD], start=True, stop=False)
                        ins = pe.matmul(o, ident_d[:, h, :],
                                        x_tok[:, batch(g, j), h * HD:(h + 1) * HD].rearrange("p a c -> p (a c)"),
                                        start=False, stop=True)
                ins.then_inc(y_psum, 1)

            def transpose_y(g):
                pe.wait_ge(yq_ready, did(g + 1))
                for j in range(GB):
                    for c in range(2):
                        ins = pe.transpose(bank[4][:, (2 * j + c) * 64:(2 * j + c + 1) * 64].bitcast(BF16),
                                           y_q[:, j, c * 128:(c + 1) * 128], ident_bf[:, :])
                ins.then_inc(yqt_psum, 1)

            def project_out(g):
                pe.wait_ge(yqt_ready, did(g + 1))
                for j in range(GB):
                    for c in range(2):
                        ins = pe.matmul(bank[3][:, j * D:(j + 1) * D], y_qT[:, j, c, :], wout_q[:, c, :],
                                        start=c == 0, stop=c == 1)
                ins.then_inc(proj_psum, 1)

            def transpose_x1(g):
                pe.wait_ge(x1s_ready, did(g + 1))
                for j in range(GB):
                    ins = pe.transpose(bank[4][:, j * L:(j + 1) * L], x1_s[:, j, :], ident)
                ins.then_inc(x1t_psum, 1)

            def context_keys(g):
                pe.wait_ge(ctx_in, 16 * (g + 1))
                pe.wait_ge(x2t_ready, did(2 * g))
                pe.matmul(bank[5][:, 0:TS], a1T[:, :], ctx_s[:, :], start=True, stop=True)
                pe.matmul(bank[5][:, TS:2 * TS], a2T[:, :], ctx_s[:, :], start=True, stop=True).then_inc(p_psum, 1)

            def context_values(g):
                pe.wait_ge(ctx_in, 16 * (g + 1))
                pe.wait_ge(logit_ready, did(g))
                for j in range(GB):
                    ins = pe.matmul(bank[6][0:LS, j * 256:(j + 1) * 256], ctx_s[:, j * LS:(j + 1) * LS], wvs[:, :],
                                    start=True, stop=True)
                ins.then_inc(vvs_psum, 1)

            def first_scores(g):
                pe.wait_ge(p_ready, did(g + 1))
                pe.wait_ge(x1t_ready, did(g + 1))
                pe.wait_ge(dif_part, did(GB * g))
                for j in range(GB):
                    pe.matmul(bank[7][:, j * LS:(j + 1) * LS], cv1[:, :], ctx_s[:, j * LS:(j + 1) * LS],
                              start=True, stop=False)
                    ins = pe.matmul(bank[7][:, j * LS:(j + 1) * LS], x1T[:, j, :], p1[:, j * LS:(j + 1) * LS],
                                    start=False, stop=True)
                ins.then_inc(s1_psum, 1)

            def second_scores(g):
                pe.wait_ge(p_ready, did(g + 1))
                pe.wait_ge(x1t_ready, did(g + 1))
                for j in range(GB):
                    pe.matmul(bank[5][0:LS, T + j:T + j + 1], ctx_s[:, j * LS:(j + 1) * LS], cvec2[:, :],
                              start=True, stop=True)
                for j in range(GB):
                    ins = pe.matmul(bank[5][0:LS, j * L:(j + 1) * L], p2[:, j * LS:(j + 1) * LS], x1T[:, j, :],
                                    start=True, stop=True)
                ins.then_inc(s2_psum, 1)

            def token_products(g):
                pe.wait_ge(x1t_ready, did(g + 1))
                pe.wait_ge(vvs_ready, did(g + 1))
                for j in range(GB):
                    ins = pe.matmul(bank[6][:, j * 256:(j + 1) * 256], x1T[:, j, :], wvc[:, :], start=True, stop=True)
                ins.then_inc(vvc_psum, 1)

            def transpose_e1(g):
                pe.wait_ge(e1n_ready, did(g + 1))
                for j in range(GB):
                    ins = pe.transpose(bank[7][0:KR, j * L:(j + 1) * L], e1n[:, j, :], ident)
                ins.then_inc(e1t_psum, 1)

            def interpolate(g):
                pe.wait_ge(ipn_ready, did(g + 1))
                for j in range(GB):
                    ins = pe.matmul(bank[5][:, j * L:(j + 1) * L], e2[:, j, :], ipn[:, j, :], start=True, stop=True)
                ins.then_inc(w2i_psum, 1)

            def attend(g):
                pe.wait_ge(vvc_ready, did(g + 1))
                pe.wait_ge(e1t_ready, did(g + 1))
                pe.wait_ge(w2i_ready, did(g + 1))
                for j in range(GB):
                    b = bank[6 + j]
                    pe.matmul(b[:, 0:384], e1T[:, j, :], vvs[0:KR, j, :], start=True, stop=False)
                    pe.matmul(b[:, 128:384], w2i[:, j, :], vvc[:, j, :], start=False, stop=True).then_inc(o_psum, 1)

            def transpose_x2(g):
                pe.wait_ge(x2_ready, did(g + 1))
                for j in range(GB):
                    ins = pe.transpose(bank[5][:, j * L:(j + 1) * L], x2_s[:, j, :], ident)
                ins.then_inc(x2t_psum, 1)

            def router_logits(g):
                pe.wait_ge(x2t_ready, did(2 * g + 1))
                for j in range(GB):
                    ins = pe.matmul(bank[6][:, j * E:(j + 1) * E], x2T_s[:, j, :], w("gate_w"), start=True, stop=True)
                ins.then_inc(logit_psum, 1)

            pe.wait_ge(ident_ready, 1)
            pe.wait_ge(win_ready, 1)
            pe.wait_ge(attw_ready, 1)
            main_loop(pe, Steps(pe, None), [
                (context_values, 0), (transpose_x1, 0), (transpose_q, 2), (first_scores, 0), (second_scores, 0),
                (log_decays, 1), (project, 2), (token_products, 0), (scan_out, 1), (transpose_e1, 0),
                (project_gates, 2), (interpolate, 0), (attend, 0), (gram, 2), (transpose_xc, 2), (transpose_y, 1),
                (project_out, 1), (transpose_x2, 0), (router_logits, 0), (context_keys, 1)])

            pe.wait_ge(gate_ready, 1)
            pe.wait_ge(sel_ready, 1)
            pe.wait_ge(x2t_ready, did(2 * NG))
            pe.wait_ge(logit_ready, did(NG))
            pe.wait_ge(g_ready, did(NG))
            pe.wait_ge(y_ready, did(NG))

            def up(g):
                for j in range(FB):
                    ins = pe.matmul(bank[5][0:3 * E, j * L:(j + 1) * L],
                                    gate3[:, bass.ds(g * FB + j, 1), :].rearrange("p a e -> p (a e)"), ident_bf[:, :],
                                    start=True, stop=True)
                ins.then_inc(gt_psum, 1)
                pe.wait_ge(gt_ready, did(g + 1))
                for t in range(NE + 1):
                    if t >= 2:
                        pe.wait_ge(hid_ready, did(NE * g + t - 1))
                        pe.wait_ge(hg_ready, did(NE * g + t - 1))
                    elif t == 1:
                        pe.wait_ge(hg_ready, did(NE * g))
                    else:
                        pe.wait_ge(hs_ready, did(2 * g))
                    pe.matmul(bank[2 + t % 2][:, :], sel_bf[:, t * 128:(t + 1) * 128], gT[:, :],
                              start=True, stop=True).then_inc(gb_psum, 1)
                    m, lhs = (128, w("w1")[:, t * 128:(t + 1) * 128]) if t < NE else (HID, w("ws1"))
                    pe.matmul(bank[t % 2][0:m, :], lhs, x2T[:, bass.ds(g * FT, FT)],
                              start=True, stop=True).then_inc(h_psum, 1)

            def down(g):
                pe.wait_ge(hg_ready, did(NE * (g + 1)))
                pe.wait_ge(hs_ready, did(2 * (g + 1)))
                pe.wait_ge(var3_ready, did(g))
                for j in range(FB):
                    for t in range(NE):
                        pe.matmul(bank[6][:, j * D:(j + 1) * D], hid[:, t, j * L:(j + 1) * L],
                                  w("w2")[:, t * D:(t + 1) * D], start=t == 0, stop=False)
                    ins = pe.matmul(bank[6][:, j * D:(j + 1) * D], hid_s[0:96, j * L:(j + 1) * L], w("w2s", 96),
                                    start=False, stop=True)
                ins.then_inc(moe_psum, 1)

            with pe.Fori(0, NF) as g:
                up(g)
                down(g)


def kernel(**inputs):
    import numpy as _np
    import concourse.bacc as _bacc
    from concourse import mybir as _mybir
    from concourse.bass_utils import run_bass_kernel_spmd as _run

    a = {k.removeprefix("L0_"): _np.asarray(v) for k, v in inputs.items()}
    f32 = _np.float32

    def tiles(m):
        n = m.shape[0] // 128
        return m.reshape(n, 128, -1).transpose(1, 0, 2).reshape(128, -1)

    def column(v):
        out = _np.zeros((128, 1), f32)
        out[:v.shape[0], 0] = v
        return out

    w_in = a["attn_in_proj_w"]
    w2s = _np.zeros((128, 128), f32)
    w2s[:HID] = a["ffn_Ws2"]
    w2s[HID:HID + E] = a["ffn_b2"]
    parts = {
        "win": _np.concatenate([w_in[DI:DI + 512], w_in[:DI], w_in[DI + 512:]]).T,
        "wout": tiles(a["attn_out_proj_w"].T),
        "conv_w": tiles(a["attn_conv_w"]), "conv_b": tiles(a["attn_conv_b"][:, None]),
        "wq_c": a["xattn_Wq_c"], "wk_s": a["xattn_Wk_s"], "wq_s": a["xattn_Wq_s"], "wk_c": a["xattn_Wk_c"],
        "wv_s": a["xattn_Wv_s"], "wv_sT": a["xattn_Wv_s"].T, "wv_c": a["xattn_Wv_c"], "wv_cT": a["xattn_Wv_c"].T,
        "wgT": tiles(a["xattn_Wg"].T),
        "bq_c": a["xattn_bq_c"][:, None], "bk_s": a["xattn_bk_s"][:, None],
        "bq_s": a["xattn_bq_s"][:, None], "bk_c": a["xattn_bk_c"][:, None],
        "bv_s": a["xattn_bv_s"][:, None], "bv_c": a["xattn_bv_c"][:, None],
        "gate_w": a["ffn_gate_W"], "w1": a["ffn_W1"].transpose(1, 0, 2).reshape(D, E * HID), "ws1": a["ffn_Ws1"],
        "b1": tiles(a["ffn_b1"].reshape(-1, 1)), "bs1": column(a["ffn_bs1"]),
        "w2": tiles(a["ffn_W2"].reshape(E * HID, D)), "w2s": w2s,
    }
    wpack = _np.concatenate([parts[n] for n, _ in _COLS], axis=1)
    rows = {
        "norm_w": a["attn_norm_w"], "out_norm_w": a["attn_out_norm_w"], "Dp": a["attn_Dp"],
        "A_log": a["attn_A_log"], "dt_bias": a["attn_dt_bias"], "bg": a["xattn_bg"],
        "bv_s": a["xattn_bv_s"], "bv_c": a["xattn_bv_c"], "bs2": a["ffn_bs2"],
        "route_scale": a["ffn_route_scale"].reshape(1),
    }
    rpack = _np.concatenate([rows[n] for n, _ in _ROWS])

    i = _np.arange(128)
    interp = _np.zeros((128, L), f32)
    pos = _np.clip((_np.arange(L, dtype=f32) + f32(0.5)) * f32(LS / L) - f32(0.5), f32(0.0), f32(LS - 1))
    lo = _np.floor(pos).astype(_np.int32)
    hi = _np.minimum(lo + 1, LS - 1)
    frac = (pos - lo.astype(f32)).astype(f32)
    for l in range(L):
        interp[lo[l], l] += f32(1) - frac[l]
        interp[hi[l], l] += frac[l]
    sel = _np.zeros((128, NE + 1, 128), f32)
    for part in range(3):
        for e in range(E):
            sel[part * E + e, e * HID // 128, e * HID % 128:e * HID % 128 + HID] = 1
            sel[part * E + e, NE, HID + e] = 1
    prio = _np.broadcast_to(_np.arange(E, 0, -1).astype(f32), (128, E))
    cpack = _np.concatenate([_np.eye(128, dtype=f32), (i[:, None] <= i[None, :]).astype(f32),
                             (i[:, None] > i[None, :]).astype(f32), interp, sel.reshape(128, -1), prio], axis=1)

    arrays = {"x": a["x"], "ctxT": a["ctx_1024"].transpose(2, 0, 1).reshape(D, NB * LS),
              "wpack": wpack, "rpack": rpack, "cpack": cpack}
    nc = _bacc.Bacc("TRN2", target_bir_lowering=False, num_devices=1)
    args = []
    for name in arrays:
        arrays[name] = _np.ascontiguousarray(arrays[name])
        args.append(nc.dram_tensor(name, arrays[name].shape, _mybir.dt.from_np(arrays[name].dtype),
                                   kind="ExternalInput").ap())
    args.append(nc.dram_tensor("out", (NB, L, D), FP32, kind="ExternalOutput").ap())
    build(nc, *args)
    res = _run(nc, [arrays], core_ids=[0])
    return res.results[0]["out"]
```

```python
import numpy as np
import concourse.bass as bass
from concourse import mybir
from contextlib import ExitStack

FP32 = mybir.dt.float32
BF16 = mybir.dt.bfloat16
ALU = mybir.AluOpType
ACT = mybir.ActivationFunctionType
AXIS = mybir.AxisListType

NB, L, D = 16, 128, 128
LS = 77
GB = 2
NG = NB // GB
T = GB * L
TS = GB * LS
DI, NH, HD = 256, 4, 64
NC = 4
TAPS = 4
E, HID = 8, 64
NE = E * HID // 128
NT = NE + 1
MAGIC = 12582912.0
FB = 4
NF = NB // FB
FT = FB * L
INV_SQRT_D = float(1.0 / np.sqrt(np.float32(D)))

_COLS = [("win", 772), ("wout", 256), ("conv_w", NC * TAPS), ("conv_b", NC),
         ("wq_c", 128), ("wk_s", 128), ("wq_s", 128), ("wk_c", 128),
         ("wv_s", 128), ("wv_sT", 128), ("wv_c", 128), ("wv_cT", 128), ("wgT", 256),
         ("bq_c", 1), ("bk_s", 1), ("bq_s", 1), ("bk_c", 1), ("bv_s", 1), ("bv_c", 1),
         ("gate_w", E), ("w1", 512), ("ws1", HID), ("b1", NE), ("bs1", 1),
         ("w2", 512), ("w2s", 128)]
_ROWS = [("norm_w", D), ("out_norm_w", DI), ("Dp", NH), ("A_log", NH), ("dt_bias", NH),
         ("bg", 128), ("bv_s", 128), ("bv_c", 128), ("bs2", D), ("route_scale", 1)]
_CONSTS = [("ident", 128), ("upto", 128), ("after", 128), ("interp", 128), ("sel", (NE + 1) * 128), ("prio", E)]


def _places(cols):
    at, out = 0, {}
    for name, n in cols:
        out[name] = (at, at + n)
        at += n
    return out, at


COL, NCOL = _places(_COLS)
ROW, NROW = _places(_ROWS)
CST, NCST = _places(_CONSTS)


class Steps:

    def __init__(self, eng, sem):
        self.eng, self.sem, self.base, self.n = eng, sem, 0, 0

    def mark(self, ins):
        ins.then_inc(self.sem, 1)
        self.n += 1
        return self.base + self.n

    def wait(self, count):
        self.eng.wait_ge(self.sem, count)

    def link(self, ins):
        self.wait(self.mark(ins))

    def total(self):
        return self.base + self.n

    def enter(self, start, steps, per):
        self.base, self.n = start + steps * per, 0

    def leave(self, start, steps, per):
        assert self.n == per, (self.n, per)
        self.base, self.n = start + steps * per, 0


def build(nc, x, ctxT, wpack, rpack, cpack, out):
    ctx = ExitStack()
    with ctx:
        def sb(name, shape, dt=FP32):
            return ctx.enter_context(nc.sbuf_tensor(name, shape, dt))

        def sem(name):
            return ctx.enter_context(nc.semaphore(name))

        counters = []

        def counter(name):
            counters.append(sem(name))
            return counters[-1]

        def did(n):
            return n + 1

        W = sb("W", [128, NCOL])
        R = sb("R", [128, NROW])
        C = sb("C", [128, NCST])

        def w(name, rows=128):
            a, b = COL[name]
            return W[0:rows, a:b]

        def r(name, rows=128):
            a, b = ROW[name]
            return R[0:rows, a:b]

        def c_(name, rows=128):
            a, b = CST[name]
            return C[0:rows, a:b]

        ident, upto, after = c_("ident"), c_("upto"), c_("after")
        ident_bf = sb("ident_bf", [128, 128], BF16)
        ones = sb("ones", [128, 128])
        neg_half = sb("neg_half", [128, GB])
        neg_one = sb("neg_one", [128, GB])
        neg_half4 = sb("neg_half4", [128, FB])
        eps5 = sb("eps5", [128, FB])
        magic_bias = sb("magic_bias", [128, 1])
        win_q = sb("win_q", [128, 772], BF16)
        wout_q = sb("wout_q", [128, 2, 128], BF16)
        low = sb("low", [128, 772])
        wsum = sb("wsum", [128, 2])
        wscale = sb("wscale", [128, 4])
        eps5_quarter = sb("eps5_quarter", [128, GB])
        a_exp = sb("a_exp", [128, NH])
        a1T = sb("a1T", [128, 128])
        a2T = sb("a2T", [128, 128])
        wvs = sb("wvs", [128, 256])
        wvc = sb("wvc", [128, 256])
        vec = sb("vec", [128, 6])
        cvec2 = sb("cvec2", [128, 1])
        bq_all = sb("bq_all", [128, 2, 128])
        cv1 = sb("cv1", [128, 128])
        bcol = sb("bcol", [128, 2, 128])

        x_all = sb("x_all", [128, NB, D])
        x_tok = sb("x_tok", [128, NB, DI])
        z_tok = sb("z_tok", [128, NB, DI])
        g_all = sb("g_all", [128, NB, L])
        dt_sp = sb("dt_sp", [128, NB, NH])
        a_dt = sb("a_dt", [128, NB, NH])
        s_in = sb("s_in", [128, NB])
        x1 = sb("x1", [128, NB, D])
        x2T = sb("x2T", [128, NB * L])
        x2b = x_all
        logit = sb("logit", [128, NB, E])

        u = sb("u", [128, GB, D])
        uc = sb("uc", [128, GB, D])
        junk = sb("junk", [128, GB, D])
        stats = sb("stats", [128, GB, 6])
        ms_x = sb("ms_x", [128, GB])
        mv_u = sb("mv_u", [128, GB, 2])
        amax_u = sb("amax_u", [128, GB])
        s_x = sb("s_x", [128, GB])
        f_x = sb("f_x", [128, GB])
        pool_t = [sb(f"pool_t{i}", [128, GB]) for i in range(3)]
        qm = sb("qm", [128, GB, D])
        q_bf = sb("q_bf", [128, GB, D], BF16)
        diag = sb("diag", [128, GB, 128])
        qT = sb("qT", [128, T], BF16)
        s_row = sb("s_row", [128, T])
        xs = sb("xs", [128, NC, GB, TAPS - 1 + L])
        acc = sb("acc", [128, NC, GB, L])
        xbc = sb("xbc", [128, NC, GB, L])
        dt_raw = sb("dt_raw", [128, GB, NH])
        v_dt = sb("v_dt", [128, GB * NH])
        na_dt = sb("na_dt", [128, GB * NH])
        e_dt = sb("e_dt", [128, GB * NH])
        l_dt = sb("l_dt", [128, GB * NH])

        seg = sb("seg", [128, GB, NH, L])
        ex = sb("ex", [128, GB, NH, L])
        u_dt = sb("u_dt", [128, GB, DI])
        y = sb("y", [128, GB, DI])
        junk_y = sb("junk_y", [128, GB, DI])
        y_w = sb("y_w", [128, GB, DI])
        y_c = sb("y_c", [128, GB, DI])
        y_qm = sb("y_qm", [128, GB, DI])
        y_q = sb("y_q", [128, GB, DI], BF16)
        y_qT = sb("y_qT", [128, GB, 2, L], BF16)
        ms_y = sb("ms_y", [128, GB])
        mv_y = sb("mv_y", [128, GB, 2])
        amax_y = sb("amax_y", [128, GB])
        s_y = sb("s_y", [128, GB])
        f_y = sb("f_y", [128, GB])
        stats_y = sb("stats_y", [128, GB, 6])
        s_y_half = sb("s_y_half", [128, GB])
        x_d = sb("x_d", [128, GB, DI])
        res1 = sb("res1", [128, GB, D])
        stats1 = sb("stats1", [128, GB, 6])
        mv1 = sb("mv1", [128, GB, 2])
        rstd1 = sb("rstd1", [128, GB])
        x1_s = sb("x1_s", [128, GB, D])
        x1T = sb("x1T", [128, GB, L])

        BIAS = 96
        KR = BIAS + 1
        ctx_s = sb("ctx_s", [128, TS])
        p1 = sb("p1", [128, TS])
        p2 = sb("p2", [128, TS])
        vvs = sb("vvs", [128, GB, 384])
        vvc = sb("vvc", [128, GB, 256])
        nmx1 = sb("nmx1", [128, GB])
        den1 = sb("den1", [128, GB])
        rden1 = sb("rden1", [128, GB])
        mx2 = sb("mx2", [LS, GB])
        shift2 = sb("shift2", [LS, GB])
        nmx2 = sb("nmx2", [LS, GB])
        den2 = sb("den2", [LS, GB])
        rden2 = sb("rden2", [LS, GB])
        e1 = sb("e1", [128, GB, LS])
        e1n = sb("e1n", [128, GB, KR])
        e1T = sb("e1T", [KR, GB, L])
        e2 = sb("e2", [LS, GB, L])
        ipn = sb("ipn", [LS, GB, L])
        w2i = sb("w2i", [128, GB, L])
        eg = sb("eg", [128, GB, D])
        gt = sb("gt", [128, GB, D])
        s2c = sb("s2c", [128, GB, D])
        s2c_x1 = sb("s2c_x1", [128, GB, D])
        dif = sb("dif", [128, GB, D])
        res2 = sb("res2", [128, GB, D])
        stats2 = sb("stats2", [128, GB, 6])
        mv2 = sb("mv2", [128, GB, 2])
        rstd2 = sb("rstd2", [128, GB])
        x2_s = sb("x2_s", [128, GB, D])
        x2T_s = sb("x2T_s", [128, GB, L])

        xf = x_tok[:, :, :].rearrange("p b c -> p (b c)")
        hid = xf[:, 0:NE * FT].rearrange("p (t n) -> p t n", t=NE)
        hid_s = xf[:, NE * FT:(NE + 1) * FT]
        res3 = xf[:, 5 * FT:6 * FT].rearrange("p (b d) -> p b d", b=FB)
        y_out = xf[:, 6 * FT:7 * FT].rearrange("p (b d) -> p b d", b=FB)
        router_bufs = [sb(f"router_buf{i}", [128, NB, E]) for i in range(6)]
        gT = sb("gT", [3 * E, NB * L], BF16)
        nm3 = sb("nm3", [128, FB])
        sel_bf = sb("sel_bf", [3 * E, (NE + 1) * 128], BF16)
        max1 = sb("max1", [128, NB])
        max2 = sb("max2", [128, NB])
        prio1 = sb("prio1", [128, NB])
        gate3 = sb("gate3", [128, NB, 3 * E], BF16)
        stats3 = sb("stats3", [128, FB, 6])
        mv3 = sb("mv3", [128, FB, 2])
        rstd3 = sb("rstd3", [128, FB])

        bank = [ctx.enter_context(nc.psum_tensor(f"bank{i}", [128, 512], FP32)) for i in range(8)]

        x0_in = sem("x0_in")
        x_in = sem("x_in")
        sp_settled = sem("sp_settled")
        w_in = sem("w_in")
        w2_in = sem("w2_in")
        r_in = sem("r_in")
        c_in = sem("c_in")
        c2_in = sem("c2_in")
        act_steps = sem("act_steps")
        dve_steps = sem("dve_steps")
        pool_steps = sem("pool_steps")
        pool_settled = sem("pool_settled")
        pe_settled = sem("pe_settled")
        dve_settled = sem("dve_settled")
        consts_ready = sem("consts_ready")
        ident_ready = sem("ident_ready")
        magic_ready = sem("magic_ready")
        wsum_ready = sem("wsum_ready")
        wsum_psum = sem("wsum_psum")
        win_ready = sem("win_ready")
        aexp_ready = sem("aexp_ready")
        bcol_ready = sem("bcol_ready")
        a_psum = sem("a_psum")
        attw_ready = sem("attw_ready")
        sel_ready = sem("sel_ready")
        score_ready = sem("score_ready")
        gt_att_ready = counter("gt_att_ready")
        res3_ready = counter("res3_ready")
        tap0_pool = counter("tap0_pool")
        xd_ready = counter("xd_ready")
        gate_ready = sem("gate_ready")
        out_done = counter("out_done")
        ctx_in = sem("ctx_in")
        (u_ready, ms_ready, amax_ready, fx_ready, qm_ready, q_ready, diag_ready, q_psum, qt_ready, zx_psum,
         xs_ready, tap0_ready, conv_ready, silu_ready, g_psum, xt_psum, g_ready, xtok_ready, zd_psum, zd_ready,
         v_ready, l_ready, dt_ready) = (counter(n) for n in (
            "u_ready ms_ready amax_ready fx_ready qm_ready q_ready diag_ready q_psum qt_ready zx_psum "
            "xs_ready tap0_ready conv_ready silu_ready g_psum xt_psum g_ready xtok_ready zd_psum zd_ready "
            "v_ready l_ready dt_ready").split())
        (seg_ready, udt_ready, ss_psum, ex_ready, m_ready, y_psum, y_ready, msy_ready, yw_ready, amaxy_ready,
         fy_ready, yqm_ready, yq_ready, yqt_psum, yqt_ready, proj_psum, var1_ready, rstd1_ready,
         x1s_ready, x1_ready, x1t_psum, x1t_ready) = (counter(n) for n in (
            "seg_ready udt_ready ss_psum ex_ready m_ready y_psum y_ready msy_ready yw_ready amaxy_ready "
            "fy_ready yqm_ready yq_ready yqt_psum yqt_ready proj_psum var1_ready rstd1_ready "
            "x1s_ready x1_ready x1t_psum x1t_ready").split())
        (p_psum, vvs_psum, p_ready, vvs_ready, vvc_psum, vvc_ready, s1_psum, s2_psum, nmx1_ready, nmx2_ready,
         e1_ready, e2_ready, e1n_ready, ipn_ready, e1t_psum, w2i_psum, e1t_ready, w2i_ready, o_psum, s2c_ready,
         eg_ready, rs_ready, dif_part, res2_ready, var2_ready, rstd2_ready, x2_ready, x2b_ready, x2t_psum,
         x2t_ready, logit_psum, logit_ready) = (counter(n) for n in (
            "p_psum vvs_psum p_ready vvs_ready vvc_psum vvc_ready s1_psum s2_psum nmx1_ready nmx2_ready "
            "e1_ready e2_ready e1n_ready ipn_ready e1t_psum w2i_psum e1t_ready w2i_ready o_psum s2c_ready "
            "eg_ready rs_ready dif_part res2_ready var2_ready rstd2_ready x2_ready x2b_ready x2t_psum "
            "x2t_ready logit_psum logit_ready").split())
        (gt_psum, gt_ready, h_psum, gb_psum, hid_ready, hs_ready, hg_ready, moe_psum, var3_ready, rstd3_ready,
         yout_ready) = (counter(n) for n in (
            "gt_psum gt_ready h_psum gb_psum hid_ready hs_ready hg_ready moe_psum var3_ready rstd3_ready "
            "yout_ready").split())

        W_FIRST = COL["wq_c"][0]
        N_CONSTS = 11
        C_FIRST = CST["interp"][0]

        def batch(g, j):
            return bass.ds(g * GB + j, 1)

        def group(g):
            return bass.ds(g * GB, GB)

        ATT, SCAN_B, SCAN_A, PROJ = 0, 1, 2, 3

        def main_loop(eng, steps, blocks, before=None, last_extras=()):
            def step(k):
                for fn, lead in blocks:
                    if not isinstance(k, int) or 0 <= k + lead < NG:
                        fn(k + lead)

            def last_step():
                mine = [fn for fn, lead in blocks if lead == 0]
                at, first = 0, len(mine) // 3
                for i, fn in enumerate(mine):
                    if i >= first:
                        upto = -(-len(last_extras) * (i + 1 - first) // (len(mine) - first))
                        for extra in last_extras[at:upto]:
                            extra()
                        at = upto
                    fn(NG - 1)

            for k in range(-PROJ, 0):
                if before and k in before:
                    before[k]()
                step(k)
            before = steps.total()
            step(0)
            start = steps.total()
            per = start - before
            with eng.Fori(1, NG - PROJ) as k:
                steps.enter(start, k - 1, per)
                step(k)
                steps.leave(start, NG - PROJ - 1, per)
            for k in range(NG - PROJ, NG - 1):
                step(k)
            last_step()

        block = ctx.enter_context(nc.Block())

        @block.sync
        def _(sp):
            sp.dma_start(x_all[:, 0:4, :], x[0:4].rearrange("b l d -> l b d")).then_inc(x0_in, 16)
            sp.dma_start(W[:, 0:W_FIRST], wpack[:, 0:W_FIRST]).then_inc(w_in, 16)
            for i in range(1, 4):
                sp.dma_start(x_all[:, 4 * i:4 * i + 4, :],
                             x[4 * i:4 * i + 4].rearrange("b l d -> l b d")).then_inc(x_in, 16)
            sp.dma_start(W[:, W_FIRST:NCOL], wpack[:, W_FIRST:NCOL]).then_inc(w2_in, 16)
            for s in counters:
                sp.sem_inc(s, 1)

            def load_context(g):
                sp.wait_ge(vvs_psum, did(g))
                sp.wait_ge(s1_psum, did(g))
                sp.wait_ge(s2_psum, did(g))
                sp.sem_inc(sp_settled, 1)
                sp.dma_start(ctx_s[:, :], ctxT[:, bass.ds(g * TS, TS)]).then_inc(ctx_in, 16)

            load_context(0)
            with sp.Fori(1, NG) as g:
                load_context(g)

            with sp.Fori(0, NF) as g:
                sp.wait_ge(yout_ready, did(g + 1))
                sp.sem_inc(sp_settled, 1)
                sp.dma_start(out[bass.ds(g * FB, FB)].rearrange("b l d -> l b d"), y_out).then_inc(out_done, 16)
            sp.wait_ge(out_done, did(16 * NF))

        @block.gpsimd
        def _(pool):
            steps = Steps(pool, pool_steps)
            for what, value in ((ones[:, :], 1.0), (neg_half[:, :], -0.5), (neg_one[:, :], -1.0), (neg_half4[:, :], -0.5),
                                (eps5[:, :], 1e-5), (eps5_quarter[:, :], 0.25e-5), (xs[:, :, :, 0:TAPS - 1], 0.0), (vvs[:, :, :], 0.0),
                                (e1n[:, :, :], 0.0), (bcol[:, :, :], 0.0)):
                pool.memset(what, value).then_inc(consts_ready, 1)
            pool.wait_ge(consts_ready, N_CONSTS - 1)
            pool.memset(e1n[:, :, BIAS:KR], 1.0).then_inc(consts_ready, 1)
            pool.wait_ge(consts_ready, N_CONSTS)

            def settle():
                pool.sem_inc(pool_settled, 1)

            def quant_scales(ms, mv, amax, s_to, f_to, ready, half_to=None):
                a, b, t = (p[:, :] for p in pool_t)
                settle()
                steps.link(pool.tensor_scalar(a, ms[:, :], 1e-5, 1e-11, ALU.mult, ALU.add))
                steps.link(pool.tensor_tensor(b, a, mv[:, :, 1], ALU.add))
                steps.link(pool.tensor_tensor(t, b, neg_half[:, :], ALU.pow))
                steps.link(pool.tensor_tensor(a, t, amax[:, :], ALU.mult))
                settle()
                steps.link(pool.tensor_scalar(s_to[:, :], a, 1e-5, 1.0 / 127.0, ALU.max, ALU.mult))
                if half_to is not None:
                    settle()
                    pool.tensor_scalar(half_to[:, :], s_to[:, :], 0.5, None, ALU.mult)
                steps.link(pool.tensor_tensor(b, s_to[:, :], neg_one[:, :], ALU.pow))
                pool.tensor_tensor(f_to[:, :], t, b, ALU.mult).then_inc(ready, 1)

            def rstd(var, dst, half, eps, ready):
                steps.link(pool.tensor_tensor(dst[:, :], var[:, :, 1], eps[:, 0:half.shape[1]], ALU.add))
                pool.tensor_tensor(dst[:, :], dst[:, :], half, ALU.pow).then_inc(ready, 1)

            def scaled_input(g):
                pool.wait_ge(amax_ready, did(g))
                settle()
                pool.tensor_tensor(u[:, :, :], x_all[:, group(g), :],
                                   r("norm_w").unsqueeze(1).to_broadcast([128, GB, D]), ALU.mult).then_inc(u_ready, 1)

            def input_scales(g):
                pool.wait_ge(ms_ready, did(GB * (g + 1)))
                pool.wait_ge(amax_ready, did(g + 1))
                pool.wait_ge(zd_ready, did(GB * g))
                pool.wait_ge(diag_ready, did(g))
                quant_scales(ms_x, mv_u, amax_u, s_x, f_x, fx_ready)

            def scan_inputs(g):
                pool.wait_ge(dt_ready, did(g + 1))
                pool.wait_ge(ss_psum, did(GB * g))
                pool.wait_ge(y_psum, did(g))
                pool.wait_ge(xtok_ready, did(g + 1))
                settle()
                for j in range(GB):
                    pool.tensor_tensor(seg[:, j], upto.unsqueeze(1).to_broadcast([128, NH, L]),
                                       a_dt[:, batch(g, j), :].rearrange("p a h -> p (a h)").unsqueeze(2)
                                       .to_broadcast([128, NH, L]), ALU.mult).then_inc(seg_ready, 1)
                    pool.tensor_tensor(x_d[:, j].rearrange("p (h c) -> p h c", h=NH),
                                       x_tok[:, batch(g, j), :].rearrange("p a (h c) -> p (a h) c", h=NH),
                                       r("Dp").unsqueeze(2).to_broadcast([128, NH, HD]), ALU.mult).then_inc(xd_ready, 1)
                    pool.tensor_tensor(u_dt[:, j].rearrange("p (h c) -> p h c", h=NH),
                                       x_tok[:, batch(g, j), :].rearrange("p a (h c) -> p (a h) c", h=NH),
                                       dt_sp[:, batch(g, j), :].rearrange("p a h -> p (a h)").unsqueeze(2)
                                       .to_broadcast([128, NH, HD]), ALU.mult).then_inc(udt_ready, 1)

            def first_tap(g):
                pool.wait_ge(silu_ready, did(2 * g))
                pool.wait_ge(xs_ready, did(2 * g + 1))
                settle()
                pool.tensor_scalar(acc[:, 1, :, :], xs[:, 1, :, TAPS - 1:],
                                   w("conv_w")[:, 2 * TAPS - 1:2 * TAPS], w("conv_b")[:, 1:2],
                                   ALU.mult, ALU.add).then_inc(tap0_pool, 1)

            def scaled_y(g):
                pool.wait_ge(y_ready, did(g + 1))
                pool.wait_ge(amaxy_ready, did(g))
                pool.tensor_tensor(y_w[:, :, :], y[:, :, :], r("out_norm_w").unsqueeze(1).to_broadcast([128, GB, DI]),
                                   ALU.mult).then_inc(yw_ready, 1)

            def y_scales(g):
                pool.wait_ge(msy_ready, did(GB * (g + 1)))
                pool.wait_ge(amaxy_ready, did(g + 1))
                pool.wait_ge(var1_ready, did(g))
                quant_scales(ms_y, mv_y, amax_y, s_y, f_y, fy_ready, half_to=s_y_half)

            def first_rstd(g):
                pool.wait_ge(var1_ready, did(g + 1))
                rstd(mv1, rstd1, neg_half[:, :], eps5_quarter, rstd1_ready)

            def attention_residual(g):
                pool.wait_ge(s2c_ready, did(GB * (g + 1)))
                pool.wait_ge(x1_ready, did(g + 1))
                pool.wait_ge(res2_ready, did(g))
                settle()
                pool.tensor_tensor(s2c_x1[:, :, :], s2c[:, :, :], x1[:, group(g), :], ALU.add).then_inc(rs_ready, 1)

            def second_rstd(g):
                pool.wait_ge(var2_ready, did(g + 1))
                rstd(mv2, rstd2, neg_half[:, :], eps5, rstd2_ready)

            def expert_residual(g):
                pool.wait_ge(x2_ready, did(g + 1))
                settle()
                pool.tensor_tensor(x2b[:, group(g), :], x2_s[:, :, :],
                                   r("bs2").unsqueeze(1).to_broadcast([128, GB, D]), ALU.add).then_inc(x2b_ready, 1)

            pool.wait_ge(r_in, 16)
            pool.wait_ge(c_in, 16)
            pool.wait_ge(x0_in, 16)
            pool.wait_ge(w_in, 16)

            def later_inputs():
                pool.wait_ge(x_in, 16 * 3)

            main_loop(pool, steps, [
                (scaled_input, 3), (first_rstd, 0), (scan_inputs, 1), (first_tap, 2), (scaled_y, 1),
                (attention_residual, 0), (y_scales, 1), (input_scales, 3), (second_rstd, 0), (expert_residual, 0)],
                before={-2: later_inputs})

            start = steps.total()
            with pool.Fori(0, NF) as g:
                steps.enter(start, g, 3)
                pool.wait_ge(var3_ready, did(g + 1))
                pool.wait_ge(yout_ready, did(g))
                settle()
                steps.link(pool.tensor_scalar(nm3[:, :], mv3[:, :, 0], -1.0, None, ALU.mult))
                steps.link(pool.tensor_tensor(rstd3[:, :], mv3[:, :, 1], eps5[:, :], ALU.add))
                steps.link(pool.tensor_tensor(rstd3[:, :], rstd3[:, :], neg_half4[:, :], ALU.pow))
                pool.tensor_tensor(nm3[:, :], nm3[:, :], rstd3[:, :], ALU.mult).then_inc(rstd3_ready, 1)
                steps.leave(start, NF, 3)

        @block.scalar
        def _(act):
            steps = Steps(act, act_steps)
            act.dma_start(R[:, :], rpack.rearrange("(a n) -> a n", a=1).to_broadcast([128, NROW])).then_inc(r_in, 16)
            act.dma_start(C[:, 0:C_FIRST], cpack[:, 0:C_FIRST]).then_inc(c_in, 16)
            act.dma_start(C[:, C_FIRST:NCST], cpack[:, C_FIRST:NCST]).then_inc(c2_in, 16)
            act.wait_ge(c_in, 16)
            act.activation(ident_bf[:, :], ident, ACT.Copy).then_inc(ident_ready, 1)
            act.wait_ge(r_in, 16)
            act.activation(a_exp[:, :], r("A_log"), ACT.Exp).then_inc(aexp_ready, 1)

            def mean_square(g):
                act.wait_ge(fx_ready, did(g))
                act.wait_ge(ms_ready, did(GB * g))
                for j in range(GB):
                    act.activation(junk[:, j, :], x_all[:, batch(g, j), :], ACT.Square, scale=float(D ** -0.5),
                                   accum_out=ms_x[:, j:j + 1]).then_inc(ms_ready, 1)

            def quantise(g):
                act.wait_ge(fx_ready, did(g + 1))
                act.wait_ge(q_ready, did(g))
                for j in range(GB):
                    act.activation(qm[:, j, :], uc[:, j, :], ACT.Identity, bias=magic_bias[:, 0:1],
                                   scale=f_x[:, j:j + 1]).then_inc(qm_ready, 1)

            def evacuate_q(g):
                act.wait_ge(q_psum, did(g + 1))
                act.wait_ge(zd_psum, did(GB * g))
                act.wait_ge(xs_ready, did(2 * g))
                act.activation(s_row[:, :], bank[0][:, 0:T], ACT.Copy)
                act.activation(qT[:, :], bank[0][:, T:T + T // 2].bitcast(BF16), ACT.Copy).then_inc(qt_ready, 1)

            def first_tap(g):
                act.wait_ge(silu_ready, did(2 * g))
                for c in (2, 3, 0):
                    act.wait_ge(xs_ready, did(2 * g + c // 2 + 1))
                    act.activation(acc[:, c, :, :], xs[:, c, :, TAPS - 1:], ACT.Identity,
                                   bias=w("conv_b")[:, c:c + 1],
                                   scale=w("conv_w")[:, c * TAPS + TAPS - 1:c * TAPS + TAPS]).then_inc(tap0_ready, 1)

            def gates(g):
                act.wait_ge(v_ready, did(g))
                for j in range(GB):
                    act.wait_ge(zd_psum, did(GB * g + j + 1))
                    act.activation(z_tok[:, batch(g, j), :], bank[j][:, 0:DI], ACT.Silu, scale=s_x[:, j:j + 1])
                    act.activation(dt_raw[:, j, :], bank[j][:, DI:DI + NH], ACT.Identity,
                                   scale=s_x[:, j:j + 1]).then_inc(zd_ready, 1)

            def silu_xbc(g):
                act.wait_ge(g_psum, did(g))
                act.wait_ge(xt_psum, did(g))
                for i in (1, 0):
                    act.wait_ge(conv_ready, did(NC * g + NC // 2 * (2 - i)))
                    act.activation(xbc[:, 2 * i:2 * i + 2, :, :], acc[:, 2 * i:2 * i + 2, :, :],
                                   ACT.Silu).then_inc(silu_ready, 1)

            def evacuate_x(g):
                act.wait_ge(xt_psum, did(g + 1))
                act.activation(x_tok[:, group(g), :], bank[1][:, :].rearrange("p (b c) -> p b c", b=GB),
                               ACT.Copy).then_inc(xtok_ready, 1)

            def softplus_log(g):
                act.wait_ge(v_ready, did(g + 1))
                act.wait_ge(dt_ready, did(g))
                steps.link(act.activation(e_dt[:, :], na_dt[:, :], ACT.Exp))
                act.activation(l_dt[:, :], e_dt[:, :], ACT.Ln, bias=ones[:, 0:1]).then_inc(l_ready, 1)

            def silus(g):
                act.preload_act_table(ACT.Silu)
                gates(g)
                silu_xbc(g)
                act.preload_act_table_set("natural_log_exp_and_others")

            def decays(g):
                act.wait_ge(y_psum, did(g))
                for j in range(GB):
                    act.wait_ge(ss_psum, did(GB * g + j + 1))
                    act.activation(ex[:, j].rearrange("p h l -> p (h l)"), bank[3 + j][:, :], ACT.Exp).then_inc(ex_ready, 1)

            def y_square(g):
                act.wait_ge(fy_ready, did(g))
                act.wait_ge(msy_ready, did(GB * g))
                act.wait_ge(y_ready, did(g + 1))
                for j in range(GB):
                    act.activation(junk_y[:, j, :], y[:, j, :], ACT.Square, scale=float(DI ** -0.5),
                                   accum_out=ms_y[:, j:j + 1]).then_inc(msy_ready, 1)

            def y_quantise(g):
                act.wait_ge(fy_ready, did(g + 1))
                act.wait_ge(yq_ready, did(g))
                for j in range(GB):
                    act.activation(y_qm[:, j, :], y_c[:, j, :], ACT.Identity, bias=magic_bias[:, 0:1],
                                   scale=f_y[:, j:j + 1]).then_inc(yqm_ready, 1)

            def y_evacuate(g):
                act.wait_ge(yqt_psum, did(g + 1))
                act.wait_ge(proj_psum, did(g))
                act.activation(y_qT[:, :, :, :].rearrange("p b c l -> p (b c l)"),
                               bank[4][:, 0:GB * DI // 2].bitcast(BF16), ACT.Copy).then_inc(yqt_ready, 1)

            def x1_evacuate(g):
                act.wait_ge(x1t_psum, did(g + 1))
                act.wait_ge(vvc_psum, did(g))
                act.wait_ge(s2_psum, did(g))
                act.activation(x1T[:, :, :].rearrange("p b l -> p (b l)"), bank[4][:, 0:T], ACT.Copy).then_inc(x1t_ready, 1)

            def context_keys(g):
                act.wait_ge(p_psum, did(g + 1))
                act.wait_ge(s2_psum, did(g))
                act.activation(p1[:, :], bank[5][:, 0:TS], ACT.Identity, bias=vec[:, 0:1], scale=INV_SQRT_D)
                act.activation(p2[:, :], bank[5][:, TS:2 * TS], ACT.Identity, bias=vec[:, 1:2],
                               scale=INV_SQRT_D).then_inc(p_ready, 1)

            def context_values(g):
                act.wait_ge(vvs_psum, did(g + 1))
                act.wait_ge(o_psum, did(GB * g))
                act.activation(vvs[0:LS, :, 0:256], bank[6][0:LS, :].rearrange("p (b c) -> p b c", b=GB),
                               ACT.Copy).then_inc(vvs_ready, 1)

            def first_exps(g):
                act.wait_ge(nmx1_ready, did(g + 1))
                act.wait_ge(e1n_ready, did(g))
                for j in range(GB):
                    act.activation(e1[:, j, :], bank[7][:, j * LS:(j + 1) * LS], ACT.Exp, bias=nmx1[:, j:j + 1],
                                   accum_out=den1[:, j:j + 1]).then_inc(e1_ready, 1)

            def second_exps(g):
                act.wait_ge(nmx2_ready, did(g + 1))
                act.wait_ge(w2i_psum, did(g))
                act.wait_ge(ipn_ready, did(g))
                for j in range(GB):
                    act.activation(e2[:, j, :], bank[5][0:LS, j * L:(j + 1) * L], ACT.Exp, bias=nmx2[:, j:j + 1],
                                   accum_out=den2[:, j:j + 1]).then_inc(e2_ready, 1)

            def token_values(g):
                act.wait_ge(vvc_psum, did(g + 1))
                act.wait_ge(o_psum, did(GB * g))
                act.activation(vvc[:, :, :].rearrange("p b c -> p (b c)"), bank[6][:, :], ACT.Copy).then_inc(vvc_ready, 1)

            def evacuate_e1(g):
                act.wait_ge(e1t_psum, did(g + 1))
                act.wait_ge(o_psum, did(GB * g))
                act.activation(e1T[:, :, :].rearrange("p b l -> p (b l)"), bank[7][0:KR, 0:T], ACT.Copy).then_inc(e1t_ready, 1)

            def evacuate_w2(g):
                act.wait_ge(w2i_psum, did(g + 1))
                act.wait_ge(o_psum, did(GB * g))
                act.activation(w2i[:, :, :].rearrange("p b l -> p (b l)"), bank[5][:, 0:T], ACT.Copy).then_inc(w2i_ready, 1)

            def mixed(g):
                act.wait_ge(dif_part, did(GB * g))
                act.wait_ge(rs_ready, did(g))
                act.wait_ge(res2_ready, did(g))
                for j in range(GB):
                    act.wait_ge(o_psum, did(GB * g + j + 1))
                    at = steps.mark(act.activation(eg[:, j, :], bank[6 + j][:, 128:256], ACT.Exp, scale=-1.0))
                    act.activation(s2c[:, j, :], bank[6 + j][:, 256:384], ACT.Copy).then_inc(s2c_ready, 1)
                steps.wait(at)
                steps.link(act.activation(eg[:, :, :], eg[:, :, :], ACT.Ln, bias=ones[:, 0:1]))
                act.activation(gt[:, :, :], eg[:, :, :], ACT.Exp, scale=-1.0).then_inc(gt_att_ready, 1)

            def x2_evacuate(g):
                act.wait_ge(x2t_psum, did(g + 1))
                act.wait_ge(logit_psum, did(g))
                act.activation(x2T_s[:, :, :].rearrange("p b l -> p (b l)"), bank[5][:, 0:T], ACT.Copy).then_inc(x2t_ready, 1)
                act.activation(x2T[:, bass.ds(g * T, T)], bank[5][:, 0:T], ACT.Copy).then_inc(x2t_ready, 1)

            def router_scores(b0, b1):
                act.wait_ge(logit_ready, did((b1 - 1) // GB + 1))
                act.activation(router_bufs[0][:, b0:b1, :], logit[:, b0:b1, :], ACT.Exp, scale=-1.0).then_inc(score_ready, 1)

            act.preload_act_table_set("natural_log_exp_and_others")
            act.wait_ge(magic_ready, 1)
            act.wait_ge(x0_in, 16)
            act.wait_ge(w_in, 16)
            act.wait_ge(consts_ready, N_CONSTS)

            def later_inputs():
                act.wait_ge(x_in, 16 * 3)
                act.wait_ge(c2_in, 16)
                act.activation(sel_bf[:, :], c_("sel", 3 * E), ACT.Copy).then_inc(sel_ready, 1)

            main_loop(act, steps, [
                (evacuate_q, 2), (context_keys, 0), (x1_evacuate, 0), (decays, 1), (context_values, 0),
                (second_exps, 0), (mean_square, 3), (first_exps, 0), (first_tap, 2), (token_values, 0),
                (evacuate_w2, 0), (evacuate_e1, 0), (y_square, 1), (mixed, 0), (silus, 2), (y_quantise, 1),
                (quantise, 3), (y_evacuate, 1), (softplus_log, 2), (x2_evacuate, 0), (evacuate_x, 2)],
                before={-2: later_inputs},
                last_extras=[lambda: router_scores(0, NB - FB)])

            router_scores(NB - FB, NB)

            act.preload_act_table(ACT.Gelu)

            def gates_to_rows(i):
                act.wait_ge(gt_psum, did(i + 1))
                act.activation(gT[:, i * FT:(i + 1) * FT], bank[4 + i][0:3 * E, :], ACT.Copy).then_inc(gt_ready, 1)

            def hidden(g, t):
                act.wait_ge(h_psum, did(NT * g + t + 1))
                act.activation(hid[:, t, :], bank[t % 2][:, :], ACT.Gelu, bias=w("b1")[:, t:t + 1]).then_inc(hid_ready, 1)

            def hidden_shared(g):
                act.wait_ge(h_psum, did(NT * (g + 1)))
                act.activation(hid_s[0:HID, :], bank[NE % 2][0:HID, :], ACT.Gelu, bias=w("bs1", HID)).then_inc(hs_ready, 1)
                act.wait_ge(gb_psum, did(NT * (g + 1)))
                act.activation(hid_s[HID:96, :], bank[2 + NE % 2][HID:96, :], ACT.Copy).then_inc(hs_ready, 1)

            def last_norm(g):
                act.wait_ge(rstd3_ready, did(g + 1))
                act.wait_ge(out_done, did(16 * g))
                for j in range(FB):
                    ins = act.activation(y_out[:, j, :], res3[:, j, :], ACT.Identity, bias=nm3[:, j:j + 1],
                                         scale=rstd3[:, j:j + 1])
                ins.then_inc(yout_ready, 1)

            for i in range(NF - 1):
                gates_to_rows(i)
            for t in range(NE):
                hidden(0, t)
            hidden_shared(0)
            with act.Fori(1, NF - 1) as g:
                for t in range(NE):
                    hidden(g, t)
                    if t == 2:
                        last_norm(g - 1)
                hidden_shared(g)
            gates_to_rows(NF - 1)
            for t in range(NE):
                hidden(NF - 1, t)
                if t == 2:
                    last_norm(NF - 2)
            hidden_shared(NF - 1)
            last_norm(NF - 1)

        @block.vector
        def _(dve):
            steps = Steps(dve, dve_steps)

            def settle():
                dve.sem_inc(dve_settled, 1)

            dve.memset(magic_bias[:, :], MAGIC).then_inc(magic_ready, 1)
            dve.wait_ge(w_in, 16)
            win, wout = w("win"), w("wout")
            dve.tensor_reduce(wsum[:, 0:1], win, AXIS.X, ALU.add, apply_absolute_value=True)
            dve.tensor_reduce(wsum[:, 1:2], wout, AXIS.X, ALU.add, apply_absolute_value=True).then_inc(wsum_ready, 1)
            dve.wait_ge(wsum_psum, 1)
            steps.link(dve.tensor_copy(wscale[:, 0:2], bank[7][:, 0:2]))
            steps.link(dve.tensor_scalar(wscale[:, 0:1], wscale[:, 0:1], 1.0 / (772 * D), 1e-5, ALU.mult, ALU.max))
            steps.link(dve.tensor_scalar(wscale[:, 1:2], wscale[:, 1:2], 1.0 / (DI * D), 1e-5, ALU.mult, ALU.max))
            steps.link(dve.tensor_scalar(wscale[:, 2:4], wscale[:, 0:2], -0.5, None, ALU.mult))
            steps.link(dve.tensor_scalar(wscale[:, 0:2], wscale[:, 0:2], 0.5, None, ALU.mult))
            steps.link(dve.tensor_scalar(low[:, :], win, wscale[:, 2:3], None, ALU.is_lt))
            steps.link(dve.scalar_tensor_tensor(win_q[:, :], win, wscale[:, 0:1], low[:, :], ALU.is_gt, ALU.subtract))
            steps.link(dve.tensor_scalar(low[:, 0:DI], wout, wscale[:, 3:4], None, ALU.is_lt))
            dve.scalar_tensor_tensor(wout_q[:, :, :].rearrange("p a b -> p (a b)"), wout, wscale[:, 1:2],
                                     low[:, 0:DI], ALU.is_gt, ALU.subtract).then_inc(win_ready, 1)

            dve.wait_ge(r_in, 16)
            dve.wait_ge(c_in, 16)
            dve.wait_ge(consts_ready, N_CONSTS)

            def attention_weights_start():
                dve.wait_ge(c2_in, 16)
                dve.wait_ge(w2_in, 16)
                dve.wait_ge(consts_ready, N_CONSTS)
                dve.tensor_copy(bcol[:, 0, BIAS:KR], w("bv_s"))
                dve.tensor_copy(bcol[:, 1, BIAS:KR], w("bv_c"))
                dve.tensor_scalar(bq_all[:, 0, :], ones[:, :], w("bq_c"), None, ALU.mult)
                dve.tensor_scalar(bq_all[:, 1, :], ones[:, :], w("bq_s"), None, ALU.mult).then_inc(bcol_ready, 1)

            def attention_weights_end():
                dve.wait_ge(a_psum, 1)
                dve.tensor_copy(a1T[:, :], bank[5][:, 0:128])
                dve.tensor_copy(a2T[:, :], bank[5][:, 128:256])
                dve.tensor_copy(wvs[:, 128:256], bank[5][:, 256:384])
                dve.tensor_copy(wvc[:, 0:128], bank[5][:, 384:512])
                dve.tensor_copy(wvs[:, 0:128], w("wv_sT"))
                dve.tensor_copy(wvc[:, 128:256], w("wv_cT"))
                steps.link(dve.tensor_scalar(vec[:, :], bank[7][:, 0:6], INV_SQRT_D, None, ALU.mult))
                dve.tensor_copy(cvec2[:, :], bank[7][:, 3:4])
                dve.tensor_scalar(cv1[:, :], ones[:, :], vec[:, 2:3], None, ALU.mult)
                for j in range(GB):
                    steps.link(dve.tensor_copy(vvs[BIAS:KR, j, :], bank[6][BIAS:KR, 0:384]))
                    ins = dve.tensor_tensor(vvs[BIAS:KR, j, 128:256], bank[6][BIAS:KR, 128:256], R[BIAS:KR, ROW["bg"][0]:ROW["bg"][1]],
                                            ALU.add)
                ins.then_inc(attw_ready, 1)

            def moments(src, stats_to, mv_to, n):
                for j in range(n):
                    at = steps.mark(dve.bn_stats(stats_to[:, j, :], src[:, j, :]))
                steps.wait(at)
                settle()
                for j in range(n):
                    ins = dve.bn_aggr(mv_to[:, j, :], stats_to[:, j, :])
                return ins

            def centred(dst, src, mv_of):
                for j in range(GB):
                    at = steps.mark(dve.tensor_scalar(dst[:, j, :], src[:, j, :], mv_of[:, j, 0:1], None, ALU.subtract))
                steps.wait(at)

            def input_stats(g):
                dve.wait_ge(u_ready, did(g + 1))
                dve.wait_ge(fx_ready, did(g))
                dve.wait_ge(qm_ready, did(GB * g))
                steps.link(moments(u, stats, mv_u, GB))
                centred(uc, u, mv_u)
                dve.tensor_reduce(amax_u[:, :], uc[:, :, :], AXIS.X, ALU.max,
                                  apply_absolute_value=True).then_inc(amax_ready, 1)

            def step_diagonal(g):
                dve.wait_ge(fx_ready, did(g + 1))
                dve.wait_ge(q_psum, did(g))
                for j in range(GB):
                    ins = dve.tensor_scalar(diag[:, j, :], ident, s_x[:, j:j + 1], None, ALU.mult)
                ins.then_inc(diag_ready, 1)

            def round_q(g):
                dve.wait_ge(q_psum, did(g))
                dve.wait_ge(qm_ready, did(GB * (g + 1)))
                dve.tensor_scalar(q_bf[:, :, :], qm[:, :, :], MAGIC, None, ALU.subtract).then_inc(q_ready, 1)

            def conv(g):
                dve.wait_ge(qt_ready, did(g + 1))
                dve.wait_ge(tap0_ready, did(3 * g))
                dve.wait_ge(tap0_pool, did(g))
                dve.wait_ge(conv_ready, did(NC * g))
                for i in range(2):
                    dve.wait_ge(zx_psum, did(2 * g + i + 1))
                    dve.tensor_tensor(xs[:, 2 * i:2 * i + 2, :, TAPS - 1:],
                                      bank[i][:, :].rearrange("p (c b l) -> p c b l", c=2, b=GB),
                                      s_row[:, :].rearrange("p (b l) -> p b l", b=GB).unsqueeze(1)
                                      .to_broadcast([128, 2, GB, L]), ALU.mult).then_inc(xs_ready, 1)

            def taps(g, tiles):
                done = [0] * NC
                for k in range(TAPS - 2, -1, -1):
                    for c in tiles:
                        if k == TAPS - 2 and c == 1:
                            dve.wait_ge(tap0_pool, did(g + 1))
                        elif k == TAPS - 2:
                            dve.wait_ge(tap0_ready, did(3 * g + (2, 3, 0).index(c) + 1))
                        else:
                            steps.wait(done[c])
                        ins = dve.scalar_tensor_tensor(acc[:, c, :, :], xs[:, c, :, k:k + L],
                                                       w("conv_w")[:, c * TAPS + k:c * TAPS + k + 1],
                                                       acc[:, c, :, :], ALU.mult, ALU.add)
                        if k:
                            done[c] = steps.mark(ins)
                        else:
                            ins.then_inc(conv_ready, 1)

            def taps_bc(g):
                taps(g, (2, 3))

            def taps_x(g):
                taps(g, (0, 1))

            def mask_g(g):
                dve.wait_ge(g_psum, did(g + 1))
                dve.tensor_tensor(g_all[:, group(g), :], bank[0][:, 0:T].rearrange("p (b l) -> p b l", b=GB),
                                  upto.unsqueeze(1).to_broadcast([128, GB, L]), ALU.mult).then_inc(g_ready, 1)

            def softplus_start(g):
                dve.wait_ge(dt_ready, did(g))
                dve.wait_ge(zd_ready, did(GB * (g + 1)))
                dve.wait_ge(l_ready, did(g))
                steps.link(dve.tensor_tensor(v_dt[:, :].rearrange("p (b h) -> p b h", h=NH), dt_raw[:, :, :],
                                             r("dt_bias").unsqueeze(1).to_broadcast([128, GB, NH]), ALU.add))
                dve.scalar_tensor_tensor(na_dt[:, :], v_dt[:, :], -1.0, v_dt[:, :], ALU.mult, ALU.min).then_inc(v_ready, 1)

            def softplus_end(g):
                dve.wait_ge(l_ready, did(g + 1))
                steps.link(dve.scalar_tensor_tensor(dt_sp[:, group(g), :].rearrange("p b h -> p (b h)"), v_dt[:, :], 0.0,
                                                    l_dt[:, :], ALU.max, ALU.add))
                dve.scalar_tensor_tensor(a_dt[:, group(g), :], dt_sp[:, group(g), :], -1.0,
                                         a_exp[:, :].unsqueeze(1).to_broadcast([128, GB, NH]),
                                         ALU.mult, ALU.mult).then_inc(dt_ready, 1)

            def decay_gram(g):
                dve.wait_ge(g_ready, did(g + 1))
                for j in range(GB):
                    dve.wait_ge(ex_ready, did(GB * g + j + 1))
                    dve.tensor_tensor(ex[:, j], ex[:, j], g_all[:, batch(g, j), :].to_broadcast([128, NH, L]),
                                      ALU.mult).then_inc(m_ready, 1)

            def gate_y(g):
                dve.wait_ge(y_psum, did(g + 1))
                dve.wait_ge(yw_ready, did(g))
                dve.wait_ge(msy_ready, did(GB * g))
                dve.tensor_tensor(y[:, :, :], bank[3][:, :].rearrange("p (b c) -> p b c", b=GB),
                                  z_tok[:, group(g), :], ALU.mult).then_inc(y_ready, 1)

            def y_stats(g):
                dve.wait_ge(yw_ready, did(g + 1))
                dve.wait_ge(fy_ready, did(g))
                dve.wait_ge(yqm_ready, did(GB * g))
                steps.link(moments(y_w, stats_y, mv_y, GB))
                centred(y_c, y_w, mv_y)
                dve.tensor_reduce(amax_y[:, :], y_c[:, :, :], AXIS.X, ALU.max,
                                  apply_absolute_value=True).then_inc(amaxy_ready, 1)

            def y_round(g):
                dve.wait_ge(yqm_ready, did(GB * (g + 1)))
                dve.wait_ge(yqt_psum, did(g))
                dve.tensor_scalar(y_q[:, :, :], y_qm[:, :, :], MAGIC, None, ALU.subtract).then_inc(yq_ready, 1)

            def first_residual(g):
                dve.wait_ge(proj_psum, did(g + 1))
                dve.wait_ge(x1s_ready, did(g))
                for j in range(GB):
                    at = steps.mark(dve.scalar_tensor_tensor(res1[:, j, :], bank[3][:, j * D:(j + 1) * D],
                                                             s_y_half[:, j:j + 1],
                                                             x_all[:, batch(g, j), :].rearrange("p a d -> p (a d)"),
                                                             ALU.mult, ALU.add))
                steps.wait(at)
                moments(res1, stats1, mv1, GB).then_inc(var1_ready, 1)

            def first_norm(g):
                dve.wait_ge(rstd1_ready, did(g + 1))
                dve.wait_ge(x1t_psum, did(g))
                for j in range(GB):
                    ins = dve.tensor_scalar(x1_s[:, j, :], res1[:, j, :], mv1[:, j, 0:1], rstd1[:, j:j + 1],
                                            ALU.subtract, ALU.mult)
                ins.then_inc(x1s_ready, 1)

            def keep_x1(g):
                dve.wait_ge(x1s_ready, did(g + 1))
                dve.tensor_copy(x1[:, group(g), :], x1_s[:, :, :]).then_inc(x1_ready, 1)

            def first_max(g):
                dve.wait_ge(s1_psum, did(g + 1))
                dve.wait_ge(e1_ready, did(GB * g))
                steps.link(dve.tensor_reduce(nmx1[:, :], bank[7][:, 0:TS].rearrange("p (b k) -> p b k", b=GB), AXIS.X,
                                             ALU.max, negate=True))
                dve.tensor_scalar(nmx1[:, :], nmx1[:, :], vec[:, 4:5], vec[:, 4:5], ALU.subtract,
                                  ALU.add).then_inc(nmx1_ready, 1)

            def second_max(g):
                dve.wait_ge(s2_psum, did(g + 1))
                dve.wait_ge(e2_ready, did(GB * g))
                dve.tensor_scalar(shift2[:, :], bank[5][0:LS, T:T + GB], INV_SQRT_D, vec[0:LS, 5:6], ALU.mult, ALU.add)
                steps.link(dve.tensor_reduce(mx2[:, :], bank[5][0:LS, 0:T].rearrange("p (b k) -> p b k", b=GB), AXIS.X,
                                             ALU.max))
                steps.link(dve.tensor_tensor(mx2[:, :], mx2[:, :], shift2[:, :], ALU.add))
                dve.tensor_tensor(nmx2[:, :], shift2[:, :], mx2[:, :], ALU.subtract).then_inc(nmx2_ready, 1)

            def first_weights(g):
                dve.wait_ge(e1_ready, did(GB * (g + 1)))
                dve.wait_ge(e1t_psum, did(g))
                steps.link(dve.reciprocal(rden1[:, :], den1[:, :]))
                dve.tensor_tensor(e1n[:, :, 0:LS], e1[:, :, :], rden1[:, :].unsqueeze(2).to_broadcast([128, GB, LS]),
                                  ALU.mult).then_inc(e1n_ready, 1)

            def second_weights(g):
                dve.wait_ge(e2_ready, did(GB * (g + 1)))
                dve.wait_ge(w2i_psum, did(g))
                steps.link(dve.reciprocal(rden2[:, :], den2[:, :]))
                for j in range(GB):
                    ins = dve.tensor_scalar(ipn[:, j, :], c_("interp", LS), rden2[:, j:j + 1], None, ALU.mult)
                ins.then_inc(ipn_ready, 1)

            def difference(g):
                dve.wait_ge(res2_ready, did(g))
                for j in range(GB):
                    dve.wait_ge(s2c_ready, did(GB * g + j + 1))
                    dve.tensor_tensor(dif[:, j, :], bank[6 + j][:, 0:D], s2c[:, j, :], ALU.subtract).then_inc(dif_part, 1)

            def blend(g):
                dve.wait_ge(dif_part, did(GB * (g + 1)))
                dve.wait_ge(gt_att_ready, did(g + 1))
                steps.link(dve.tensor_tensor(dif[:, :, :], dif[:, :, :], gt[:, :, :], ALU.mult))
                dve.wait_ge(rs_ready, did(g + 1))
                dve.wait_ge(x2_ready, did(g))
                dve.tensor_tensor(res2[:, :, :], dif[:, :, :], s2c_x1[:, :, :], ALU.add).then_inc(res2_ready, 1)

            def second_moments(g):
                dve.wait_ge(res2_ready, did(g + 1))
                moments(res2, stats2, mv2, GB).then_inc(var2_ready, 1)

            def second_norm(g):
                dve.wait_ge(rstd2_ready, did(g + 1))
                dve.wait_ge(x2t_psum, did(g))
                dve.wait_ge(x2b_ready, did(g))
                for j in range(GB):
                    ins = dve.tensor_scalar(x2_s[:, j, :], res2[:, j, :], mv2[:, j, 0:1], rstd2[:, j:j + 1],
                                            ALU.subtract, ALU.mult)
                ins.then_inc(x2_ready, 1)

            def router_logits(g):
                dve.wait_ge(logit_psum, did(g + 1))
                dve.tensor_copy(logit[:, group(g), :], bank[6][:, 0:GB * E].rearrange("p (b e) -> p b e", e=E))\
                   .then_inc(logit_ready, 1)

            def router(i, b0, b1):
                n = b1 - b0
                score, top, first, rest, pick, second = (v[:, b0:b1, :] for v in router_bufs)
                largest1, largest2, largest_prio = (v[:, b0:b1] for v in (max1, max2, prio1))
                bc = lambda v: v.unsqueeze(2).to_broadcast([128, n, E])
                prio = c_("prio").unsqueeze(1).to_broadcast([128, n, E])
                gates = gate3[:, b0:b1, :]

                def do(ins_of):
                    return lambda: steps.link(ins_of())

                def pick_largest(src, largest, mask):
                    return [do(lambda: dve.tensor_reduce(largest, src, AXIS.X, ALU.max)),
                            do(lambda: dve.tensor_tensor(pick, src, bc(largest), ALU.is_equal)),
                            do(lambda: dve.tensor_tensor(pick, pick, prio, ALU.mult)),
                            do(lambda: dve.tensor_reduce(largest_prio, pick, AXIS.X, ALU.max)),
                            do(lambda: dve.tensor_tensor(mask, pick, bc(largest_prio), ALU.is_equal))]

                def begin():
                    dve.wait_ge(score_ready, i + 1)
                    steps.link(dve.tensor_scalar(score, score, 1.0, None, ALU.add))

                return [
                    begin,
                    do(lambda: dve.reciprocal(score, score)),
                    do(lambda: dve.tensor_scalar(score, score, r("route_scale"), None, ALU.mult)),
                    *pick_largest(score, largest1, first),
                    do(lambda: dve.scalar_tensor_tensor(rest, first, -3.0e38, score, ALU.mult, ALU.add)),
                    *pick_largest(rest, largest2, second),
                    do(lambda: dve.tensor_tensor(first, first, second, ALU.add)),
                    do(lambda: dve.tensor_tensor(largest1, largest1, largest2, ALU.add)),
                    do(lambda: dve.reciprocal(largest2, largest1)),
                    do(lambda: dve.tensor_tensor(first, first, score, ALU.mult)),
                    do(lambda: dve.tensor_tensor(top, first, bc(largest2), ALU.mult)),
                    do(lambda: dve.tensor_copy(gates[:, :, 0:E], top)),
                    do(lambda: dve.tensor_tensor(rest, top, gates[:, :, 0:E], ALU.subtract)),
                    do(lambda: dve.tensor_copy(gates[:, :, E:2 * E], rest)),
                    do(lambda: dve.tensor_tensor(pick, rest, gates[:, :, E:2 * E], ALU.subtract)),
                    lambda: dve.tensor_copy(gates[:, :, 2 * E:3 * E], pick).then_inc(gate_ready, 1)]

            def dve_main_end():
                for piece in router(1, NB - FB, NB):
                    piece()

            dve.wait_ge(aexp_ready, 1)
            main_loop(dve, steps, [
                (first_norm, 0), (input_stats, 3), (conv, 2), (second_max, 0), (decay_gram, 1), (first_max, 0),
                (keep_x1, 0), (second_weights, 0), (first_weights, 0), (gate_y, 1), (taps_bc, 2), (y_stats, 1),
                (difference, 0), (taps_x, 2), (blend, 0), (second_moments, 0), (mask_g, 2), (softplus_start, 2),
                (y_round, 1), (step_diagonal, 3), (round_q, 3), (second_norm, 0), (first_residual, 1),
                (router_logits, 0), (softplus_end, 2)],
                before={-2: attention_weights_start, -1: attention_weights_end},
                last_extras=router(0, 0, NB - FB))

            dve_main_end()

            def gate_hidden(g):
                for t in range(NE):
                    dve.wait_ge(hid_ready, did(NE * g + t + 1))
                    dve.wait_ge(gb_psum, did(NT * g + t + 1))
                    dve.tensor_tensor(hid[:, t, :], hid[:, t, :], bank[2 + t % 2][:, :], ALU.mult).then_inc(hg_ready, 1)

            def residual(g):
                dve.wait_ge(moe_psum, did(g + 1))
                dve.wait_ge(yout_ready, did(g))
                for j in range(FB):
                    at = steps.mark(dve.tensor_tensor(res3[:, j:j + 1, :],
                                                      bank[4 + j][:, 0:D].rearrange("p (a d) -> p a d", a=1),
                                                      x2b[:, bass.ds(g * FB + j, 1), :], ALU.add))
                steps.wait(at)
                dve.sem_inc(res3_ready, 1)
                moments(res3, stats3, mv3, FB).then_inc(var3_ready, 1)

            gate_hidden(0)
            start = steps.total()
            with dve.Fori(1, NF) as g:
                steps.enter(start, g - 1, 2 * FB)
                residual(g - 1)
                gate_hidden(g)
                steps.leave(start, NF - 1, 2 * FB)
            residual(NF - 1)

        @block.tensor
        def _(pe):
            pe.wait_ge(consts_ready, N_CONSTS)
            pe.wait_ge(wsum_ready, 1)
            pe.matmul(bank[7][:, 0:2], ones[:, :], wsum[:, :], start=True, stop=True).then_inc(wsum_psum, 1)

            def attention_weights():
                pe.wait_ge(w2_in, 16)
                pe.wait_ge(c_in, 16)
                for at, lhs, rhs in ((0, w("wk_s"), w("wq_c")), (128, w("wq_s"), w("wk_c")),
                                     (256, w("wv_s"), w("wgT")[:, 0:128]), (384, w("wv_c"), w("wgT")[:, 128:256])):
                    pe.matmul(bank[5][:, at:at + 128], lhs, rhs, start=True, stop=True)
                pe.wait_ge(bcol_ready, 1)
                for at, lhs, rhs in ((0, w("wq_c"), w("bk_s")), (1, w("wk_c"), w("bq_s")),
                                     (2, w("wk_s"), w("bq_c")), (3, w("wq_s"), w("bk_c")),
                                     (4, bq_all[:, 0, :], w("bk_s")), (5, bq_all[:, 1, :], w("bk_c"))):
                    pe.matmul(bank[7][:, at:at + 1], lhs, rhs, start=True, stop=True)
                pe.matmul(bank[6][:, 0:128], bcol[:, 0, :], ident, start=True, stop=True)
                pe.matmul(bank[6][:, 256:384], bcol[:, 1, :], ident, start=True, stop=True)
                pe.matmul(bank[6][:, 128:256], bcol[:, 0, :], w("wgT")[:, 0:128], start=True, stop=False)
                pe.matmul(bank[6][:, 128:256], bcol[:, 1, :], w("wgT")[:, 128:256], start=False, stop=True).then_inc(a_psum, 1)

            def attention_weights_there():
                pe.wait_ge(attw_ready, 1)

            def keep_warm(g):
                for _ in range(2):
                    pe.matmul(bank[2][:, :], ident_bf[:, :], win_q[:, 0:512], start=True, stop=True)

            def transpose_q(g):
                pe.wait_ge(diag_ready, did(g + 1))
                pe.wait_ge(q_ready, did(g + 1))
                pe.wait_ge(g_ready, did(g))
                pe.matmul(bank[0][:, 0:T], ones[:, :], diag[:, :, :].rearrange("p b l -> p (b l)"), start=True, stop=True)
                for j in range(GB):
                    ins = pe.transpose(bank[0][:, T + j * 64:T + (j + 1) * 64].bitcast(BF16), q_bf[:, j, :], ident_bf[:, :])
                ins.then_inc(q_psum, 1)

            def project(g):
                pe.wait_ge(qt_ready, did(g + 1))
                pe.wait_ge(g_ready, did(g))
                pe.wait_ge(xtok_ready, did(g))
                for c in range(NC):
                    ins = pe.matmul(bank[c // 2][:, c % 2 * T:(c % 2 + 1) * T], win_q[:, c * 128:(c + 1) * 128], qT[:, :],
                                    start=True, stop=True)
                    if c % 2:
                        ins.then_inc(zx_psum, 1)

            def project_gates(g):
                for j in range(GB):
                    pe.wait_ge(xs_ready, did(2 * g + j + 1))
                    pe.matmul(bank[j][:, 0:DI + NH], qT[:, j * L:(j + 1) * L], win_q[:, 512:772],
                              start=True, stop=True).then_inc(zd_psum, 1)

            def gram(g):
                pe.wait_ge(zd_ready, did(GB * (g + 1)))
                pe.wait_ge(silu_ready, did(2 * g + 1))
                for j in range(GB):
                    ins = pe.matmul(bank[0][:, j * L:(j + 1) * L], xbc[:, 2, j, :], xbc[:, 3, j, :], start=True, stop=True)
                ins.then_inc(g_psum, 1)

            def transpose_xc(g):
                pe.wait_ge(zd_ready, did(GB * (g + 1)))
                pe.wait_ge(silu_ready, did(2 * g + 2))
                for j in range(GB):
                    for c in range(2):
                        ins = pe.transpose(bank[1][:, j * DI + c * 128:j * DI + (c + 1) * 128], xbc[:, c, j, :], ident)
                ins.then_inc(xt_psum, 1)

            def log_decays(g):
                pe.wait_ge(var1_ready, did(g))
                pe.wait_ge(x1t_ready, did(g))
                for j in range(GB):
                    pe.wait_ge(seg_ready, did(GB * g + j + 1))
                    pe.matmul(bank[3 + j][:, :], after, seg[:, j].rearrange("p h l -> p (h l)"),
                              start=True, stop=True).then_inc(ss_psum, 1)

            def scan_out(g):
                for j in range(GB):
                    pe.wait_ge(xd_ready, did(GB * g + j + 1))
                    pe.wait_ge(m_ready, did(GB * g + j + 1))
                    pe.matmul(bank[3][:, j * DI:(j + 1) * DI], ident, x_d[:, j, :], start=True, stop=False)
                    pe.wait_ge(udt_ready, did(GB * g + j + 1))
                    for h in range(NH):
                        o = bank[3][:, j * DI + h * HD:j * DI + (h + 1) * HD]
                        ins = pe.matmul(o, ex[:, j, h, :], u_dt[:, j, h * HD:(h + 1) * HD],
                                        start=False, stop=h == NH - 1)
                ins.then_inc(y_psum, 1)

            def transpose_y(g):
                pe.wait_ge(yq_ready, did(g + 1))
                for j in range(GB):
                    for c in range(2):
                        ins = pe.transpose(bank[4][:, (2 * j + c) * 64:(2 * j + c + 1) * 64].bitcast(BF16),
                                           y_q[:, j, c * 128:(c + 1) * 128], ident_bf[:, :])
                ins.then_inc(yqt_psum, 1)

            def project_out(g):
                pe.wait_ge(yqt_ready, did(g + 1))
                for j in range(GB):
                    for c in range(2):
                        ins = pe.matmul(bank[3][:, j * D:(j + 1) * D], y_qT[:, j, c, :], wout_q[:, c, :],
                                        start=c == 0, stop=c == 1)
                ins.then_inc(proj_psum, 1)

            def transpose_x1(g):
                pe.wait_ge(x1s_ready, did(g + 1))
                for j in range(GB):
                    ins = pe.transpose(bank[4][:, j * L:(j + 1) * L], x1_s[:, j, :], ident)
                ins.then_inc(x1t_psum, 1)

            def context_keys(g):
                pe.wait_ge(ctx_in, 16 * (g + 1))
                pe.wait_ge(x2t_ready, did(2 * g))
                pe.matmul(bank[5][:, 0:TS], a1T[:, :], ctx_s[:, :], start=True, stop=True)
                pe.matmul(bank[5][:, TS:2 * TS], a2T[:, :], ctx_s[:, :], start=True, stop=True).then_inc(p_psum, 1)

            def context_values(g):
                pe.wait_ge(ctx_in, 16 * (g + 1))
                pe.wait_ge(logit_ready, did(g))
                for j in range(GB):
                    ins = pe.matmul(bank[6][0:LS, j * 256:(j + 1) * 256], ctx_s[:, j * LS:(j + 1) * LS], wvs[:, :],
                                    start=True, stop=True)
                ins.then_inc(vvs_psum, 1)

            def first_scores(g):
                pe.wait_ge(p_ready, did(g + 1))
                pe.wait_ge(x1t_ready, did(g + 1))
                pe.wait_ge(dif_part, did(GB * g))
                for j in range(GB):
                    pe.matmul(bank[7][:, j * LS:(j + 1) * LS], cv1[:, :], ctx_s[:, j * LS:(j + 1) * LS],
                              start=True, stop=False)
                    ins = pe.matmul(bank[7][:, j * LS:(j + 1) * LS], x1T[:, j, :], p1[:, j * LS:(j + 1) * LS],
                                    start=False, stop=True)
                ins.then_inc(s1_psum, 1)

            def second_scores(g):
                pe.wait_ge(p_ready, did(g + 1))
                pe.wait_ge(x1t_ready, did(g + 1))
                for j in range(GB):
                    pe.matmul(bank[5][0:LS, T + j:T + j + 1], ctx_s[:, j * LS:(j + 1) * LS], cvec2[:, :],
                              start=True, stop=True)
                for j in range(GB):
                    ins = pe.matmul(bank[5][0:LS, j * L:(j + 1) * L], p2[:, j * LS:(j + 1) * LS], x1T[:, j, :],
                                    start=True, stop=True)
                ins.then_inc(s2_psum, 1)

            def token_products(g):
                pe.wait_ge(x1t_ready, did(g + 1))
                pe.wait_ge(vvs_ready, did(g + 1))
                for j in range(GB):
                    ins = pe.matmul(bank[6][:, j * 256:(j + 1) * 256], x1T[:, j, :], wvc[:, :], start=True, stop=True)
                ins.then_inc(vvc_psum, 1)

            def transpose_e1(g):
                pe.wait_ge(e1n_ready, did(g + 1))
                for j in range(GB):
                    ins = pe.transpose(bank[7][0:KR, j * L:(j + 1) * L], e1n[:, j, :], ident)
                ins.then_inc(e1t_psum, 1)

            def interpolate(g):
                pe.wait_ge(ipn_ready, did(g + 1))
                for j in range(GB):
                    ins = pe.matmul(bank[5][:, j * L:(j + 1) * L], e2[:, j, :], ipn[:, j, :], start=True, stop=True)
                ins.then_inc(w2i_psum, 1)

            def attend(g):
                pe.wait_ge(vvc_ready, did(g + 1))
                pe.wait_ge(e1t_ready, did(g + 1))
                pe.wait_ge(w2i_ready, did(g + 1))
                for j in range(GB):
                    b = bank[6 + j]
                    pe.matmul(b[:, 0:384], e1T[:, j, :], vvs[0:KR, j, :], start=True, stop=False)
                    pe.matmul(b[:, 128:384], w2i[:, j, :], vvc[:, j, :], start=False, stop=True).then_inc(o_psum, 1)

            def transpose_x2(g):
                pe.wait_ge(x2_ready, did(g + 1))
                for j in range(GB):
                    ins = pe.transpose(bank[5][:, j * L:(j + 1) * L], x2_s[:, j, :], ident)
                ins.then_inc(x2t_psum, 1)

            def router_logits(g):
                pe.wait_ge(x2t_ready, did(2 * g + 1))
                for j in range(GB):
                    ins = pe.matmul(bank[6][:, j * E:(j + 1) * E], x2T_s[:, j, :], w("gate_w"), start=True, stop=True)
                ins.then_inc(logit_psum, 1)

            pe.wait_ge(ident_ready, 1)
            pe.wait_ge(win_ready, 1)
            main_loop(pe, Steps(pe, None), [
                (transpose_x1, 0), (project, 2), (second_scores, 0), (log_decays, 1), (first_scores, 0),
                (scan_out, 1), (token_products, 0), (interpolate, 0), (transpose_e1, 0), (keep_warm, 3),
                (project_gates, 2), (attend, 0), (keep_warm, 1), (keep_warm, 3), (gram, 2), (transpose_xc, 2),
                (keep_warm, 2), (keep_warm, 1), (transpose_y, 1), (keep_warm, 0), (project_out, 1), (keep_warm, 2),
                (transpose_q, 3), (transpose_x2, 0), (keep_warm, 0), (router_logits, 0), (context_keys, 1),
                (context_values, 1)],
                before={-2: attention_weights, -1: attention_weights_there})

            pe.wait_ge(sel_ready, 1)
            pe.wait_ge(x2t_ready, did(2 * NG))
            pe.wait_ge(logit_ready, did(NG))
            pe.wait_ge(g_ready, did(NG))
            pe.wait_ge(xtok_ready, did(NG))
            pe.wait_ge(x1t_ready, did(NG))
            pe.wait_ge(dif_part, did(NB))
            pe.wait_ge(w2i_ready, did(NG))

            def gates_to_rows(i, part):
                pe.wait_ge(gate_ready, part)
                if i == NF - 1:
                    pe.wait_ge(res3_ready, did(NF - 1))
                for j in range(FB):
                    ins = pe.matmul(bank[4 + i][0:3 * E, j * L:(j + 1) * L],
                                    gate3[:, i * FB + j, :], ident_bf[:, :], start=True, stop=True)
                ins.then_inc(gt_psum, 1)

            def up_hidden(g, t):
                if t >= 2:
                    pe.wait_ge(hid_ready, did(NE * g + t - 1))
                elif t == 1:
                    pe.wait_ge(hid_ready, did(NE * g))
                else:
                    pe.wait_ge(hs_ready, did(2 * g))
                pe.sem_inc(pe_settled, 1)
                m, lhs = (128, w("w1")[:, t * 128:(t + 1) * 128]) if t < NE else (HID, w("ws1"))
                pe.matmul(bank[t % 2][0:m, :], lhs, x2T[:, bass.ds(g * FT, FT)],
                          start=True, stop=True).then_inc(h_psum, 1)

            def up_gates(g, t):
                if t >= 2:
                    pe.wait_ge(hg_ready, did(NE * g + t - 1))
                elif t == 1:
                    pe.wait_ge(hg_ready, did(NE * g))
                else:
                    pe.wait_ge(hs_ready, did(2 * g))
                pe.sem_inc(pe_settled, 1)
                pe.matmul(bank[2 + t % 2][:, :], sel_bf[:, t * 128:(t + 1) * 128], gT[:, bass.ds(g * FT, FT)],
                          start=True, stop=True).then_inc(gb_psum, 1)

            def down(g, t):
                if t < NE:
                    pe.wait_ge(hg_ready, did(NE * g + t + 1))
                else:
                    pe.wait_ge(hs_ready, did(2 * (g + 1)))
                if t == 0:
                    pe.wait_ge(res3_ready, did(g))
                for j in range(FB):
                    lhs, rhs = ((hid[:, t, j * L:(j + 1) * L], w("w2")[:, t * D:(t + 1) * D]) if t < NE else
                                (hid_s[0:96, j * L:(j + 1) * L], w("w2s", 96)))
                    ins = pe.matmul(bank[4 + j][:, 0:D], lhs, rhs, start=t == 0, stop=t == NE)
                if t == NE:
                    ins.then_inc(moe_psum, 1)

            def expert_group(g, begun=False):
                for t in range(NT):
                    if t or not begun:
                        up_hidden(g, t)
                    up_gates(g, t)
                    if t >= 2:
                        down(g, t - 2)
                down(g, NT - 2)
                down(g, NT - 1)

            up_hidden(0, 0)
            for i in range(NF - 1):
                gates_to_rows(i, 1)
            pe.wait_ge(gt_ready, did(NF - 1))
            expert_group(0, begun=True)
            with pe.Fori(1, NF - 1) as g:
                expert_group(g)
            gates_to_rows(NF - 1, 2)
            pe.wait_ge(gt_ready, did(NF))
            expert_group(NF - 1)
def kernel(**inputs):
    import numpy as _np
    import concourse.bacc as _bacc
    from concourse import mybir as _mybir
    from concourse.bass_utils import run_bass_kernel_spmd as _run

    a = {k.removeprefix("L0_"): _np.asarray(v) for k, v in inputs.items()}
    f32 = _np.float32

    def tiles(m):
        n = m.shape[0] // 128
        return m.reshape(n, 128, -1).transpose(1, 0, 2).reshape(128, -1)

    def column(v):
        out = _np.zeros((128, 1), f32)
        out[:v.shape[0], 0] = v
        return out

    w_in = a["attn_in_proj_w"]
    w2s = _np.zeros((128, 128), f32)
    w2s[:HID] = a["ffn_Ws2"]
    w2s[HID:HID + E] = a["ffn_b2"]
    parts = {
        "win": _np.concatenate([w_in[DI:DI + 512], w_in[:DI], w_in[DI + 512:]]).T,
        "wout": tiles(a["attn_out_proj_w"].T),
        "conv_w": tiles(a["attn_conv_w"]), "conv_b": tiles(a["attn_conv_b"][:, None]),
        "wq_c": a["xattn_Wq_c"], "wk_s": a["xattn_Wk_s"], "wq_s": a["xattn_Wq_s"], "wk_c": a["xattn_Wk_c"],
        "wv_s": a["xattn_Wv_s"], "wv_sT": a["xattn_Wv_s"].T, "wv_c": a["xattn_Wv_c"], "wv_cT": a["xattn_Wv_c"].T,
        "wgT": tiles(a["xattn_Wg"].T),
        "bq_c": a["xattn_bq_c"][:, None], "bk_s": a["xattn_bk_s"][:, None],
        "bq_s": a["xattn_bq_s"][:, None], "bk_c": a["xattn_bk_c"][:, None],
        "bv_s": a["xattn_bv_s"][:, None], "bv_c": a["xattn_bv_c"][:, None],
        "gate_w": a["ffn_gate_W"], "w1": a["ffn_W1"].transpose(1, 0, 2).reshape(D, E * HID), "ws1": a["ffn_Ws1"],
        "b1": tiles(a["ffn_b1"].reshape(-1, 1)), "bs1": column(a["ffn_bs1"]),
        "w2": tiles(a["ffn_W2"].reshape(E * HID, D)), "w2s": w2s,
    }
    wpack = _np.concatenate([parts[n] for n, _ in _COLS], axis=1)
    rows = {
        "norm_w": a["attn_norm_w"], "out_norm_w": a["attn_out_norm_w"], "Dp": a["attn_Dp"],
        "A_log": a["attn_A_log"], "dt_bias": a["attn_dt_bias"], "bg": a["xattn_bg"],
        "bv_s": a["xattn_bv_s"], "bv_c": a["xattn_bv_c"], "bs2": a["ffn_bs2"],
        "route_scale": a["ffn_route_scale"].reshape(1),
    }
    rpack = _np.concatenate([rows[n] for n, _ in _ROWS])

    i = _np.arange(128)
    interp = _np.zeros((128, L), f32)
    pos = _np.clip((_np.arange(L, dtype=f32) + f32(0.5)) * f32(LS / L) - f32(0.5), f32(0.0), f32(LS - 1))
    lo = _np.floor(pos).astype(_np.int32)
    hi = _np.minimum(lo + 1, LS - 1)
    frac = (pos - lo.astype(f32)).astype(f32)
    for l in range(L):
        interp[lo[l], l] += f32(1) - frac[l]
        interp[hi[l], l] += frac[l]
    sel = _np.zeros((128, NE + 1, 128), f32)
    for part in range(3):
        for e in range(E):
            sel[part * E + e, e * HID // 128, e * HID % 128:e * HID % 128 + HID] = 1
            sel[part * E + e, NE, HID + e] = 1
    prio = _np.broadcast_to(_np.arange(E, 0, -1).astype(f32), (128, E))
    cpack = _np.concatenate([_np.eye(128, dtype=f32), (i[:, None] <= i[None, :]).astype(f32),
                             (i[:, None] > i[None, :]).astype(f32), interp, sel.reshape(128, -1), prio], axis=1)

    arrays = {"x": a["x"], "ctxT": a["ctx_1024"].transpose(2, 0, 1).reshape(D, NB * LS),
              "wpack": wpack, "rpack": rpack, "cpack": cpack}
    nc = _bacc.Bacc("TRN2", target_bir_lowering=False, num_devices=1)
    args = []
    for name in arrays:
        arrays[name] = _np.ascontiguousarray(arrays[name])
        args.append(nc.dram_tensor(name, arrays[name].shape, _mybir.dt.from_np(arrays[name].dtype),
                                   kind="ExternalInput").ap())
    args.append(nc.dram_tensor("out", (NB, L, D), FP32, kind="ExternalOutput").ap())
    build(nc, *args)
    res = _run(nc, [arrays], core_ids=[0])
    return res.results[0]["out"]
```
